# Optimizing a Trainium2 kernel written in Bass

```python
import numpy as np
import jax
import jax.numpy as jnp

def _softmax(x, axis=-1):
    return jax.nn.softmax(x, axis=axis)

def _gelu(x):
    return jax.nn.gelu(x, approximate=True)

def _silu(x):
    return jax.nn.silu(x)

def _sigmoid(x):
    return jax.nn.sigmoid(x)

def _layernorm(x, axis=-1, eps=1e-05):
    m = jnp.mean(x, axis=axis, keepdims=True)
    v = jnp.var(x, axis=axis, keepdims=True)
    return (x - m) / jnp.sqrt(v + eps)

def _scatter_add(tgt, idx, src, axis=0):
    return tgt.at[idx].add(src)

def _segment_sum(src, seg, n):
    return jax.ops.segment_sum(src, seg, n)
kernel_name = 'mk_decoder_postln_d2_seqx_r4_b9fffd'

def setup_inputs(seed: int=0):
    np.random.seed(seed)
    _w = jnp.asarray

    def _rec_inputs():
        import jax
        import jax.numpy as jnp
        _rk = jax.random.key(seed)
        x = -0.0003929 + 0.9999 * jax.random.normal(jax.random.fold_in(_rk, 1), (4, 512, 256), jnp.float32)
        _lenS = 512 - jax.random.randint(jax.random.fold_in(_rk, 7), (4,), 0, max(1, 512 // 4) + 1, jnp.int32)
        _lenS2 = 512 - jax.random.randint(jax.random.fold_in(_rk, 8), (4,), 0, max(1, 512 // 4) + 1, jnp.int32)
        _ctx_1024P = jax.random.normal(jax.random.fold_in(_rk, 11), (4, 16, 256), jnp.float32)
        _ctx_1024c = jax.random.dirichlet(jax.random.fold_in(_rk, 511), 0.3 * jnp.ones((16,), jnp.float32), (4, 512))
        _ctx_1024t = jnp.einsum('bsk,bkd->bsd', _ctx_1024c, _ctx_1024P)
        _ctx_1024t = _ctx_1024t * jax.lax.rsqrt(jnp.mean(jnp.square(_ctx_1024t)) + 1e-12) * 0.953939
        ctx_1024 = 2.81802e-05 + 1.00001 * (_ctx_1024t + 0.3 * jax.random.normal(jax.random.fold_in(_rk, 611), (4, 512, 256), jnp.float32))
        fside_BxSxS2_0 = jax.random.uniform(jax.random.fold_in(_rk, 12), (4, 512, 512), jnp.float32, 0.0, 1)
        _validS = jnp.arange(512)[None, :] < _lenS[:, None]
        _validS2 = jnp.arange(512)[None, :] < _lenS2[:, None]
        _causal = jnp.tril(jnp.ones((512, 512), dtype=bool))
        mask_BxSxS2_ik1 = jnp.where(jnp.broadcast_to(_validS2[:, None, :], (4, 512, 512)), 1, 0).astype(jnp.int32)
        return (x, ctx_1024, fside_BxSxS2_0, mask_BxSxS2_ik1)
    x, ctx_1024, fside_BxSxS2_0, mask_BxSxS2_ik1 = _rec_inputs()

    def _L0_attn_setup():
        import math
        import jax, jax.numpy as jnp
        import numpy as np
        C = 8.0
        _MIN_RAD, _MAX_RAD = (0.9, 0.999)

        def block_diag_linear(x, w):
            B, T, D = x.shape
            H, bs, _ = w.shape
            xh = x.reshape(B, T, H, bs)
            return jnp.einsum('bthd,hde->bthe', xh, w).reshape(B, T, D)

        def linear_scan(a, b):

            def op(l, r):
                a1, b1 = l
                a2, b2 = r
                return (a1 * a2, a2 * b1 + b2)
            return jax.lax.associative_scan(op, (a, b), axis=1)[1]

        def _reference_tuple_inner(x, a_param, w_in, w_a):
            gate_x = jax.nn.sigmoid(block_diag_linear(x, w_in))
            gate_a = jax.nn.sigmoid(block_diag_linear(x, w_a))
            log_a = -C * jax.nn.softplus(a_param) * gate_a
            a = jnp.exp(log_a)
            multiplier = jnp.sqrt(1.0 - jnp.exp(2.0 * log_a))
            b = multiplier * (gate_x * x)
            y = linear_scan(a, b)
            h_last = y[:, -1, :]
            return (y, h_last)
        key = jax.random.key(seed)
        k1, k2, k3, k4 = jax.random.split(key, 4)
        B, T, D, H = (4, 1024, 256, 8)
        bs = D // H
        x = jax.random.normal(k1, (B, T, D), dtype=jnp.float32)
        std = 1.0 / math.sqrt(bs)
        w_in = jax.random.normal(k2, (H, bs, bs), dtype=jnp.float32) * std
        w_a = jax.random.normal(k3, (H, bs, bs), dtype=jnp.float32) * std
        sp = jax.random.uniform(k4, (D,), dtype=jnp.float32, minval=-math.log(_MAX_RAD) / C, maxval=-math.log(_MIN_RAD) / C)
        a_param = jnp.log(jnp.exp(sp) - 1.0 + 1e-08)
        return {'x': x, 'a_param': a_param, 'w_in': w_in, 'w_a': w_a}
    _L0_attn_all = _L0_attn_setup()
    _L0_attn_in = {k: v for k, v in _L0_attn_all.items() if k in ('a_param', 'w_in', 'w_a')}
    del _L0_attn_all

    def _L0_xattn_setup():
        import jax, jax.numpy as jnp
        import numpy as np
        D_MODEL = 256
        NHEAD = 16
        WINDOW = 128
        key = jax.random.key(seed)
        ks = jax.random.split(key, 7)
        B, L, D = (4, 1024, D_MODEL)
        s = 0.02
        return {'q': jax.random.normal(ks[0], (B, L, D), jnp.float32), 'k': jax.random.normal(ks[1], (B, L, D), jnp.float32), 'v': jax.random.normal(ks[2], (B, L, D), jnp.float32), 'in_proj_w': jax.random.normal(ks[3], (3 * D, D), jnp.float32) * s, 'in_proj_b': jnp.zeros((3 * D,), jnp.float32), 'out_w': jax.random.normal(ks[4], (D, D), jnp.float32) * s, 'out_b': jnp.zeros((D,), jnp.float32)}
    _L0_xattn_all = _L0_xattn_setup()
    _L0_xattn_in = {k: v for k, v in _L0_xattn_all.items() if k in ('in_proj_w', 'in_proj_b', 'out_w', 'out_b')}
    del _L0_xattn_all

    def _L0_ffn_setup():
        import jax, jax.numpy as jnp
        import numpy as np
        BITS = 8
        LORA_RANK = 16
        LORA_ALPHA = 32
        SCALING = LORA_ALPHA / LORA_RANK

        def fake_quant_weight(w, bits=BITS):
            qmax = 2.0 ** (bits - 1) - 1
            scale = jnp.max(jnp.abs(w)) / qmax
            wq = jnp.clip(jnp.round(w / scale), -qmax - 1, qmax) * scale
            return w + jax.lax.stop_gradient(wq - w)

        def qat_lora_linear(x, W, b, A, B):
            Wq = fake_quant_weight(W)
            base = jnp.einsum('bsi,oi->bso', x, Wq) + b
            lora = jnp.einsum('bsr,or->bso', jnp.einsum('bsi,ri->bsr', x, A), B)
            return base + SCALING * lora
        key = jax.random.key(seed)
        ks = jax.random.split(key, 9)
        d, f = (256, 1024)
        s_in = 1.0 / np.sqrt(d)
        s_ff = 1.0 / np.sqrt(f)
        return {'hidden_states': jax.random.normal(ks[0], (4, 512, d), jnp.float32), 'W_fc': jax.random.normal(ks[1], (f, d), jnp.float32) * s_in, 'b_fc': jnp.zeros((f,), jnp.float32), 'A_fc': jax.random.normal(ks[2], (LORA_RANK, d), jnp.float32) * s_in, 'B_fc': jnp.zeros((f, LORA_RANK), jnp.float32), 'W_proj': jax.random.normal(ks[3], (d, f), jnp.float32) * s_ff, 'b_proj': jnp.zeros((d,), jnp.float32), 'A_proj': jax.random.normal(ks[4], (LORA_RANK, f), jnp.float32) * s_ff, 'B_proj': jnp.zeros((d, LORA_RANK), jnp.float32)}
    _L0_ffn_all = _L0_ffn_setup()
    _L0_ffn_in = {k: v for k, v in _L0_ffn_all.items() if k in ('W_fc', 'b_fc', 'A_fc', 'B_fc', 'W_proj', 'b_proj', 'A_proj', 'B_proj')}
    del _L0_ffn_all

    def _L1_attn_setup():
        import jax, jax.numpy as jnp
        import numpy as np
        import math
        NUM_HEADS = 16
        MAX_BIAS = 8.0

        def _alibi_slopes(n_heads):

            def slopes(n):
                start = 2.0 ** (-2 ** (-(math.log2(n) - 3)))
                return [start * start ** i for i in range(n)]
            if math.log2(n_heads).is_integer():
                s = slopes(n_heads)
            else:
                p = 2 ** math.floor(math.log2(n_heads))
                s = slopes(p) + slopes(2 * p)[0::2][:n_heads - p]
            return jnp.asarray(np.array(s, dtype=np.float32))
        key = jax.random.key(seed)
        ks = jax.random.split(key, 5)
        B, S, C = (2, 512, 256)
        return {'x': jax.random.normal(ks[0], (B, S, C), jnp.float32), 'in_proj_weight': jax.random.normal(ks[1], (3 * C, C), jnp.float32) * C ** (-0.5), 'in_proj_bias': jax.random.normal(ks[2], (3 * C,), jnp.float32) * 0.02, 'out_proj_weight': jax.random.normal(ks[3], (C, C), jnp.float32) * C ** (-0.5), 'out_proj_bias': jax.random.normal(ks[4], (C,), jnp.float32) * 0.02}
    _L1_attn_all = _L1_attn_setup()
    _L1_attn_in = {k: v for k, v in _L1_attn_all.items() if k in ('in_proj_weight', 'in_proj_bias', 'out_proj_weight', 'out_proj_bias')}
    del _L1_attn_all

    def _L1_xattn_setup():
        import jax, jax.numpy as jnp
        import numpy as np
        NUM_HEADS = 16
        HIDDEN = 256
        B, S = (2, 512)

        def _split_heads(x, H):
            b, s, d = x.shape
            return x.reshape(b, s, H, d // H).transpose(0, 2, 1, 3)
        key = jax.random.key(seed)
        ks = jax.random.split(key, 14)
        D = HIDDEN
        scale = 1.0 / np.sqrt(D)
        inp = {'query': jax.random.normal(ks[0], (B, S, D), jnp.float32), 'key_in': jax.random.normal(ks[1], (B, S, D), jnp.float32), 'value': jax.random.normal(ks[2], (B, S, D), jnp.float32), 'group_prob': jax.random.uniform(ks[3], (B, S, S), jnp.float32), 'mask': jax.random.randint(ks[4], (B, S, S), 0, 2, jnp.int32), 'wq_k': jax.random.normal(ks[5], (D, D), jnp.float32) * scale, 'wq_b': jnp.zeros((D,), jnp.float32), 'wk_k': jax.random.normal(ks[6], (D, D), jnp.float32) * scale, 'wk_b': jnp.zeros((D,), jnp.float32), 'wv_k': jax.random.normal(ks[7], (D, D), jnp.float32) * scale, 'wv_b': jnp.zeros((D,), jnp.float32), 'wo_k': jax.random.normal(ks[8], (D, D), jnp.float32) * scale, 'wo_b': jnp.zeros((D,), jnp.float32)}
        return inp
    _L1_xattn_all = _L1_xattn_setup()
    _L1_xattn_in = {k: v for k, v in _L1_xattn_all.items() if k in ('wq_k', 'wq_b', 'wk_k', 'wk_b', 'wv_k', 'wv_b', 'wo_k', 'wo_b')}
    del _L1_xattn_all

    def _L1_ffn_setup():
        import jax, jax.numpy as jnp
        import numpy as np
        EMB = 256
        HEADS = 16
        SEQ = 512
        LATENT = 128
        N_EXP = 8
        TOP_K = 2
        EXP_DIM = 512
        BATCH = 2
        EPS = 1e-06

        def _rmsnorm(x, g):
            return x * jax.lax.rsqrt(jnp.mean(x * x, axis=-1, keepdims=True) + EPS) * g

        def _mla(h, Wq, Wdkv, Wuk, Wuv, Wo):
            B, S, D = h.shape
            hd = D // HEADS
            q = (h @ Wq).reshape(B, S, HEADS, hd)
            c = h @ Wdkv
            k = (c @ Wuk).reshape(B, S, HEADS, hd)
            v = (c @ Wuv).reshape(B, S, HEADS, hd)
            scores = jnp.einsum('bqhd,bkhd->bhqk', q, k) / jnp.sqrt(jnp.asarray(hd, h.dtype))
            causal = jnp.tril(jnp.ones((S, S), bool))
            scores = jnp.where(causal, scores, jnp.asarray(-1000000000.0, h.dtype))
            a = jax.nn.softmax(scores, axis=-1)
            out = jnp.einsum('bhqk,bkhd->bqhd', a, v).reshape(B, S, D)
            return out @ Wo

        def _moe(h, gate_w, w1, w2):
            B, S, D = h.shape
            t = h.reshape(B * S, D)
            logits = t @ gate_w
            top_v, top_i = jax.lax.top_k(logits, TOP_K)
            gates = jax.nn.softmax(top_v, axis=-1)
            T = t.shape[0]
            combine = jnp.zeros((T, N_EXP), t.dtype).at[jnp.arange(T)[:, None], top_i].add(gates)
            hid = jax.nn.silu(jnp.einsum('td,edh->teh', t, w1))
            ye = jnp.einsum('teh,ehd->ted', hid, w2)
            out = jnp.einsum('te,ted->td', combine, ye)
            return out.reshape(B, S, D)
        key = jax.random.key(seed)
        ks = jax.random.split(key, 12)
        s = 0.02
        return {'x': jax.random.normal(ks[0], (BATCH, SEQ, EMB), jnp.float32), 'g1': jnp.ones((EMB,), jnp.float32), 'Wq': jax.random.normal(ks[1], (EMB, EMB), jnp.float32) * s, 'Wdkv': jax.random.normal(ks[2], (EMB, LATENT), jnp.float32) * s, 'Wuk': jax.random.normal(ks[3], (LATENT, EMB), jnp.float32) * s, 'Wuv': jax.random.normal(ks[4], (LATENT, EMB), jnp.float32) * s, 'Wo': jax.random.normal(ks[5], (EMB, EMB), jnp.float32) * s, 'g2': jnp.ones((EMB,), jnp.float32), 'gate_w': jax.random.normal(ks[6], (EMB, N_EXP), jnp.float32) * s, 'w1': jax.random.normal(ks[7], (N_EXP, EMB, EXP_DIM), jnp.float32) * s, 'w2': jax.random.normal(ks[8], (N_EXP, EXP_DIM, EMB), jnp.float32) * s}
    _L1_ffn_all = _L1_ffn_setup()
    _L1_ffn_in = {k: v for k, v in _L1_ffn_all.items() if k in ('g1', 'Wq', 'Wdkv', 'Wuk', 'Wuv', 'Wo', 'g2', 'gate_w', 'w1', 'w2')}
    del _L1_ffn_all
    return {'x': x, 'ctx_1024': ctx_1024, 'fside_BxSxS2_0': fside_BxSxS2_0, 'mask_BxSxS2_ik1': mask_BxSxS2_ik1, 'L0_attn_a_param': _L0_attn_in['a_param'], 'L0_attn_w_in': _L0_attn_in['w_in'], 'L0_attn_w_a': _L0_attn_in['w_a'], 'L0_xattn_in_proj_w': _L0_xattn_in['in_proj_w'], 'L0_xattn_in_proj_b': _L0_xattn_in['in_proj_b'], 'L0_xattn_out_w': _L0_xattn_in['out_w'], 'L0_xattn_out_b': _L0_xattn_in['out_b'], 'L0_ffn_W_fc': _L0_ffn_in['W_fc'], 'L0_ffn_b_fc': _L0_ffn_in['b_fc'], 'L0_ffn_A_fc': _L0_ffn_in['A_fc'], 'L0_ffn_B_fc': _L0_ffn_in['B_fc'], 'L0_ffn_W_proj': _L0_ffn_in['W_proj'], 'L0_ffn_b_proj': _L0_ffn_in['b_proj'], 'L0_ffn_A_proj': _L0_ffn_in['A_proj'], 'L0_ffn_B_proj': _L0_ffn_in['B_proj'], 'L1_attn_in_proj_weight': _L1_attn_in['in_proj_weight'], 'L1_attn_in_proj_bias': _L1_attn_in['in_proj_bias'], 'L1_attn_out_proj_weight': _L1_attn_in['out_proj_weight'], 'L1_attn_out_proj_bias': _L1_attn_in['out_proj_bias'], 'L1_xattn_wq_k': _L1_xattn_in['wq_k'], 'L1_xattn_wq_b': _L1_xattn_in['wq_b'], 'L1_xattn_wk_k': _L1_xattn_in['wk_k'], 'L1_xattn_wk_b': _L1_xattn_in['wk_b'], 'L1_xattn_wv_k': _L1_xattn_in['wv_k'], 'L1_xattn_wv_b': _L1_xattn_in['wv_b'], 'L1_xattn_wo_k': _L1_xattn_in['wo_k'], 'L1_xattn_wo_b': _L1_xattn_in['wo_b'], 'L1_ffn_g1': _L1_ffn_in['g1'], 'L1_ffn_Wq': _L1_ffn_in['Wq'], 'L1_ffn_Wdkv': _L1_ffn_in['Wdkv'], 'L1_ffn_Wuk': _L1_ffn_in['Wuk'], 'L1_ffn_Wuv': _L1_ffn_in['Wuv'], 'L1_ffn_Wo': _L1_ffn_in['Wo'], 'L1_ffn_g2': _L1_ffn_in['g2'], 'L1_ffn_gate_w': _L1_ffn_in['gate_w'], 'L1_ffn_w1': _L1_ffn_in['w1'], 'L1_ffn_w2': _L1_ffn_in['w2']}

def reference(x, ctx_1024, fside_BxSxS2_0, mask_BxSxS2_ik1, L0_attn_a_param, L0_attn_w_in, L0_attn_w_a, L0_xattn_in_proj_w, L0_xattn_in_proj_b, L0_xattn_out_w, L0_xattn_out_b, L0_ffn_W_fc, L0_ffn_b_fc, L0_ffn_A_fc, L0_ffn_B_fc, L0_ffn_W_proj, L0_ffn_b_proj, L0_ffn_A_proj, L0_ffn_B_proj, L1_attn_in_proj_weight, L1_attn_in_proj_bias, L1_attn_out_proj_weight, L1_attn_out_proj_bias, L1_xattn_wq_k, L1_xattn_wq_b, L1_xattn_wk_k, L1_xattn_wk_b, L1_xattn_wv_k, L1_xattn_wv_b, L1_xattn_wo_k, L1_xattn_wo_b, L1_ffn_g1, L1_ffn_Wq, L1_ffn_Wdkv, L1_ffn_Wuk, L1_ffn_Wuv, L1_ffn_Wo, L1_ffn_g2, L1_ffn_gate_w, L1_ffn_w1, L1_ffn_w2):
    import jax
    import jax.numpy as jnp

    def _L0_attn_ref(x, a_param, w_in, w_a):
        import math
        import jax, jax.numpy as jnp
        import numpy as np
        C = 8.0
        _MIN_RAD, _MAX_RAD = (0.9, 0.999)

        def block_diag_linear(x, w):
            B, T, D = x.shape
            H, bs, _ = w.shape
            xh = x.reshape(B, T, H, bs)
            return jnp.einsum('bthd,hde->bthe', xh, w).reshape(B, T, D)

        def linear_scan(a, b):

            def op(l, r):
                a1, b1 = l
                a2, b2 = r
                return (a1 * a2, a2 * b1 + b2)
            return jax.lax.associative_scan(op, (a, b), axis=1)[1]

        def _reference_tuple_inner(x, a_param, w_in, w_a):
            gate_x = jax.nn.sigmoid(block_diag_linear(x, w_in))
            gate_a = jax.nn.sigmoid(block_diag_linear(x, w_a))
            log_a = -C * jax.nn.softplus(a_param) * gate_a
            a = jnp.exp(log_a)
            multiplier = jnp.sqrt(1.0 - jnp.exp(2.0 * log_a))
            b = multiplier * (gate_x * x)
            y = linear_scan(a, b)
            h_last = y[:, -1, :]
            return (y, h_last)
        return _reference_tuple_inner(x, a_param, w_in, w_a)[0]

    def _L0_xattn_ref(q, k, v, in_proj_w, in_proj_b, out_w, out_b):
        import jax, jax.numpy as jnp
        import numpy as np
        D_MODEL = 256
        NHEAD = 16
        WINDOW = 128
        B, L, D = q.shape
        H, W = (NHEAD, WINDOW)
        hd = D // H
        nW = L // W
        Wq, Wk, Wv = (in_proj_w[:D], in_proj_w[D:2 * D], in_proj_w[2 * D:])
        bq, bk, bv = (in_proj_b[:D], in_proj_b[D:2 * D], in_proj_b[2 * D:])
        qp = (q @ Wq.T + bq).reshape(B, nW, W, H, hd)
        kp = (k @ Wk.T + bk).reshape(B, nW, W, H, hd)
        vp = (v @ Wv.T + bv).reshape(B, nW, W, H, hd)
        scale = 1.0 / np.sqrt(hd).astype(np.float32)
        scores = jnp.einsum('bnqhd,bnkhd->bnhqk', qp, kp) * scale
        attn = jax.nn.softmax(scores, axis=-1)
        out = jnp.einsum('bnhqk,bnkhd->bnqhd', attn, vp).reshape(B, L, D)
        return out @ out_w.T + out_b

    def _L0_ffn_ref(hidden_states, W_fc, b_fc, A_fc, B_fc, W_proj, b_proj, A_proj, B_proj):
        import jax, jax.numpy as jnp
        import numpy as np
        BITS = 8
        LORA_RANK = 16
        LORA_ALPHA = 32
        SCALING = LORA_ALPHA / LORA_RANK

        def fake_quant_weight(w, bits=BITS):
            qmax = 2.0 ** (bits - 1) - 1
            scale = jnp.max(jnp.abs(w)) / qmax
            wq = jnp.clip(jnp.round(w / scale), -qmax - 1, qmax) * scale
            return w + jax.lax.stop_gradient(wq - w)

        def qat_lora_linear(x, W, b, A, B):
            Wq = fake_quant_weight(W)
            base = jnp.einsum('bsi,oi->bso', x, Wq) + b
            lora = jnp.einsum('bsr,or->bso', jnp.einsum('bsi,ri->bsr', x, A), B)
            return base + SCALING * lora
        h = qat_lora_linear(hidden_states, W_fc, b_fc, A_fc, B_fc)
        h = jax.nn.gelu(h, approximate=False)
        h = qat_lora_linear(h, W_proj, b_proj, A_proj, B_proj)
        return h

    def _L1_attn_ref(x, in_proj_weight, in_proj_bias, out_proj_weight, out_proj_bias):
        import jax, jax.numpy as jnp
        import numpy as np
        import math
        NUM_HEADS = 16
        MAX_BIAS = 8.0

        def _alibi_slopes(n_heads):

            def slopes(n):
                start = 2.0 ** (-2 ** (-(math.log2(n) - 3)))
                return [start * start ** i for i in range(n)]
            if math.log2(n_heads).is_integer():
                s = slopes(n_heads)
            else:
                p = 2 ** math.floor(math.log2(n_heads))
                s = slopes(p) + slopes(2 * p)[0::2][:n_heads - p]
            return jnp.asarray(np.array(s, dtype=np.float32))
        B, S, C = x.shape
        H = NUM_HEADS
        D = C // H
        qkv = x @ in_proj_weight.T + in_proj_bias
        qkv = qkv.reshape(B, S, 3, H, D).transpose(2, 0, 3, 1, 4)
        q, k, v = (qkv[0], qkv[1], qkv[2])
        slopes = _alibi_slopes(H)
        pos = jnp.arange(S, dtype=jnp.float32)
        rel = pos[:, None] - pos[None, :]
        bias = jnp.minimum(rel[None, :, :] * slopes[:, None, None], MAX_BIAS)
        scores = jnp.einsum('bhqd,bhkd->bhqk', q, k) * D ** (-0.5) + bias[None]
        probs = jax.nn.softmax(scores, axis=-1)
        out = jnp.einsum('bhqk,bhkd->bhqd', probs, v)
        out = out.transpose(0, 2, 1, 3).reshape(B, S, C)
        return out @ out_proj_weight.T + out_proj_bias

    def _L1_xattn_ref(query, key_in, value, group_prob, mask, wq_k, wq_b, wk_k, wk_b, wv_k, wv_b, wo_k, wo_b):
        import jax, jax.numpy as jnp
        import numpy as np
        NUM_HEADS = 16
        HIDDEN = 256
        B, S = (2, 512)

        def _split_heads(x, H):
            b, s, d = x.shape
            return x.reshape(b, s, H, d // H).transpose(0, 2, 1, 3)
        H = NUM_HEADS
        dh = query.shape[-1] // H
        q = _split_heads(query @ wq_k + wq_b, H)
        k = _split_heads(key_in @ wk_k + wk_b, H)
        v = _split_heads(value @ wv_k + wv_b, H)
        logits = jnp.einsum('bhqd,bhkd->bhqk', q, k) / jnp.sqrt(jnp.asarray(dh, q.dtype))
        neg = (1.0 - mask.astype(q.dtype)) * -1000000000.0
        logits = logits + neg[:, None, :, :]
        attn = jax.nn.softmax(logits, axis=-1)
        attn = attn * group_prob[:, None, :, :]
        out = jnp.einsum('bhqk,bhkd->bhqd', attn, v)
        out = out.transpose(0, 2, 1, 3).reshape(query.shape[0], -1, H * dh)
        return out @ wo_k + wo_b

    def _L1_ffn_ref(x, g1, Wq, Wdkv, Wuk, Wuv, Wo, g2, gate_w, w1, w2):
        import jax, jax.numpy as jnp
        import numpy as np
        EMB = 256
        HEADS = 16
        SEQ = 512
        LATENT = 128
        N_EXP = 8
        TOP_K = 2
        EXP_DIM = 512
        BATCH = 2
        EPS = 1e-06

        def _rmsnorm(x, g):
            return x * jax.lax.rsqrt(jnp.mean(x * x, axis=-1, keepdims=True) + EPS) * g

        def _mla(h, Wq, Wdkv, Wuk, Wuv, Wo):
            B, S, D = h.shape
            hd = D // HEADS
            q = (h @ Wq).reshape(B, S, HEADS, hd)
            c = h @ Wdkv
            k = (c @ Wuk).reshape(B, S, HEADS, hd)
            v = (c @ Wuv).reshape(B, S, HEADS, hd)
            scores = jnp.einsum('bqhd,bkhd->bhqk', q, k) / jnp.sqrt(jnp.asarray(hd, h.dtype))
            causal = jnp.tril(jnp.ones((S, S), bool))
            scores = jnp.where(causal, scores, jnp.asarray(-1000000000.0, h.dtype))
            a = jax.nn.softmax(scores, axis=-1)
            out = jnp.einsum('bhqk,bkhd->bqhd', a, v).reshape(B, S, D)
            return out @ Wo

        def _moe(h, gate_w, w1, w2):
            B, S, D = h.shape
            t = h.reshape(B * S, D)
            logits = t @ gate_w
            top_v, top_i = jax.lax.top_k(logits, TOP_K)
            gates = jax.nn.softmax(top_v, axis=-1)
            T = t.shape[0]
            combine = jnp.zeros((T, N_EXP), t.dtype).at[jnp.arange(T)[:, None], top_i].add(gates)
            hid = jax.nn.silu(jnp.einsum('td,edh->teh', t, w1))
            ye = jnp.einsum('teh,ehd->ted', hid, w2)
            out = jnp.einsum('te,ted->td', combine, ye)
            return out.reshape(B, S, D)
        x = x + _mla(_rmsnorm(x, g1), Wq, Wdkv, Wuk, Wuv, Wo)
        x = x + _moe(_rmsnorm(x, g2), gate_w, w1, w2)
        return x
    x = _layernorm(x + _L0_attn_ref(x, L0_attn_a_param, L0_attn_w_in, L0_attn_w_a), axis=-1)
    x = _layernorm(x + _L0_xattn_ref(x, ctx_1024, ctx_1024, L0_xattn_in_proj_w, L0_xattn_in_proj_b, L0_xattn_out_w, L0_xattn_out_b), axis=-1)
    x = _layernorm(x + _L0_ffn_ref(x, L0_ffn_W_fc, L0_ffn_b_fc, L0_ffn_A_fc, L0_ffn_B_fc, L0_ffn_W_proj, L0_ffn_b_proj, L0_ffn_A_proj, L0_ffn_B_proj), axis=-1)
    x = _layernorm(x + _L1_attn_ref(x, L1_attn_in_proj_weight, L1_attn_in_proj_bias, L1_attn_out_proj_weight, L1_attn_out_proj_bias), axis=-1)
    x = _layernorm(x + _L1_xattn_ref(x, ctx_1024, ctx_1024, fside_BxSxS2_0, mask_BxSxS2_ik1, L1_xattn_wq_k, L1_xattn_wq_b, L1_xattn_wk_k, L1_xattn_wk_b, L1_xattn_wv_k, L1_xattn_wv_b, L1_xattn_wo_k, L1_xattn_wo_b), axis=-1)
    x = _layernorm(x + _L1_ffn_ref(x, L1_ffn_g1, L1_ffn_Wq, L1_ffn_Wdkv, L1_ffn_Wuk, L1_ffn_Wuv, L1_ffn_Wo, L1_ffn_g2, L1_ffn_gate_w, L1_ffn_w1, L1_ffn_w2), axis=-1)
    return x

_drawn_inputs = setup_inputs


def setup_inputs(seed=0):
    import zlib

    import numpy as np

    out = dict(_drawn_inputs(seed))
    spreads = {'L0_xattn_in_proj_b': (0.0, 0.1),
     'L0_xattn_out_b': (0.0, 0.1),
     'L0_ffn_b_fc': (0.0, 0.1),
     'L0_ffn_B_fc': (0.0, 0.1),
     'L0_ffn_b_proj': (0.0, 0.1),
     'L0_ffn_B_proj': (0.0, 0.1),
     'L1_xattn_wq_b': (0.0, 0.641),
     'L1_xattn_wk_b': (0.0, 2.0),
     'L1_xattn_wv_b': (0.0, 0.1),
     'L1_xattn_wo_b': (0.0, 0.1),
     'L1_ffn_g1': (1.0, 0.6),
     'L1_ffn_g2': (1.0, 0.6)}
    factors = {'L1_attn_in_proj_bias': 2.829,
     'L1_attn_out_proj_bias': 3.405,
     'L1_ffn_Wq': 8.0,
     'L1_ffn_Wdkv': 5.771,
     'L1_ffn_Wuk': 8.0,
     'L1_ffn_Wuv': 5.978,
     'L1_ffn_Wo': 5.829,
     'L1_ffn_gate_w': 6.149,
     'L1_ffn_w1': 5.185,
     'L1_ffn_w2': 5.109}
    for name, (base, spread) in spreads.items():
        noise = np.random.default_rng([zlib.crc32(name.encode()), seed]).standard_normal(out[name].shape)
        drawn = base * np.exp(spread * noise) if base else spread * noise
        out[name] = jnp.asarray(drawn.astype(out[name].dtype))
    for name, factor in factors.items():
        out[name] = (out[name] * factor).astype(out[name].dtype)
    return out
```

```python
import concourse.bass as bass
from concourse import mybir
from contextlib import ExitStack

F32 = mybir.dt.float32
BF16 = mybir.dt.bfloat16
I32 = mybir.dt.int32
ALU = mybir.AluOpType
ACT = mybir.ActivationFunctionType
AX = mybir.AxisListType

P = 128
NB, S, D = 4, 512, 256
H, HD = 16, 16
NT = S // P
NC = D // P
G, J = 4, 4
F = 1024
NF = F // P
R = 16
LAT = 128
NE, EH = 8, 512
NH = EH // P
BANK = 512
QSCALE = 0.25
LN_EPS, RMS_EPS = 1e-5, 1e-6
LORA_SCALING = 2.0
QMAX = 127.0
ROUND = 1.5 * 2.0 ** 23
NEG = -998244352.0
LOWEST = -3.0e38
RMAX = bass.bass_isa.ReduceOp.max

Q_PARTS = (0, 0, 1, 1, 0, 2)
K_PARTS = (0, 1, 0, 1, 2, 0)
ROWS = len(Q_PARTS) * HD
Q_SLOPE = ROWS
K_SLOPE = ROWS + 3
ALL_ROWS = ROWS + 9

CLAMPED = {h: (0 if h < 7 else 1 if h < 9 else 2, 3 if h % 2 == 0 else 2) for h in range(11)}
CLAMP_AT = {}
_at = 0
for _h, (_d, _n) in CLAMPED.items():
    CLAMP_AT[_h] = _at
    _at += _n * (S - _d * P)
CLAMP_COLS = _at

PACK = [
    ("gates", 2 * NC * P), ("a_param", NC),
    ("l0_q", NC * D), ("l0_k", NC * D), ("l0_v", NC * D), ("l0_o", G * D),
    ("l0_qb", NC), ("l0_kb", NC), ("l0_vb", D), ("l0_ob", D),
    ("fc", NC * F), ("fc_b", NF), ("proj", NF * D), ("proj_b", D),
    ("l1_q", NC * D), ("l1_k", NC * D), ("l1_v", NC * D), ("l1_o", G * D),
    ("l1_qb", NC), ("l1_kb", NC), ("l1_vb", D), ("l1_ob", D),
    ("x_q", NC * D), ("x_k", NC * D), ("x_v", NC * D), ("x_o", G * D),
    ("x_qb", NC), ("x_kb", NC), ("x_vb", D), ("x_ob", D),
    ("m_q", NC * D), ("m_lat", NC * LAT), ("m_k", D), ("m_v", D), ("m_o", G * D),
    ("g1", D), ("g2", D), ("router", NC * NE), ("ident", P), ("before", NE * NE),
]
PACK_AT, _at = {}, 0
for _name, _n in PACK:
    PACK_AT[_name] = (_at, _n)
    _at += _n
PACK_COLS = _at
CONST = {"ident": 0, "tri_q": P, "tri_k": 2 * P}
CONST_COLS = 3 * P

WINDOW, ALIBI, MASKED, CAUSAL = range(4)
STEPS = {WINDOW: 1, ALIBI: NT, MASKED: NT, CAUSAL: NT}
KINDS = (WINDOW, ALIBI, MASKED, CAUSAL)
QUADS_BEFORE = {WINDOW: 0, ALIBI: G, MASKED: G * 5, CAUSAL: G * 9}
QUADS = G * 13


def corrections(h, q):
    first, n = CLAMPED.get(h, (NT, 0))
    return [(d, CLAMP_AT[h] + m * (S - first * P) + (d - first) * P) for d in range(first, q + 1) for m in range(n)]


def steps_of(kind):
    n, out = STEPS[kind], []
    for g in range(G + 1):
        ahead = [("S", g, s) for s in range(n)] if g < G else []
        if g == 0:
            out += ahead + [("M", 0, 0)]
            continue
        lead = len(ahead) // 2
        out += ahead[:lead]
        ahead = ahead[lead:]
        for s in range(n):
            out.append(("T", g - 1, s))
            if s > 0:
                out.append(("V", g - 1, s - 1))
            if ahead:
                out.append(ahead.pop(0))
        if g < G:
            out += ahead + [("M", g, 0)]
        out.append(("V", g - 1, n - 1))
    return out


class Events:

    def __init__(self, ctx, nc, name, per_turn, once=0):
        self.sem = ctx.enter_context(nc.semaphore(name))
        self.per_turn, self.once, self.name = per_turn, once, name

    def at(self, turn, count):
        return turn * self.per_turn + (self.once + count)


class Steps:

    def __init__(self, counted):
        self.counted, self.count, self.turn = counted, 0, None

    def one(self):
        self.count += 1
        return 1

    def so_far(self):
        return self.count if self.turn is None else self.counted.at(self.turn, self.count)

    def begin(self, turn):
        assert self.count == self.counted.once, (self.counted.name, "once", self.count)
        self.count, self.turn = 0, turn

    def end(self):
        assert self.count == self.counted.per_turn, (self.counted.name, "per turn", self.count)


VECTOR_ONCE, VECTOR_TURN = 25, 185
ACT_ONCE, ACT_TURN = 3, 1


def decoder(nc, ins, out):
    ctx = ExitStack()
    with ctx:
        def sb(name, shape, dt=F32):
            return ctx.enter_context(nc.sbuf_tensor(name, shape, dt))

        def events(name, per_turn, once=0):
            return Events(ctx, nc, name, per_turn, once)

        pack = sb("pack", [P, PACK_COLS])
        const = sb("const", [P, CONST_COLS], BF16)
        x = sb("x", [P, NT, D])
        y = sb("y", [P, NT, D])
        xt = sb("xt", [P, NC, S])
        ct = sb("ct", [P, NC, S])
        qs = sb("qs", [P, H, S], BF16)
        ks = sb("ks", [P, H, S], BF16)
        va = sb("va", [P, NT, H, 32])
        ones = sb("ones", [P, 32])
        ot = sb("ot", [P, G, S])
        big = sb("big", [P, 4 * J * S])
        side = sb("side", [P, max(CLAMP_COLS // 2, 2 * NT * S + NT * S // 2)])
        w1 = sb("w1", [P, 2, NC, EH])
        w2 = sb("w2", [P, 2, NH, D])
        mx = sb("mx", [P, G, NT, J])
        mr = sb("mr", [P, NT, J])
        mp = sb("mp", [P, G, NT, 3, J], BF16)
        mrow = sb("mrow", [3 * J, S], BF16)
        stats = sb("stats", [P, NT, 6])
        mv = sb("mv", [P, NT, 2])
        ve = sb("ve", [P, NT])
        rstd = sb("rstd", [P, NT])
        half = sb("half", [P, NT])
        small = sb("small", [P, 24])
        logit = sb("logit", [P, 4, NT * NE])
        spare = sb("spare", [P, 88])
        comb = sb("comb", [P, NT, NE])
        gat = sb("gat", [P, 3, NT])
        ps = ctx.enter_context(nc.psum_tensor("ps", [P, 8 * BANK], F32))

        def bank(b, n=1):
            return ps[:, b * BANK:(b + n) * BANK]

        def w(name):
            at, n = PACK_AT[name]
            return pack[:, at:at + n]

        def w3(name, a):
            return w(name).rearrange("p (a n) -> p a n", a=a)

        def part(at, *dims):
            n = 1
            for d in dims:
                n *= d
            v = big[:, at:at + n]
            if len(dims) == 2:
                return v.rearrange("p (a b) -> p a b", a=dims[0])
            return v.rearrange("p (a b c) -> p a b c", a=dims[0], b=dims[1])

        tg = part(0, 2, NC, S)
        dec = part(2048, NC, S)
        stp = part(3072, NC, S)
        gx = part(4096, NC, S)
        st = part(5120, NC, S)
        qk = part(0, 2, NC, S)
        parts = big[:, 2048:2048 + 3072].bitcast(BF16).rearrange(
            "p (o i c s) -> p o i c s", o=2, i=3, c=NC)
        hid = part(0, NF, S)
        prob = part(0, 4, J, S)
        rank = big[:, 7168:7168 + 2 * NT * NE * NE].rearrange("p (a n) -> p a n", a=2)
        qtmp = big[:, 0:2048]
        lora = big[0:R, 2048:2048 + 2 * (D + F)]
        clamp = side[:, 0:CLAMP_COLS // 2].bitcast(BF16)
        grp = side[:, 0:NT * S].rearrange("p (a s) -> p a s", a=NT)
        neg = side[:, NT * S:2 * NT * S].rearrange("p (a s) -> p a s", a=NT)
        negt = side[:, 2 * NT * S:2 * NT * S + NT * S // 2].bitcast(BF16).rearrange(
            "p (a s) -> p a s", a=NT)
        rinv = xt[:, 0, :]
        base = ct[:, :, :].rearrange("p c (t d) -> p (c t) d", d=D)
        recip = y[:, 2:4, :].rearrange("p a n -> p (a n)")
        identf = w("ident")
        identb = const[:, CONST["ident"]:CONST["ident"] + P]
        tri_q = const[:, CONST["tri_q"]:CONST["tri_q"] + P]
        tri_k = const[:, CONST["tri_k"]:CONST["tri_k"] + P]

        s_w = events("weights_loaded", 0, 16)
        s_c = events("constants_loaded", 0, 16 * 5)
        s_set = events("buffers_set", 0, 4)
        s_amax = events("weight_max", 0, 2)
        s_amaxall = events("weight_max_everywhere", 0, 2)
        s_lora = events("lora_product", 0, 4)
        s_loraused = events("lora_used", 0, 4)
        s_sp = events("softplus_exp", 0, 2)
        s_prep = events("weights_prepared", 0, 1)
        s_x = events("inputs_loaded", 16 * 2)
        s_alibi = events("alibi_loaded", 16 * 2)
        s_side = events("group_and_mask_loaded", 16 * 3)
        s_vec = events("vector_steps", VECTOR_TURN, VECTOR_ONCE)
        s_act = events("scalar_steps", ACT_TURN, ACT_ONCE)
        s_gates = events("gates_ready", 1)
        s_decay = events("decay_ready", 1)
        s_sq = events("decay_squared", 1)
        s_mult = events("step_ready", 1)
        s_rg = events("recurrence_done", 1)
        s_z = events("output_tile_ready", 6 * NT)
        s_var = events("variance_ready", 8)
        s_rstd = events("rstd_ready", 8)
        s_norm = events("normalised_tile", 8 * NT)
        s_xtp = events("transposed", 6)
        s_xt = events("feature_major_ready", 6)
        s_bias = events("residual_plus_bias", 4)
        s_proj = events("projection_ready", 12)
        s_lat = events("latent_ready", 1)
        s_latc = events("latent_copied", 1)
        s_f = events("q_or_k_float", 2 * 4)
        s_p = [events(f"part_{i}_ready", 2 * 4) for i in range(3)]
        s_negt = events("mask_turned", 1)
        s_sum = events("latent_attention_added", 1)
        s_op = events("operands_loaded", 16 * 12 * 4)
        s_va = events("values_ready", 4)
        s_s = events("scores_ready", J * QUADS)
        s_max = events("maximum_taken", J * QUADS)
        s_mp = events("maximum_split", 4 * G)
        s_mt = events("maximum_transposed", 4 * G)
        s_mc = events("maximum_copied", 4 * G)
        s_md = events("maximum_in_operand", 16 * 4 * G)
        s_t = events("key_major_ready", 2 * QUADS)
        s_exp = events("exp_done", 2 * QUADS)
        s_pg = events("grouped_ready", G * NT)
        s_pv = events("values_summed", QUADS)
        s_o = events("heads_normalised", 4 * G)
        s_h = events("hidden_ready", NF + NE * NH)
        s_hc = events("hidden_done", NF + NE * NH)
        s_router = events("router_ready", 1)
        s_dif = events("router_shifted", 1)
        s_rexp = events("router_exp", 1)
        s_e = events("expert_tile", NE * NT)
        s_ec = events("expert_added", NE * NT)
        s_w1 = [events(f"expert_up_{i}_loaded", 16 * NE // 2) for i in range(2)]
        s_w2 = [events(f"expert_down_{i}_loaded", 16 * NE // 2) for i in range(2)]
        s_ss = events("squares_summed", 2)
        s_out = events("stored", 16)

        def quad(kind, g, s):
            return QUADS_BEFORE[kind] + g * STEPS[kind] + s

        block = ctx.enter_context(nc.Block())

        @block.sync
        def _(sp):
            sp.dma_start(pack[:, :], ins["pack"]).then_inc(s_w.sem, 16)
            sp.dma_start(lora, ins["lora"]).then_inc(s_c.sem, 16)
            sp.dma_start(const[:, :], ins["const"]).then_inc(s_c.sem, 16)
            sp.dma_start(ks[ROWS:ALL_ROWS, :, :], ins["k_rows"]).then_inc(s_c.sem, 16)
            sp.dma_start(qs[K_SLOPE:K_SLOPE + 3, :, :], ins["one_rows"]).then_inc(s_c.sem, 16)
            sp.dma_start(half[:, :], ins["half"]).then_inc(s_c.sem, 16)

            with sp.Fori(0, NB) as turn:
                def expert_up(e):
                    if e >= 2:
                        sp.wait_ge(s_h.sem, s_h.at(turn, NF + NH * (e - 1)))
                    sp.dma_start(w1[:, e % 2, :, :], ins["w1"][e]).then_inc(s_w1[e % 2].sem, 16)

                def expert_down(e):
                    if e >= 2:
                        sp.wait_ge(s_e.sem, s_e.at(turn, NT * (e - 1)))
                    sp.dma_start(w2[:, e % 2, :, :], ins["w2"][e]).then_inc(s_w2[e % 2].sem, 16)

                def one(name):
                    return ins[name][bass.ds(turn, 1)].rearrange("a p n m -> (a p) n m")

                x_in, c_in = one("x"), one("c")
                sp.dma_start(xt[:, :, :], x_in).then_inc(s_x.sem, 16)
                sp.dma_start(ct[:, :, :], c_in).then_inc(s_x.sem, 16)
                sp.dma_start(clamp, ins["clamp"]).then_inc(s_alibi.sem, 16)
                for e in range(2):
                    expert_up(e)
                    expert_down(e)
                for a, kind in enumerate(KINDS):
                    if kind == ALIBI:
                        sp.wait_ge(s_pv.sem, s_pv.at(turn, QUADS_BEFORE[ALIBI]))
                        sp.dma_start(qs[Q_SLOPE:Q_SLOPE + 3, :, :], ins["q_rows"]).then_inc(s_alibi.sem, 16)
                    if kind == MASKED:
                        sp.wait_ge(s_pv.sem, s_pv.at(turn, QUADS_BEFORE[MASKED]))
                        g_in, m_in, mt_in = one("group"), one("mask"), one("mask_t")
                        sp.dma_start(neg.bitcast(I32), m_in).then_inc(s_side.sem, 16)
                        sp.dma_start(grp.bitcast(I32), mt_in).then_inc(s_side.sem, 16)
                        sp.wait_ge(s_negt.sem, s_negt.at(turn, 1))
                        sp.dma_start(grp, g_in).then_inc(s_side.sem, 16)
                    for o, dst, slots in ((0, qs, Q_PARTS), (1, ks, K_PARTS)):
                        for i in range(3):
                            sp.wait_ge(s_p[i].sem, s_p[i].at(turn, 2 * a + o + 1))
                            for slot in range(6):
                                if slots[slot] == i:
                                    sp.dma_start(dst[slot * HD:(slot + 1) * HD, :, :], parts[:, o, i, :, :])\
                                      .then_inc(s_op.sem, 16)
                    at = Q_SLOPE + 6 if kind == ALIBI else ROWS
                    for g in range(G):
                        sp.wait_ge(s_mc.sem, s_mc.at(turn, G * a + g + 1))
                        sp.dma_start(qs[at:at + 3, J * g:J * g + J, :], mrow[:, :]).then_inc(s_md.sem, 16)
                for e in range(2, NE):
                    expert_up(e)
                    expert_down(e)
                o_out = out[bass.ds(turn, 1)].rearrange("a p n m -> (a p) n m")
                sp.wait_ge(s_norm.sem, s_norm.at(turn, 8 * NT))
                sp.dma_start(o_out, x[:, :, :]).then_inc(s_out.sem, 16)
                stored = sp.snap(s_out.at(turn, 16))
                sp.wait_ge(s_w.sem, 16)
                sp.wait_ge(s_out.sem, stored)

        @block.tensor
        def _(pe):
            def product(dst, lhs_rhs):
                for i, (lhs, rhs) in enumerate(lhs_rhs):
                    ins_ = pe.matmul(dst, lhs, rhs, start=(i == 0), stop=(i == len(lhs_rhs) - 1))
                return ins_

            pe.wait_ge(s_c.sem, 16 * 5)
            pe.wait_ge(s_w.sem, 16)
            a_fc, b_fc = lora[:, 0:D], lora[:, D:D + F]
            a_pr, b_pr = lora[:, D + F:D + 2 * F], lora[:, D + 2 * F:2 * D + 2 * F]
            for c in range(NC):
                for n in range(F // BANK):
                    i = pe.matmul(bank(2 * c + n), a_fc[:, c * P:(c + 1) * P], b_fc[:, n * BANK:(n + 1) * BANK],
                                  start=True, stop=True)
            i.then_inc(s_lora.sem, 1)
            for f in range(NF):
                i = pe.matmul(ps[:, 4 * BANK + f * D:4 * BANK + (f + 1) * D], a_pr[:, f * P:(f + 1) * P], b_pr,
                              start=True, stop=True)
            i.then_inc(s_lora.sem, 1)
            pe.wait_ge(s_prep.sem, 1)

            with pe.Fori(0, NB) as turn:
                gates = w("gates").rearrange("p (g c n) -> p g c n", g=2, c=NC)
                pe.wait_ge(s_x.sem, s_x.at(turn, 16 * 2))
                for g in range(2):
                    for c in range(NC):
                        i = pe.matmul(bank(2 * g + c), gates[:, g, c, :], xt[:, c, :], start=True, stop=True)
                i.then_inc(s_gates.sem, 1)
                pe.wait_ge(s_rg.sem, s_rg.at(turn, 1))
                for t in range(NT):
                    for c in range(NC):
                        i = pe.transpose(ps[:, 4 * BANK + t * D + c * P:4 * BANK + t * D + (c + 1) * P],
                                         xt[:, c, t * P:(t + 1) * P], identf)
                    i.then_inc(s_z.sem, 1)

                def to_feature_major(n, norm, src):
                    for t in range(NT):
                        pe.wait_ge(s_norm.sem, s_norm.at(turn, NT * norm + t + 1))
                        for c in range(NC):
                            i = pe.transpose(ps[:, (6 + c) * BANK + t * P:(6 + c) * BANK + (t + 1) * P],
                                             src[:, t, c * P:(c + 1) * P], identf)
                    i.then_inc(s_xtp.sem, 1)
                    pe.wait_ge(s_xt.sem, s_xt.at(turn, n + 1))

                def project(a, q, k, v, q_src, kv_src, nk=NC):
                    for c in range(NC):
                        i = product(bank(c), [(q[:, n, c * P:(c + 1) * P], q_src[:, n, :]) for n in range(NC)])
                    i.then_inc(s_proj.sem, 1)
                    for c in range(NC):
                        i = product(bank(2 + c), [(k[:, n, c * P:(c + 1) * P], kv_src[:, n, :]) for n in range(nk)])
                    i.then_inc(s_proj.sem, 1)
                    for t in range(NT):
                        i = product(ps[:, 4 * BANK + t * D:4 * BANK + (t + 1) * D],
                                    [(kv_src[:, n, t * P:(t + 1) * P], v[:, n, :]) for n in range(nk)])
                    i.then_inc(s_proj.sem, 1)

                def attend(a, kind):
                    rows = ALL_ROWS - 3 if kind == ALIBI else ROWS
                    pe.wait_ge(s_op.sem, s_op.at(turn, 16 * 12 * (a + 1)))
                    pe.wait_ge(s_va.sem, s_va.at(turn, a + 1))
                    if kind == ALIBI:
                        pe.wait_ge(s_alibi.sem, s_alibi.at(turn, 32))
                    score, key = J * QUADS_BEFORE[kind], 2 * QUADS_BEFORE[kind]
                    for what, g, s in steps_of(kind):
                        heads = range(J * g, J * g + J)
                        if what == "S":
                            for h in heads:
                                if score >= 2:
                                    pe.wait_ge(s_max.sem, s_max.at(turn, score - 1))
                                dst = bank(score % 2)
                                if kind == WINDOW:
                                    for q in range(NT):
                                        t = slice(q * P, (q + 1) * P)
                                        i = pe.matmul(dst[:, t], qs[0:rows, h, t], ks[0:rows, h, t], start=True, stop=True)
                                elif kind == CAUSAL:
                                    t = slice(s * P, (s + 1) * P)
                                    pe.matmul(dst[:, 0:(s + 1) * P], qs[0:rows, h, t], ks[0:rows, h, 0:(s + 1) * P],
                                              start=True, stop=False)
                                    i = pe.matmul(dst[:, t], identb, tri_q, start=False, stop=True)
                                else:
                                    t = slice(s * P, (s + 1) * P)
                                    fix = corrections(h, s) if kind == ALIBI else []
                                    i = pe.matmul(dst, qs[0:rows, h, t], ks[0:rows, h, :], start=True, stop=not fix)
                                    for m, (d, col) in enumerate(fix):
                                        i = pe.matmul(dst[:, (s - d) * P:(s - d + 1) * P], clamp[:, col:col + P], identb,
                                                      start=False, stop=(m == len(fix) - 1))
                                i.then_inc(s_s.sem, 1)
                                score += 1
                        elif what == "M":
                            pe.wait_ge(s_mp.sem, s_mp.at(turn, G * a + g + 1))
                            if g > 0:
                                pe.wait_ge(s_mc.sem, s_mc.at(turn, G * a + g))
                            rows_out = bank(2).bitcast(BF16)
                            for q in range(NT):
                                i = pe.transpose(rows_out[0:3 * J, q * P:(q + 1) * P],
                                                 mp[:, g, q, :, :].rearrange("p i j -> p (i j)"), identb)
                            i.then_inc(s_mt.sem, 1)
                        elif what == "T":
                            pe.wait_ge(s_md.sem, s_md.at(turn, 16 * (G * a + g + 1)))
                            for n in range(J):
                                h = J * g + n
                                if n % 2 == 0 and key >= 2:
                                    pe.wait_ge(s_exp.sem, s_exp.at(turn, key - 1))
                                dst = bank(4 + 2 * (key % 2) + n % 2)
                                if kind == WINDOW:
                                    for q in range(NT):
                                        t = slice(q * P, (q + 1) * P)
                                        i = pe.matmul(dst[:, t], ks[0:rows + 3, h, t], qs[0:rows + 3, h, t], start=True, stop=True)
                                else:
                                    t = slice(s * P, (s + 1) * P)
                                    lo = s * P if kind == CAUSAL else 0
                                    d, np_ = CLAMPED.get(h, (NT, 0)) if kind == ALIBI else (NT, 0)
                                    fixed = [(d, p) for p in range(np_) if d + s < NT]
                                    if kind == MASKED:
                                        pe.matmul(dst, identb, negt[:, s, :], start=True, stop=False)
                                    i = pe.matmul(dst[:, lo:S], ks[0:rows + 3, h, t], qs[0:rows + 3, h, lo:S],
                                                  start=(kind != MASKED), stop=(kind != CAUSAL and not fixed))
                                    if kind == CAUSAL:
                                        i = pe.matmul(dst[:, t], identb, tri_k, start=False, stop=True)
                                    for m, (d, p) in enumerate(fixed):
                                        width = S - d * P
                                        col = CLAMP_AT[h] + p * width
                                        i = pe.matmul(dst[:, (d + s) * P:S], identb, clamp[:, col:col + S - (d + s) * P],
                                                      start=False, stop=(m == len(fixed) - 1))
                                if n % 2 == 1:
                                    i.then_inc(s_t.sem, 1)
                                    key += 1
                        else:
                            q_ = quad(kind, g, s)
                            pe.wait_ge(s_exp.sem, s_exp.at(turn, 2 * (q_ + 1)))
                            if kind == MASKED:
                                pe.wait_ge(s_pg.sem, s_pg.at(turn, NT * g + s + 1))
                            if s == 0 and (a or g):
                                pe.wait_ge(s_o.sem, s_o.at(turn, G * a + g))
                            slot = q_ % 2 if kind == MASKED else q_ % 3
                            first, last = s == 0, s == STEPS[kind] - 1
                            if kind == WINDOW:
                                for q in range(NT):
                                    t = slice(q * P, (q + 1) * P)
                                    for n in range(J):
                                        i = pe.matmul(bank(3)[32 * n:32 * n + 32, t], va[:, q, J * g + n, :],
                                                      prob[:, slot, n, t], start=True, stop=True, tile_position=(0, 32 * n))
                            elif kind == MASKED:
                                for n in range(J):
                                    pe.matmul(bank(3)[32 * n:32 * n + 32, :], ones[:, :], prob[:, slot, n, :],
                                              start=first, stop=False, tile_position=(0, 32 * n), skip_group_check=True)
                                for n in range(J):
                                    i = pe.matmul(bank(3)[32 * n:32 * n + 16, :], va[:, s, J * g + n, 0:HD],
                                                  prob[:, 2 + slot, n, :], start=False, stop=last,
                                                  tile_position=(0, 32 * n), skip_group_check=True)
                            else:
                                lo = s * P if kind == CAUSAL else 0
                                for n in range(J):
                                    i = pe.matmul(bank(3)[32 * n:32 * n + 32, lo:S], va[:, s, J * g + n, :],
                                                  prob[:, slot, n, lo:S], start=first, stop=last, tile_position=(0, 32 * n))
                            i.then_inc(s_pv.sem, 1)

                def project_out(a, wo):
                    pe.wait_ge(s_o.sem, s_o.at(turn, G * (a + 1)))
                    for t in range(NT):
                        i = product(ps[:, 4 * BANK + t * D:4 * BANK + (t + 1) * D],
                                    [(ot[:, g, t * P:(t + 1) * P], wo[:, g, :]) for g in range(G)])
                        i.then_inc(s_z.sem, 1)

                to_feature_major(0, 0, x)
                project(0, w3("l0_q", NC), w3("l0_k", NC), w3("l0_v", NC), xt, ct)
                attend(0, WINDOW)
                project_out(0, w3("l0_o", G))
                to_feature_major(1, 1, x)
                fc, proj = w3("fc", NC), w3("proj", NF)
                for m in range(NF):
                    if m >= 4:
                        pe.wait_ge(s_hc.sem, s_hc.at(turn, m - 3))
                    i = product(bank(m % 4), [(fc[:, n, m * P:(m + 1) * P], xt[:, n, :]) for n in range(NC)])
                    i.then_inc(s_h.sem, 1)
                pe.wait_ge(s_hc.sem, s_hc.at(turn, NF))
                for t in range(NT):
                    i = product(ps[:, 4 * BANK + t * D:4 * BANK + (t + 1) * D],
                                [(hid[:, m, t * P:(t + 1) * P], proj[:, m, :]) for m in range(NF)])
                    i.then_inc(s_z.sem, 1)
                to_feature_major(2, 2, x)
                project(1, w3("l1_q", NC), w3("l1_k", NC), w3("l1_v", NC), xt, xt)
                attend(1, ALIBI)
                project_out(1, w3("l1_o", G))
                to_feature_major(3, 3, x)
                project(2, w3("x_q", NC), w3("x_k", NC), w3("x_v", NC), xt, ct)
                pe.wait_ge(s_negt.sem, s_negt.at(turn, 1))
                attend(2, MASKED)
                project_out(2, w3("x_o", G))
                to_feature_major(4, 5, y)
                product(bank(6), [(w3("m_lat", NC)[:, n, :], xt[:, n, :]) for n in range(NC)]).then_inc(s_lat.sem, 1)
                pe.wait_ge(s_latc.sem, s_latc.at(turn, 1))
                lat = ct[:, 0:1, :]
                project(3, w3("m_q", NC), w3("m_k", 1), w3("m_v", 1), xt, lat, nk=1)
                attend(3, CAUSAL)
                project_out(3, w3("m_o", G))
                to_feature_major(5, 6, y)
                router = w3("router", NC)
                for t in range(NT):
                    i = product(bank(6)[:, t * NE:(t + 1) * NE], [(xt[:, n, t * P:(t + 1) * P], router[:, n, :]) for n in range(NC)])
                i.then_inc(s_router.sem, 1)

                def up(e):
                    pe.wait_ge(s_w1[e % 2].sem, s_w1[e % 2].at(turn, 16 * (e // 2 + 1)))
                    for m in range(NH):
                        pe.wait_ge(s_hc.sem, s_hc.at(turn, NF + NH * e + m - 3))
                        i = product(bank(m), [(w1[:, e % 2, n, m * P:(m + 1) * P], xt[:, n, :]) for n in range(NC)])
                        i.then_inc(s_h.sem, 1)

                def down(e):
                    pe.wait_ge(s_w2[e % 2].sem, s_w2[e % 2].at(turn, 16 * (e // 2 + 1)))
                    pe.wait_ge(s_hc.sem, s_hc.at(turn, NF + NH * (e + 1)))
                    if e == 1:
                        pe.wait_ge(s_dif.sem, s_dif.at(turn, 1))
                    for t in range(NT):
                        if e >= 2:
                            pe.wait_ge(s_ec.sem, s_ec.at(turn, NT * (e - 2) + 2 * (t // 2) + 2))
                        b = (4 if e % 2 == 0 else 6) * BANK
                        i = product(ps[:, b + t * D:b + (t + 1) * D],
                                    [(hid[:, NH * (e % 2) + m, t * P:(t + 1) * P], w2[:, e % 2, m, :]) for m in range(NH)])
                        i.then_inc(s_e.sem, 1)

                up(0)
                for e in range(NE):
                    if e + 1 < NE:
                        up(e + 1)
                    down(e)

        @block.scalar
        def _(act):
            step = Steps(s_act)
            act.wait_ge(s_sp.sem, 1)
            act.activation(small[:, 2:4], small[:, 0:2], ACT.Exp, scale=-1.0).then_inc(s_act.sem, step.one())
            act.wait_ge(s_act.sem, step.so_far())
            act.activation(small[:, 4:6], small[:, 2:4], ACT.Copy, bias=1.0).then_inc(s_act.sem, step.one())
            act.wait_ge(s_act.sem, step.so_far())
            act.activation(small[:, 6:8], small[:, 4:6], ACT.Ln).then_inc(s_act.sem, step.one())
            act.wait_ge(s_prep.sem, 1)

            with act.Fori(0, NB) as turn:
                step.begin(turn)

                act.wait_ge(s_gates.sem, s_gates.at(turn, 1))
                act.activation(tg.rearrange("p g c s -> p (g c s)"), bank(0, 4), ACT.Tanh, scale=0.5).then_inc(s_act.sem, step.one())
                act.wait_ge(s_act.sem, step.so_far())
                for c in range(NC):
                    i = act.activation(dec[:, c, :], tg[:, 1, c, :], ACT.Exp, bias=small[:, 12 + c:13 + c],
                                       scale=small[:, 12 + c:13 + c])
                i.then_inc(s_decay.sem, 1)
                act.wait_ge(s_sq.sem, s_sq.at(turn, 1))
                for c in range(NC):
                    i = act.activation(stp[:, c, :], stp[:, c, :], ACT.Sqrt, bias=small[:, 14:15], scale=-0.25)
                i.then_inc(s_mult.sem, 1)

                def copy_xt(n):
                    act.wait_ge(s_xtp.sem, s_xtp.at(turn, n + 1))
                    act.activation(xt[:, :, :].rearrange("p c s -> p (c s)"), bank(6, 2), ACT.Copy).then_inc(s_xt.sem, 1)

                def squares():
                    for t in range(NT):
                        i = act.activation(big[:, 6144 + t * D:6144 + (t + 1) * D], x[:, t, :], ACT.Square, accum_out=ve[:, t:t + 1])
                    return i

                def split(a, qb, kb):
                    for o, (b, scale) in enumerate(((qb, QSCALE), (kb, 1.0))):
                        act.wait_ge(s_proj.sem, s_proj.at(turn, 3 * a + o + 1))
                        for c in range(NC):
                            bias = b[:, c:c + 1] if b is not None else 0.0
                            i = act.activation(parts[:, o, 0, c, :], bank(2 * o + c), ACT.Identity, bias=bias, scale=scale)
                        i.then_inc(s_p[0].sem, 1)
                        for c in range(NC):
                            bias = b[:, c:c + 1] if b is not None else 0.0
                            i = act.activation(qk[:, o, c, :], bank(2 * o + c), ACT.Identity, bias=bias, scale=scale)
                        i.then_inc(s_f.sem, 1)

                def attend(a, kind):
                    key = 2 * QUADS_BEFORE[kind]
                    for what, g, s in steps_of(kind):
                        if what == "M":
                            act.wait_ge(s_mt.sem, s_mt.at(turn, G * a + g + 1))
                            if a or g:
                                act.wait_ge(s_md.sem, s_md.at(turn, 16 * (G * a + g)))
                            act.activation(mrow[:, :], bank(2)[0:3 * J, :].bitcast(BF16)[:, 0:S], ACT.Copy)\
                               .then_inc(s_mc.sem, 1)
                        elif what == "T":
                            q_ = quad(kind, g, s)
                            ring = 2 if kind == MASKED else 3
                            slot = q_ % ring
                            if q_ - ring >= QUADS_BEFORE[kind]:
                                act.wait_ge(s_pv.sem, s_pv.at(turn, q_ - ring + 1))
                            lo = s * P if kind == CAUSAL else 0
                            for pair in range(2):
                                act.wait_ge(s_t.sem, s_t.at(turn, key + 1))
                                src = bank(4 + 2 * (key % 2), 2).rearrange("p (j s) -> p j s", j=2)
                                act.activation(prob[:, slot, 2 * pair:2 * pair + 2, lo:S], src[:, :, lo:S], ACT.Exp)\
                                   .then_inc(s_exp.sem, 1)
                                key += 1

                copy_xt(0)
                split(0, small[:, 8:10], w("l0_kb"))
                attend(0, WINDOW)
                copy_xt(1)
                for m in range(NF):
                    act.wait_ge(s_h.sem, s_h.at(turn, m + 1))
                    act.activation(hid[:, m, :], bank(m % 4), ACT.Gelu, bias=w("fc_b")[:, m:m + 1]).then_inc(s_hc.sem, 1)
                copy_xt(2)
                split(1, small[:, 10:12], w("l1_kb"))
                attend(1, ALIBI)
                copy_xt(3)
                split(2, small[:, 16:18], w("x_kb"))
                attend(2, MASKED)
                act.wait_ge(s_norm.sem, s_norm.at(turn, 5 * NT))
                squares().then_inc(s_ss.sem, 1)
                copy_xt(4)
                act.wait_ge(s_lat.sem, s_lat.at(turn, 1))
                act.activation(ct[:, 0, :], bank(6), ACT.Copy).then_inc(s_latc.sem, 1)
                split(3, None, None)
                attend(3, CAUSAL)
                act.wait_ge(s_sum.sem, s_sum.at(turn, 1))
                squares().then_inc(s_ss.sem, 1)
                copy_xt(5)
                act.wait_ge(s_dif.sem, s_dif.at(turn, 1))
                act.activation(logit[:, 2, :], logit[:, 1, :], ACT.Exp).then_inc(s_rexp.sem, 1)
                for e in range(NE):
                    for m in range(NH):
                        if m == 0 and e >= 2:
                            act.wait_ge(s_e.sem, s_e.at(turn, NT * (e - 1)))
                        act.wait_ge(s_h.sem, s_h.at(turn, NF + NH * e + m + 1))
                        act.activation(hid[:, NH * (e % 2) + m, :], bank(m), ACT.Silu).then_inc(s_hc.sem, 1)
                step.end()

        @block.gpsimd
        def _(pool):
            pool.memset(va[:, :, :, :].rearrange("p t h n -> p (t h n)"), 1.0).then_inc(s_set.sem, 1)
            pool.memset(ones[:, 0:HD], 0.0).then_inc(s_set.sem, 1)
            pool.memset(ones[:, HD:32], 1.0).then_inc(s_set.sem, 1)
            pool.memset(small[:, 14:15], 0.25).then_inc(s_set.sem, 1)
            for n in range(2):
                pool.wait_ge(s_amax.sem, n + 1)
                pool.partition_all_reduce(small[:, 20 + n:21 + n], small[:, 18 + n:19 + n], P, RMAX)\
                    .then_inc(s_amaxall.sem, 1)
            pool.wait_ge(s_c.sem, 16 * 5)

            with pool.Fori(0, NB) as turn:
                def inverse_root(n):
                    pool.wait_ge(s_var.sem, s_var.at(turn, n + 1))
                    pool.tensor_tensor(rstd[:, :], ve[:, :], half[:, :], ALU.pow).then_inc(s_rstd.sem, 1)

                def add_bias(n, name):
                    pool.wait_ge(s_xtp.sem, s_xtp.at(turn, n + 1))
                    pool.tensor_tensor(x[:, :, :], x[:, :, :], w(name).rearrange("p (a n) -> p a n", a=1)
                                       .to_broadcast([P, NT, D]), ALU.add).then_inc(s_bias.sem, 1)

                for n, name in enumerate(("l0_ob", "proj_b", "l1_ob", "x_ob")):
                    inverse_root(n)
                    add_bias(n, name)
                for n in range(4, 8):
                    inverse_root(n)

        @block.vector
        def _(dve):
            step = Steps(s_vec)
            dve.wait_ge(s_w.sem, 16)
            dve.wait_ge(s_set.sem, 4)
            ap = w("a_param")
            dve.tensor_scalar(small[:, 0:2], ap, -1.0, None, ALU.mult).then_inc(s_vec.sem, step.one())
            dve.wait_ge(s_vec.sem, step.so_far())
            dve.tensor_tensor(small[:, 0:2], small[:, 0:2], ap, ALU.max).then_inc(s_sp.sem, 1)
            for name, at in (("l0_qb", 8), ("l1_qb", 10), ("x_qb", 16)):
                dve.tensor_scalar(small[:, at:at + 2], w(name), QSCALE, None, ALU.mult).then_inc(s_vec.sem, step.one())
            for n, name in enumerate(("fc", "proj")):
                dve.tensor_reduce(small[:, 18 + n:19 + n], w(name), AX.X, ALU.max, apply_absolute_value=True)\
                   .then_inc(s_amax.sem, 1)
            scale, inv = small[:, 20:22], small[:, 22:24]
            dve.wait_ge(s_amaxall.sem, 2)
            dve.tensor_scalar(scale, scale, 1.0 / QMAX, None, ALU.mult).then_inc(s_vec.sem, step.one())
            dve.wait_ge(s_vec.sem, step.so_far())
            dve.reciprocal(inv, scale).then_inc(s_vec.sem, step.one())
            dve.wait_ge(s_vec.sem, step.so_far())
            for n, name in enumerate(("fc", "proj")):
                wt = w(name)
                dve.tensor_scalar(qtmp, wt, inv[:, n:n + 1], ROUND, ALU.mult, ALU.add).then_inc(s_vec.sem, step.one())
                dve.wait_ge(s_vec.sem, step.so_far())
                dve.tensor_scalar(qtmp, qtmp, -ROUND, QMAX, ALU.add, ALU.min).then_inc(s_vec.sem, step.one())
                dve.wait_ge(s_vec.sem, step.so_far())
                dve.tensor_scalar(qtmp, qtmp, -QMAX - 1.0, scale[:, n:n + 1], ALU.max, ALU.mult).then_inc(s_vec.sem, step.one())
                dve.wait_ge(s_vec.sem, step.so_far())
                dve.tensor_tensor(qtmp, qtmp, wt, ALU.subtract).then_inc(s_vec.sem, step.one())
                dve.wait_ge(s_vec.sem, step.so_far())
                dve.tensor_tensor(wt, wt, qtmp, ALU.add).then_inc(s_vec.sem, step.one())
                dve.wait_ge(s_vec.sem, step.so_far())
                dve.wait_ge(s_lora.sem, n + 1)
                dve.scalar_tensor_tensor(wt, bank(4 * n, 4), LORA_SCALING, wt, ALU.mult, ALU.add).then_inc(s_vec.sem, step.one())
            dve.wait_ge(s_act.sem, ACT_ONCE)
            e_, u_, l_ = small[:, 2:4], small[:, 4:6], small[:, 6:8]
            dve.tensor_scalar(u_, u_, -1.0, 1e-30, ALU.add, ALU.add).then_inc(s_vec.sem, step.one())
            dve.tensor_scalar(l_, l_, 1e-30, None, ALU.add).then_inc(s_vec.sem, step.one())
            dve.wait_ge(s_vec.sem, step.so_far())
            dve.reciprocal(u_, u_).then_inc(s_vec.sem, step.one())
            dve.wait_ge(s_vec.sem, step.so_far())
            dve.tensor_tensor(l_, l_, u_, ALU.mult).then_inc(s_vec.sem, step.one())
            dve.wait_ge(s_vec.sem, step.so_far())
            dve.tensor_tensor(l_, l_, e_, ALU.mult).then_inc(s_vec.sem, step.one())
            dve.tensor_scalar(small[:, 12:14], ap, 0.0, None, ALU.max).then_inc(s_vec.sem, step.one())
            dve.wait_ge(s_vec.sem, step.so_far())
            dve.tensor_tensor(l_, l_, small[:, 12:14], ALU.add).then_inc(s_vec.sem, step.one())
            dve.wait_ge(s_vec.sem, step.so_far())
            dve.tensor_scalar(small[:, 12:14], l_, -4.0, None, ALU.mult).then_inc(s_prep.sem, 1)

            with dve.Fori(0, NB) as turn:
                step.begin(turn)

                carried = []

                def carry():
                    dve.memset(spare[:, len(carried):len(carried) + 1], 0.0)
                    carried.append(0)

                def z(t):
                    return ps[:, 4 * BANK + t * D:4 * BANK + (t + 1) * D]

                dve.wait_ge(s_decay.sem, s_decay.at(turn, 1))
                dve.tensor_tensor(stp, dec, dec, ALU.mult).then_inc(s_vec.sem, step.one())
                dve.wait_ge(s_vec.sem, step.so_far())
                dve.tensor_scalar(stp, stp, 1.0, None, ALU.min).then_inc(s_sq.sem, 1)
                dve.scalar_tensor_tensor(gx, tg[:, 0, :, :], 1.0, xt[:, :, :], ALU.add, ALU.mult).then_inc(s_vec.sem, step.one())
                dve.wait_ge(s_vec.sem, step.so_far())
                dve.wait_ge(s_mult.sem, s_mult.at(turn, 1))
                dve.tensor_tensor(gx, gx, stp, ALU.mult).then_inc(s_vec.sem, step.one())
                dve.wait_ge(s_vec.sem, step.so_far())
                for c in range(NC):
                    dve.tensor_tensor_scan(st[:, c, :], dec[:, c, :], gx[:, c, :], 0.0, ALU.mult, ALU.add).then_inc(s_vec.sem, step.one())
                dve.wait_ge(s_vec.sem, step.so_far())
                dve.tensor_tensor(xt[:, :, :], xt[:, :, :], st, ALU.add).then_inc(s_rg.sem, 1)

                def moments(n, src):
                    for t in range(NT):
                        dve.bn_stats(stats[:, t, :], src(t)).then_inc(s_vec.sem, step.one())
                    dve.wait_ge(s_vec.sem, step.so_far())
                    carry()
                    for t in range(NT):
                        dve.bn_aggr(mv[:, t, :], stats[:, t, :]).then_inc(s_vec.sem, step.one())
                    dve.wait_ge(s_vec.sem, step.so_far())
                    dve.tensor_scalar(ve[:, :], mv[:, :, 1], LN_EPS, None, ALU.add).then_inc(s_var.sem, 1)
                    dve.wait_ge(s_rstd.sem, s_rstd.at(turn, n + 1))
                    for t in range(NT):
                        dve.tensor_scalar(x[:, t, :], src(t), mv[:, t, 0:1], rstd[:, t:t + 1],
                                          ALU.subtract, ALU.mult).then_inc(s_norm.sem, 1)

                def layer_norm(n, zi):
                    for t in range(NT):
                        if t % 2 == 0:
                            dve.wait_ge(s_z.sem, s_z.at(turn, NT * zi + t + 2))
                        if zi and t == 0:
                            dve.wait_ge(s_bias.sem, s_bias.at(turn, zi))
                        if zi:
                            dve.tensor_tensor(y[:, t, :], z(t), x[:, t, :], ALU.add).then_inc(s_vec.sem, step.one())
                    if zi:
                        dve.wait_ge(s_vec.sem, step.so_far())
                    moments(n, (lambda t: y[:, t, :]) if zi else z)

                def rms_norm(n, k, gain):
                    dve.wait_ge(s_ss.sem, s_ss.at(turn, k + 1))
                    dve.tensor_scalar(ve[:, :], ve[:, :], 1.0 / D, RMS_EPS, ALU.mult, ALU.add).then_inc(s_var.sem, 1)
                    dve.wait_ge(s_rstd.sem, s_rstd.at(turn, n + 1))
                    for t in range(NT):
                        dve.scalar_tensor_tensor(y[:, t, :], x[:, t, :], rstd[:, t:t + 1], w(gain), ALU.mult, ALU.mult)\
                           .then_inc(s_norm.sem, 1)

                def split(a, vb):
                    for o in range(2):
                        f = qk[:, o, :, :]
                        dve.wait_ge(s_f.sem, s_f.at(turn, 2 * a + o + 1))
                        dve.tensor_tensor(f, f, parts[:, o, 0, :, :], ALU.subtract).then_inc(s_vec.sem, step.one())
                        dve.wait_ge(s_vec.sem, step.so_far())
                        dve.tensor_copy(parts[:, o, 1, :, :], f).then_inc(s_p[1].sem, 1)
                        dve.wait_ge(s_p[1].sem, s_p[1].at(turn, 2 * a + o + 1))
                        dve.tensor_tensor(parts[:, o, 2, :, :], f, parts[:, o, 1, :, :], ALU.subtract)\
                           .then_inc(s_p[2].sem, 1)
                    dve.wait_ge(s_proj.sem, s_proj.at(turn, 3 * a + 3))
                    vout = va[:, :, :, 0:HD]
                    vin = bank(4, 2).rearrange("p (t h d) -> p t h d", t=NT, h=H)
                    if vb is None:
                        i = dve.tensor_copy(vout, vin)
                    else:
                        for t in range(NT):
                            i = dve.tensor_tensor(vout[:, t, :, :], vin[:, t, :, :],
                                                  w(vb).rearrange("p (h d) -> p h d", h=H), ALU.add)
                    i.then_inc(s_va.sem, 1)

                def attend(a, kind):
                    score = J * QUADS_BEFORE[kind]
                    for what, g, s in steps_of(kind):
                        if what == "S":
                            for n in range(J):
                                dve.wait_ge(s_s.sem, s_s.at(turn, score + 1))
                                if kind == MASKED:
                                    carry()
                                src = bank(score % 2)
                                if kind == WINDOW:
                                    i = dve.tensor_reduce(mx[:, g, :, n], src.rearrange("p (q k) -> p q k", q=NT), AX.X, ALU.max)
                                elif kind == MASKED:
                                    i = dve.tensor_tensor_reduce(out=src, in0=src, in1=neg[:, s, :], scale=1.0, scalar=LOWEST,
                                                                 op0=ALU.add, op1=ALU.max, accum_out=mx[:, g, s, n:n + 1])
                                else:
                                    width = (s + 1) * P if kind == CAUSAL else S
                                    i = dve.tensor_reduce(mx[:, g, s, n:n + 1], src[:, 0:width], AX.X, ALU.max)
                                i.then_inc(s_max.sem, 1)
                                score += 1
                        elif what == "M":
                            m, p3 = mx[:, g, :, :], mp[:, g, :, :, :]
                            dve.wait_ge(s_max.sem, s_max.at(turn, score))
                            dve.tensor_scalar(p3[:, :, 0, :], m, -1.0, None, ALU.mult).then_inc(s_vec.sem, step.one())
                            dve.wait_ge(s_vec.sem, step.so_far())
                            dve.scalar_tensor_tensor(mr[:, :, :], m, -1.0, p3[:, :, 0, :], ALU.mult, ALU.subtract).then_inc(s_vec.sem, step.one())
                            dve.wait_ge(s_vec.sem, step.so_far())
                            dve.tensor_copy(p3[:, :, 1, :], mr[:, :, :]).then_inc(s_vec.sem, step.one())
                            dve.wait_ge(s_vec.sem, step.so_far())
                            dve.tensor_tensor(p3[:, :, 2, :], mr[:, :, :], p3[:, :, 1, :], ALU.subtract).then_inc(s_mp.sem, 1)
                        elif what == "T":
                            if kind == MASKED:
                                q_ = quad(kind, g, s)
                                slot = q_ % 2
                                dve.wait_ge(s_exp.sem, s_exp.at(turn, 2 * (q_ + 1)))
                                if q_ - 2 >= QUADS_BEFORE[kind]:
                                    dve.wait_ge(s_pv.sem, s_pv.at(turn, q_ - 1))
                                if NT * g + s == 0:
                                    dve.wait_ge(s_side.sem, s_side.at(turn, 16 * 3))
                                for n in range(J):
                                    i = dve.tensor_tensor(prob[:, 2 + slot, n, :], prob[:, slot, n, :], grp[:, s, :], ALU.mult)
                                i.then_inc(s_pg.sem, 1)
                        elif s == STEPS[kind] - 1:
                            dve.wait_ge(s_pv.sem, s_pv.at(turn, quad(kind, g, s) + 1))
                            dve.reciprocal(recip, bank(3)).then_inc(s_vec.sem, step.one())
                            dve.wait_ge(s_vec.sem, step.so_far())
                            carry()
                            dve.stream_shuffle(rinv, recip, [HD] * 32).then_inc(s_vec.sem, step.one())
                            dve.wait_ge(s_vec.sem, step.so_far())
                            dve.tensor_tensor(ot[:, g, :], bank(3), rinv, ALU.mult).then_inc(s_o.sem, 1)

                layer_norm(0, 0)
                split(0, "l0_vb")
                attend(0, WINDOW)
                layer_norm(1, 1)
                layer_norm(2, 2)
                split(1, "l1_vb")
                attend(1, ALIBI)
                layer_norm(3, 3)
                dve.wait_ge(s_side.sem, s_side.at(turn, 16 * 2))
                dve.tensor_scalar(neg, neg.bitcast(I32), -NEG, NEG, ALU.mult, ALU.add).then_inc(s_vec.sem, step.one())
                dve.tensor_scalar(negt, grp.bitcast(I32), -NEG, NEG, ALU.mult, ALU.add).then_inc(s_negt.sem, 1)
                dve.wait_ge(s_vec.sem, step.so_far())
                split(2, "x_vb")
                attend(2, MASKED)
                layer_norm(4, 4)
                rms_norm(5, 0, "g1")
                split(3, None)
                attend(3, CAUSAL)
                for t in range(NT):
                    if t % 2 == 0:
                        dve.wait_ge(s_z.sem, s_z.at(turn, NT * 5 + t + 2))
                    dve.scalar_tensor_tensor(base[:, t, :], x[:, t, :], 2.0, z(t), ALU.mult, ALU.add).then_inc(s_vec.sem, step.one())
                dve.wait_ge(s_vec.sem, step.so_far())
                for t in range(NT):
                    i = dve.tensor_tensor(x[:, t, :], z(t), x[:, t, :], ALU.add)
                i.then_inc(s_sum.sem, 1)
                rms_norm(6, 1, "g2")

                lg, ld, le, lr = (logit[:, i, :] for i in range(4))
                te = "p (t e) -> p t e"
                dve.wait_ge(s_router.sem, s_router.at(turn, 1))
                dve.tensor_copy(lg, bank(6)[:, 0:NT * NE]).then_inc(s_vec.sem, step.one())
                dve.wait_ge(s_vec.sem, step.so_far())
                dve.tensor_reduce(gat[:, 0, :], lg.rearrange(te, t=NT), AX.X, ALU.max).then_inc(s_vec.sem, step.one())
                l3 = lg.rearrange(te, t=NT)
                dve.wait_ge(s_vec.sem, step.so_far())
                for t in range(NT):
                    i = dve.tensor_scalar(ld[:, t * NE:(t + 1) * NE], lg[:, t * NE:(t + 1) * NE], gat[:, 0, t:t + 1], None,
                                          ALU.subtract)
                i.then_inc(s_dif.sem, 1)
                for t in range(NT):
                    other = l3[:, t:t + 1, :].to_broadcast([P, NE, NE])
                    own = l3[:, t, :].rearrange("p (e a) -> p e a", a=1).to_broadcast([P, NE, NE])
                    for i, op in enumerate((ALU.is_gt, ALU.is_equal)):
                        dve.tensor_tensor(rank[:, i, t * NE * NE:(t + 1) * NE * NE].rearrange("p (e f) -> p e f", e=NE),
                                                    other, own, op).then_inc(s_vec.sem, step.one())
                dve.wait_ge(s_vec.sem, step.so_far())
                for t in range(NT):
                    r1 = rank[:, 1, t * NE * NE:(t + 1) * NE * NE]
                    dve.tensor_tensor(r1, r1, w("before"), ALU.mult).then_inc(s_vec.sem, step.one())
                dve.wait_ge(s_vec.sem, step.so_far())
                dve.tensor_tensor(rank[:, 0, :], rank[:, 0, :], rank[:, 1, :], ALU.add).then_inc(s_vec.sem, step.one())
                dve.wait_ge(s_vec.sem, step.so_far())
                dve.tensor_reduce(lr, rank[:, 0, :].rearrange("p (a f) -> p a f", f=NE), AX.X, ALU.add).then_inc(s_vec.sem, step.one())
                dve.wait_ge(s_vec.sem, step.so_far())
                dve.wait_ge(s_rexp.sem, s_rexp.at(turn, 1))
                dve.scalar_tensor_tensor(lr, lr, 2.0, le, ALU.is_lt, ALU.mult).then_inc(s_vec.sem, step.one())
                dve.wait_ge(s_vec.sem, step.so_far())
                dve.tensor_reduce(gat[:, 1, :], lr.rearrange(te, t=NT), AX.X, ALU.add).then_inc(s_vec.sem, step.one())
                dve.wait_ge(s_vec.sem, step.so_far())
                dve.reciprocal(gat[:, 2, :], gat[:, 1, :]).then_inc(s_vec.sem, step.one())
                dve.wait_ge(s_vec.sem, step.so_far())
                for t in range(NT):
                    dve.tensor_scalar(comb[:, t, :], lr[:, t * NE:(t + 1) * NE], gat[:, 2, t:t + 1], None, ALU.mult).then_inc(s_vec.sem, step.one())
                dve.wait_ge(s_vec.sem, step.so_far())
                for e in range(NE):
                    for t in range(NT):
                        if t % 2 == 0:
                            dve.wait_ge(s_e.sem, s_e.at(turn, NT * e + t + 2))
                        if e > 0:
                            dve.wait_ge(s_ec.sem, s_ec.at(turn, NT * (e - 1) + t + 1))
                        b = (4 if e % 2 == 0 else 6) * BANK
                        dve.scalar_tensor_tensor(y[:, t, :], ps[:, b + t * D:b + (t + 1) * D], comb[:, t, e:e + 1],
                                                 base[:, t, :] if e == 0 else y[:, t, :], ALU.mult, ALU.add)\
                           .then_inc(s_ec.sem, 1)
                dve.wait_ge(s_ec.sem, s_ec.at(turn, NE * NT))
                moments(7, lambda t: y[:, t, :])
                step.end()


def by_heads(np, v):
    a = v.reshape(v.shape[:-1] + (H // NC, NC, HD))
    return np.ascontiguousarray(np.moveaxis(a, (-3, -2, -1), (-1, -3, -2))).reshape(v.shape)


def lay_out(np, i):
    def rows(m):
        return np.ascontiguousarray(m.reshape(m.shape[0] // P, P, -1).transpose(1, 0, 2)).reshape(P, -1)

    def padded(m):
        out = np.zeros((G, J, 32, D), np.float32)
        out[:, :, 0:HD] = m.reshape(G, J, HD, D)
        return np.ascontiguousarray(out.reshape(G, P, D).transpose(1, 0, 2)).reshape(P, G * D)

    def column(v):
        return np.ascontiguousarray(v.reshape(-1, P).T)

    def everywhere(v):
        return np.broadcast_to(v.reshape(1, -1), (P, v.size))

    def diagonal(m):
        out = np.zeros((NC, P, P), np.float32)
        for h in range(8):
            c, at = h // 4, 32 * (h % 4)
            out[c, at:at + 32, at:at + 32] = m[h]
        return np.ascontiguousarray(out.transpose(1, 0, 2)).reshape(P, NC * P)

    w0, b0 = i["L0_xattn_in_proj_w"], i["L0_xattn_in_proj_b"]
    w1, b1 = i["L1_attn_in_proj_weight"], i["L1_attn_in_proj_bias"]
    p = {
        "gates": np.concatenate([diagonal(i["L0_attn_w_in"]), diagonal(i["L0_attn_w_a"])], 1),
        "a_param": column(i["L0_attn_a_param"]),
        "fc": rows(i["L0_ffn_W_fc"].T), "fc_b": column(i["L0_ffn_b_fc"]),
        "proj": rows(i["L0_ffn_W_proj"].T), "proj_b": everywhere(i["L0_ffn_b_proj"]),
        "m_q": rows(by_heads(np, i["L1_ffn_Wq"])), "m_lat": rows(i["L1_ffn_Wdkv"]),
        "m_k": rows(by_heads(np, i["L1_ffn_Wuk"])), "m_v": rows(i["L1_ffn_Wuv"]),
        "m_o": padded(i["L1_ffn_Wo"]), "g1": everywhere(i["L1_ffn_g1"]), "g2": everywhere(i["L1_ffn_g2"]),
        "router": rows(i["L1_ffn_gate_w"]), "ident": np.eye(P, dtype=np.float32),
        "before": everywhere(np.tril(np.ones((NE, NE), np.float32), -1)),
    }
    for name, wq, wk, wv, wo, bq, bk, bv, bo in (
        ("l0", w0[:D].T, w0[D:2 * D].T, w0[2 * D:].T, i["L0_xattn_out_w"].T,
         b0[:D], b0[D:2 * D], b0[2 * D:], i["L0_xattn_out_b"]),
        ("l1", w1[:D].T, w1[D:2 * D].T, w1[2 * D:].T, i["L1_attn_out_proj_weight"].T,
         b1[:D], b1[D:2 * D], b1[2 * D:], i["L1_attn_out_proj_bias"]),
        ("x", i["L1_xattn_wq_k"], i["L1_xattn_wk_k"], i["L1_xattn_wv_k"], i["L1_xattn_wo_k"],
         i["L1_xattn_wq_b"], i["L1_xattn_wk_b"], i["L1_xattn_wv_b"], i["L1_xattn_wo_b"]),
    ):
        p |= {name + "_q": rows(by_heads(np, wq)), name + "_k": rows(by_heads(np, wk)), name + "_v": rows(wv),
              name + "_o": padded(wo), name + "_qb": column(by_heads(np, bq)), name + "_kb": column(by_heads(np, bk)),
              name + "_vb": everywhere(bv), name + "_ob": everywhere(bo)}
    pack = np.concatenate([p[name].reshape(P, n) for name, n in PACK], 1)

    def tiles(a):
        return np.ascontiguousarray(a.reshape(NB, a.shape[1] // P, P, a.shape[2]).transpose(0, 2, 1, 3))

    return {
        "pack": pack,
        "lora": np.concatenate([i["L0_ffn_A_fc"], i["L0_ffn_B_fc"].T, i["L0_ffn_A_proj"], i["L0_ffn_B_proj"].T], 1),
        "x": tiles(i["x"].transpose(0, 2, 1)), "c": tiles(i["ctx_1024"].transpose(0, 2, 1)),
        "group": tiles(i["fside_BxSxS2_0"].transpose(0, 2, 1)),
        "mask": tiles(i["mask_BxSxS2_ik1"]), "mask_t": tiles(i["mask_BxSxS2_ik1"].transpose(0, 2, 1)),
        "w1": np.ascontiguousarray(i["L1_ffn_w1"].reshape(NE, NC, P, EH).transpose(0, 2, 1, 3)),
        "w2": np.ascontiguousarray(i["L1_ffn_w2"].reshape(NE, NH, P, D).transpose(0, 2, 1, 3)),
    } | constants(np)


def constants(np):
    bf16 = mybir.dt.np(BF16)

    def in_parts(v):
        out = []
        for _ in range(3):
            out.append(v.astype(bf16))
            v = (v - out[-1].astype(np.float32)).astype(np.float32)
        return out

    slope = np.float32([2.0 ** -0.5 * (2.0 ** -0.5) ** n for n in range(H)])
    pos = np.arange(S, dtype=np.float32)
    line = (slope[:, None] * pos[None, :]).astype(np.float32)
    one = np.ones((3, H, S), bf16)
    k_rows = np.concatenate([one, np.stack(in_parts(-line)), one])
    clamp = np.zeros((P, CLAMP_COLS), bf16)
    for h, (d, n) in CLAMPED.items():
        rel = np.arange(d * P, S, dtype=np.float32)[None, :] - np.arange(P, dtype=np.float32)[:, None]
        fix = np.minimum(8.0 - rel * slope[h], 0.0).astype(np.float32)
        for m, part in enumerate(in_parts(fix)[:n]):
            clamp[:, CLAMP_AT[h] + m * (S - d * P):CLAMP_AT[h] + (m + 1) * (S - d * P)] = part
    q, k = np.arange(P)[:, None], np.arange(P)[None, :]
    const = np.concatenate([np.eye(P), np.where(k > q, NEG, 0.0), np.where(q > k, NEG, 0.0)], 1).astype(bf16)
    return {"k_rows": k_rows, "one_rows": one, "q_rows": np.stack(in_parts(line)), "clamp": clamp, "const": const,
            "half": np.full((P, NT), -0.5, np.float32)}


def kernel(**inputs):
    import numpy as np
    import concourse.bacc as bacc
    from concourse.bass_utils import run_bass_kernel_spmd

    arrays = lay_out(np, {k: np.asarray(v) for k, v in inputs.items()})
    nc = bacc.Bacc("TRN2", target_bir_lowering=False, num_devices=1)
    ins = {name: nc.dram_tensor(f"in_{name}", a.shape, mybir.dt.from_np(a.dtype), kind="ExternalInput").ap()
           for name, a in arrays.items()}
    out = nc.dram_tensor("out", (NB, P, NT, D), F32, kind="ExternalOutput").ap()
    decoder(nc, ins, out)
    result = run_bass_kernel_spmd(nc, [{f"in_{name}": a for name, a in arrays.items()}], core_ids=[0])
    tokens = result.results[0]["out"]
    return np.ascontiguousarray(tokens.transpose(0, 2, 1, 3)).reshape(NB, S, D)
```

```python
import concourse.bass as bass
from concourse import mybir
from contextlib import ExitStack

F32 = mybir.dt.float32
BF16 = mybir.dt.bfloat16
I32 = mybir.dt.int32
ALU = mybir.AluOpType
ACT = mybir.ActivationFunctionType
AX = mybir.AxisListType

P = 128
NB, S, D = 4, 512, 256
H, HD = 16, 16
NT = S // P
NC = D // P
G, J = 4, 4
F = 1024
NF = F // P
R = 16
LAT = 128
NE, EH = 8, 512
NH = EH // P
BANK = 512
QSCALE = 0.25
LN_EPS, RMS_EPS = 1e-5, 1e-6
LORA_SCALING = 2.0
QMAX = 127.0
ROUND = 1.5 * 2.0 ** 23
NEG = -998244352.0
LOWEST = -3.0e38
RMAX = bass.bass_isa.ReduceOp.max

Q_PARTS = (0, 0, 1, 1, 0, 2)
K_PARTS = (0, 1, 0, 1, 2, 0)
ROWS = len(Q_PARTS) * HD
Q_SLOPE = ROWS
K_SLOPE = ROWS + 3
ALL_ROWS = ROWS + 9

CLAMPED = {h: (0 if h < 7 else 1 if h < 9 else 2, 3 if h % 2 == 0 else 2) for h in range(11)}
CLAMP_AT = {}
_at = 0
for _h, (_d, _n) in CLAMPED.items():
    CLAMP_AT[_h] = _at
    _at += _n * (S - _d * P)
CLAMP_COLS = _at

PACK = [
    ("gates", 2 * NC * P), ("a_param", NC), ("l0_qb", NC), ("l0_kb", NC), ("l0_vb", D), ("l0_ob", D),
    ("fc", NC * F), ("fc_b", NF), ("proj", NF * D), ("proj_b", D),
    ("l1_qb", NC), ("l1_kb", NC), ("l1_vb", D), ("l1_ob", D),
    ("x_qb", NC), ("x_kb", NC), ("x_vb", D), ("x_ob", D), ("m_lat", NC * LAT),
    ("g1", D), ("g2", D), ("router", NC * NE), ("ident", P), ("before", NE * NE),
]
PACK_AT, _at = {}, 0
for _name, _n in PACK:
    PACK_AT[_name] = (_at, _n)
    _at += _n
PACK_COLS = _at
QKVO = 3 * NC * D + G * D
CONST = {"ident": 0, "tri_q": P, "tri_k": 2 * P}
CONST_COLS = 3 * P

WINDOW, ALIBI, MASKED, CAUSAL = range(4)
STEPS = {WINDOW: 1, ALIBI: NT, MASKED: NT, CAUSAL: NT}
KINDS = (WINDOW, ALIBI, MASKED, CAUSAL)
QUADS_BEFORE = {WINDOW: 0, ALIBI: G, MASKED: G * 5, CAUSAL: G * 9}
QUADS = G * 13


def corrections(h, q):
    first, n = CLAMPED.get(h, (NT, 0))
    return [(d, CLAMP_AT[h] + m * (S - first * P) + (d - first) * P) for d in range(first, q + 1) for m in range(n)]


def steps_of(kind):
    n, out = STEPS[kind], []
    ahead = [("S", g, s, pair) for g in range(G) for s in range(n) for pair in range(2)]
    waiting = []

    def scores(count):
        for _ in range(min(count, len(ahead))):
            out.append(ahead.pop(0))
            _, g, s, pair = out[-1]
            tick()
            if (s, pair) == (n - 1, 1):
                out.append(("P", g, 0, 0))
                waiting.append([M_AFTER[kind], ("M", g, 0, 0)])

    def tick():
        for entry in waiting:
            entry[0] -= 1
        take(lambda count, entry: count <= 0)

    def take(due):
        for late in [w for w in waiting if due(*w)]:
            waiting.remove(late)
            out.append(late[1])

    def way_out(g):
        out.append(("C", g, 0, 0))
        waiting.append([R_AFTER[kind], ("R", g, 0, 0)])
        waiting.append([N_AFTER[kind], ("N", g, 0, 0)])

    scores(2 * n + LEAD[kind])
    for g in range(G):
        for s in range(n):
            for pair in range(2):
                take(lambda count, entry: entry[:2] == ("M", g))
                out.append(("T", g, s, pair))
                tick()
                scores(1)
            if s > 0:
                out.append(("V", g, s - 1, 0))
            elif g > 0:
                take(lambda count, entry: entry[1] < g - 1)
                out.append(("V", g - 1, n - 1, 0))
                way_out(g - 1)
            if kind == MASKED:
                out.append(("E", g, s, 0))
    take(lambda count, entry: True)
    out.append(("V", G - 1, n - 1, 0))
    way_out(G - 1)
    take(lambda count, entry: True)
    return out


LEAD = {WINDOW: 2, ALIBI: 4, MASKED: 4, CAUSAL: 4}
R_AFTER = {WINDOW: 2, ALIBI: 4, MASKED: 3, CAUSAL: 4}
N_AFTER = {WINDOW: 4, ALIBI: 8, MASKED: 6, CAUSAL: 8}
M_AFTER = {WINDOW: 1, ALIBI: 2, MASKED: 2, CAUSAL: 2}

EXPERT_WORK = [("up", 0, 0)]
for _e in range(NE):
    EXPERT_WORK += [("up", _e, m) for m in range(1, NH)]
    EXPERT_WORK += [("up", _e + 1, 0)] if _e + 1 < NE else []
    EXPERT_WORK += [("down", _e, m) for m in range(NT // 2)]
ITEMS = len(EXPERT_WORK)
ITEM_AT = {w: k for k, w in enumerate(EXPERT_WORK)}
EH_SLOTS = NH + 1
EXPERT_BANKS = (6, 7)
TAIL_BANKS = (6, 7, 0, 1)


def fill_plan():
    plan, at = {}, 0

    def put(place, n):
        nonlocal at
        n = min(n, ITEMS - at)
        plan[place] = (at, at + n)
        at += n

    put("load", FILL["load"])
    put("gates", FILL["gates"])
    put("decay", FILL["decay"])
    put("rg", FILL["norm"])
    for a, kind in enumerate(KINDS):
        put(("xt", a), FILL["xt"])
        put(("project", a), FILL["project"])
        steps = steps_of(kind)
        for k, (what, g, s, pair) in enumerate(steps):
            put(("attend", a, k), 1 if (what, s, pair) in FILL["after"][kind] or (what, g) == ("N", G - 1) else 0)
        put(("norm", a), FILL["norm"])
        if a == 0:
            put("ffn_norm", FILL["norm"])
        if a == 2:
            put("rms", FILL["norm"])
    final = next(place for place, (_, end) in plan.items() if end == ITEMS)
    return plan, final


FILL = {"load": 0, "gates": 2, "decay": 2, "norm": 1, "xt": 0, "project": 3,
        "after": {WINDOW: (("V", 0, 0),), ALIBI: (("V", 1, 0), ("V", 3, 0)), MASKED: (("V", 0, 0), ("V", 2, 0)), CAUSAL: (("V", 1, 0),)}}
PLAN, FINAL = fill_plan()
assert FINAL[0] in ("attend", "project") and FINAL[1] == 3, FINAL
CATCH_UP = {"load", "gates", FINAL} | {(what, a) for what in ("xt", "project") for a in range(len(KINDS))}


class Events:

    def __init__(self, ctx, nc, name, per_turn, once=0):
        self.sem = ctx.enter_context(nc.semaphore(name))
        self.per_turn, self.once, self.name = per_turn, once, name

    def at(self, turn, count):
        return turn * self.per_turn + (self.once + count)

    def prior(self, turn, count):
        return turn * self.per_turn + (self.once + count - self.per_turn)


class Steps:

    def __init__(self, counted):
        self.counted, self.count, self.turn = counted, 0, None

    def one(self):
        self.count += 1
        return 1

    def so_far(self):
        return self.count if self.turn is None else self.counted.at(self.turn, self.count)

    def begin(self, turn):
        if self.turn is None:
            assert self.count == self.counted.once, (self.counted.name, "once", self.count)
        self.count, self.turn = 0, turn

    def end(self):
        assert self.count == self.counted.per_turn, (self.counted.name, "per turn", self.count)


VECTOR_ONCE, VECTOR_TURN = 25, 161
ACT_ONCE, ACT_TURN = 3, 1


def decoder(nc, ins, out):
    ctx = ExitStack()
    with ctx:
        def sb(name, shape, dt=F32):
            return ctx.enter_context(nc.sbuf_tensor(name, shape, dt))

        def events(name, per_turn, once=0):
            return Events(ctx, nc, name, per_turn, once)

        pack = sb("pack", [P, PACK_COLS])
        const = sb("const", [P, CONST_COLS], BF16)
        x = sb("x", [P, NT, D])
        y = sb("y", [P, NT, D])
        xt = sb("xt", [P, NC, S])
        ct = sb("ct", [P, NC, S])
        qs = sb("qs", [P, H, S], BF16)
        ks = sb("ks", [P, H, S], BF16)
        va = sb("va", [P, NT, H, 32])
        sums = sb("sums", [P, J * S // P])
        ones = sb("ones", [P, 32])
        ot = sb("ot", [P, G, S])
        big = sb("big", [P, 4 * J * S])
        side = sb("side", [P, max(CLAMP_COLS // 2, 2 * NT * S + NT * S // 2)])
        wa = sb("wa", [P, 2, QKVO])
        w1 = sb("w1", [P, 2, NC, EH])
        w2 = sb("w2", [P, 2, NH, D])
        ht = sb("ht", [P, NC, S])
        eh = sb("eh", [P, EH_SLOTS, S])
        ys = sb("ys", [P, NT, D])
        mx = sb("mx", [P, G, NT, J])
        mr = sb("mr", [P, NT, J])
        mp = sb("mp", [P, G, NT, 3, J], BF16)
        mrow = sb("mrow", [3 * J, S], BF16)
        stats = sb("stats", [P, NT, 6])
        mv = sb("mv", [P, NT, 2])
        ve = sb("ve", [P, NT])
        rstd = sb("rstd", [P, NT])
        fstats = sb("fstats", [P, NT, 6])
        fmv = sb("fmv", [P, NT, 2])
        fve = sb("fve", [P, NT])
        frstd = sb("frstd", [P, NT])
        half = sb("half", [P, NT])
        small = sb("small", [P, 24])
        logit = sb("logit", [P, 4, NT * NE])
        spare = sb("spare", [P, 88])
        comb = sb("comb", [P, NT, NE])
        gat = sb("gat", [P, 3, NT])
        ps = ctx.enter_context(nc.psum_tensor("ps", [P, 8 * BANK], F32))

        def bank(b, n=1):
            return ps[:, b * BANK:(b + n) * BANK]

        def attention_weights(a):
            at, out = wa[:, a % 2, :], []
            for n, c in enumerate((NC, NC, NC, G)):
                out.append(at[:, n * NC * D:(n * NC + c) * D].rearrange("p (c n) -> p c n", c=c))
            return out

        def w(name):
            at, n = PACK_AT[name]
            return pack[:, at:at + n]

        def w3(name, a):
            return w(name).rearrange("p (a n) -> p a n", a=a)

        def part(at, *dims):
            n = 1
            for d in dims:
                n *= d
            v = big[:, at:at + n]
            if len(dims) == 2:
                return v.rearrange("p (a b) -> p a b", a=dims[0])
            return v.rearrange("p (a b c) -> p a b c", a=dims[0], b=dims[1])

        tg = part(0, 2, NC, S)
        dec = part(2048, NC, S)
        stp = part(3072, NC, S)
        gx = part(4096, NC, S)
        st = part(5120, NC, S)
        qk = part(0, 2, NC, S)
        parts = big[:, 2048:2048 + 3072].bitcast(BF16).rearrange(
            "p (o i c s) -> p o i c s", o=2, i=3, c=NC)
        hid = part(0, NF, S)
        prob = part(0, 4, J, S)
        rank = big[:, 7168:7168 + 2 * NT * NE * NE].rearrange("p (a n) -> p a n", a=2)
        qtmp = big[:, 0:2048]
        lora = big[0:R, 2048:2048 + 2 * (D + F)]
        clamp = side[:, 0:CLAMP_COLS // 2].bitcast(BF16)
        grp = side[:, 0:NT * S].rearrange("p (a s) -> p a s", a=NT)
        neg = side[:, NT * S:2 * NT * S].rearrange("p (a s) -> p a s", a=NT)
        negt = side[:, 2 * NT * S:2 * NT * S + NT * S // 2].bitcast(BF16).rearrange(
            "p (a s) -> p a s", a=NT)
        rinv = xt[:, 0, :]
        sum_rows = ot[HD:P:32, :, :]
        recip_rows = xt[HD:P:32, 1, :]
        identf = w("ident")
        identb = const[:, CONST["ident"]:CONST["ident"] + P]
        tri_q = const[:, CONST["tri_q"]:CONST["tri_q"] + P]
        tri_k = const[:, CONST["tri_k"]:CONST["tri_k"] + P]

        s_w = events("weights_loaded", 0, 16)
        s_c = events("constants_loaded", 0, 16 * 5)
        s_set = events("buffers_set", 0, 4)
        s_amax = events("weight_max", 0, 2)
        s_amaxall = events("weight_max_everywhere", 0, 2)
        s_lora = events("lora_product", 0, 4)
        s_loraused = events("lora_used", 0, 4)
        s_sp = events("softplus_exp", 0, 2)
        s_prep = events("weights_prepared", 0, 1)
        s_x = events("inputs_loaded", 16 * 2)
        s_alibi = events("alibi_loaded", 16 * 2)
        s_side = events("group_and_mask_loaded", 16 * 3)
        s_vec = events("vector_steps", VECTOR_TURN, VECTOR_ONCE)
        s_act = events("scalar_steps", ACT_TURN, ACT_ONCE)
        s_gates = events("gates_ready", 1)
        s_decay = events("decay_ready", 1)
        s_sq = events("decay_squared", 1)
        s_mult = events("step_ready", 1)
        s_rg = events("recurrence_done", 1)
        s_z = events("output_tile_ready", 6 * NT)
        s_var = events("variance_ready", 7)
        s_rstd = events("rstd_ready", 7)
        s_norm = events("normalised_tile", 7 * NT)
        s_final = events("result_normalised", NT)
        s_fstat = events("result_statistics", NT)
        s_fmv = events("result_moments", NT)
        s_fvar = events("result_variance_ready", 1)
        s_frstd = events("result_rstd_ready", 1)
        s_xtp = events("transposed", 6)
        s_xt = events("feature_major_ready", 6)
        s_bias = events("residual_plus_bias", 4)
        s_proj = events("projection_ready", 12)
        s_lat = events("latent_ready", 1)
        s_latc = events("latent_copied", 1)
        s_f = events("q_or_k_float", 2 * 4)
        s_p = [events(f"part_{i}_ready", 2 * 4) for i in range(3)]
        s_negt = events("mask_turned", 1)
        s_sum = events("latent_attention_added", 1)
        s_op = events("operands_loaded", 16 * 12 * 4)
        s_va = events("values_ready", 4)
        s_s = events("scores_ready", J * QUADS)
        s_max = events("maximum_taken", J * QUADS)
        s_mp = events("maximum_split", 4 * G)
        s_mt = events("maximum_transposed", 4 * G)
        s_mc = events("maximum_copied", 4 * G)
        s_md = events("maximum_in_operand", 16 * 4 * G)
        s_t = events("key_major_ready", J * QUADS)
        s_exp = events("exp_done", J * QUADS)
        s_pg = events("grouped_by_vector", G * NT)
        s_pgp = events("grouped_by_gpsimd", G * NT)
        s_pv = events("values_summed", QUADS)
        s_oc = events("heads_copied", 4 * G)
        s_sum_in = events("sums_spread", 16 * 4 * G)
        s_rc = events("reciprocals_ready", 4 * G)
        s_rc_in = events("reciprocals_in_rows", 16 * 4 * G)
        s_o = events("heads_normalised", 4 * G)
        s_h = events("hidden_ready", NF)
        s_hc = events("hidden_done", NF)
        s_item = events("expert_product", ITEMS)
        s_th = events("expert_tanh", NE * NH)
        s_done = events("expert_item_done", ITEMS)
        s_router = events("router_ready", 1)
        s_dif = events("router_shifted", 1)
        s_rexp = events("router_exp", 1)
        s_w1 = [events(f"expert_up_{i}_loaded", 16 * NE // 2) for i in range(2)]
        s_w2 = [events(f"expert_down_{i}_loaded", 16 * NE // 2) for i in range(2)]
        s_wa = [events(f"attention_weights_{i}_loaded", 16 * 2) for i in range(2)]
        s_ss = events("squares_summed", 2)
        s_out = events("stored", 16)

        def quad(kind, g, s):
            return QUADS_BEFORE[kind] + g * STEPS[kind] + s

        block = ctx.enter_context(nc.Block())

        @block.sync
        def _(sp):
            sp.dma_start(pack[:, :], ins["pack"]).then_inc(s_w.sem, 16)
            sp.dma_start(lora, ins["lora"]).then_inc(s_c.sem, 16)
            sp.dma_start(const[:, :], ins["const"]).then_inc(s_c.sem, 16)
            sp.dma_start(ks[ROWS:ALL_ROWS, :, :], ins["k_rows"]).then_inc(s_c.sem, 16)
            sp.dma_start(qs[K_SLOPE:K_SLOPE + 3, :, :], ins["one_rows"]).then_inc(s_c.sem, 16)
            sp.dma_start(half[:, :], ins["half"]).then_inc(s_c.sem, 16)

            def weights_up(e):
                sp.dma_start(w1[:, e % 2, :, :], ins["w1"][e]).then_inc(s_w1[e % 2].sem, 16)

            def weights_down(e):
                sp.dma_start(w2[:, e % 2, :, :], ins["w2"][e]).then_inc(s_w2[e % 2].sem, 16)

            def first_experts():
                for e in range(2):
                    weights_up(e)
                    weights_down(e)

            def expert_items(turn, first, end):
                for k in range(first, end):
                    what, e, m = EXPERT_WORK[k]
                    if what == "up" and m == NH - 1 and e + 2 < NE:
                        sp.wait_ge(s_item.sem, s_item.prior(turn, k + 1))
                        weights_up(e + 2)
                    if what == "down" and m == NT // 2 - 1 and e + 2 < NE:
                        sp.wait_ge(s_item.sem, s_item.prior(turn, k + 1))
                        weights_down(e + 2)

            def store(turn, place):
                sp.wait_ge(s_final.sem, s_final.prior(turn, NT))
                sp.dma_start(place, ys[:, :, :]).then_inc(s_out.sem, 16)

            def sequence(turn, filled):
                def one(name):
                    return ins[name][bass.ds(turn, 1)].rearrange("a p n m -> (a p) n m")

                def fill(place):
                    if filled:
                        expert_items(turn, *PLAN[place])
                        if place == FINAL:
                            store(turn, o_out)

                def weights(a):
                    sp.dma_start(wa[:, a % 2, :], ins["attention"][a]).then_inc(s_wa[a % 2].sem, 16)

                x_in, c_in = one("x"), one("c")
                if filled:
                    o_out = out[bass.ds(turn - 1, 1)].rearrange("a p n m -> (a p) n m")
                g_in, m_in, mt_in = one("group"), one("mask"), one("mask_t")
                if filled:
                    sp.wait_ge(s_o.sem, s_o.prior(turn, 4 * G))
                sp.dma_start(xt[:, :, :], x_in).then_inc(s_x.sem, 16)
                sp.dma_start(ct[:, :, :], c_in).then_inc(s_x.sem, 16)
                if filled:
                    first_experts()
                weights(0)
                sp.dma_start(clamp, ins["clamp"]).then_inc(s_alibi.sem, 16)
                if filled:
                    sp.wait_ge(s_z.sem, s_z.prior(turn, 6 * NT))
                weights(1)
                fill("load")
                fill("gates")
                fill("decay")
                fill("rg")
                for a, kind in enumerate(KINDS):
                    if kind in (ALIBI, MASKED):
                        sp.wait_ge(s_z.sem, s_z.at(turn, NT * 2 * a))
                        weights(a + 1)
                    if kind == ALIBI:
                        sp.wait_ge(s_pv.sem, s_pv.at(turn, QUADS_BEFORE[ALIBI]))
                        sp.dma_start(qs[Q_SLOPE:Q_SLOPE + 3, :, :], ins["q_rows"]).then_inc(s_alibi.sem, 16)
                    if kind == MASKED:
                        sp.wait_ge(s_pv.sem, s_pv.at(turn, QUADS_BEFORE[MASKED]))
                        sp.dma_start(neg.bitcast(I32), m_in).then_inc(s_side.sem, 16)
                        sp.dma_start(grp.bitcast(I32), mt_in).then_inc(s_side.sem, 16)
                        sp.wait_ge(s_negt.sem, s_negt.at(turn, 1))
                        sp.dma_start(grp, g_in).then_inc(s_side.sem, 16)
                    for o, dst, slots in ((0, qs, Q_PARTS), (1, ks, K_PARTS)):
                        for i in range(3):
                            sp.wait_ge(s_p[i].sem, s_p[i].at(turn, 2 * a + o + 1))
                            for slot in range(6):
                                if slots[slot] == i:
                                    sp.dma_start(dst[slot * HD:(slot + 1) * HD, :, :], parts[:, o, i, :, :])\
                                      .then_inc(s_op.sem, 16)
                    at = Q_SLOPE + 6 if kind == ALIBI else ROWS
                    fill(("xt", a))
                    fill(("project", a))
                    for k, (what, g, s, half_) in enumerate(steps_of(kind)):
                        if what == "M":
                            sp.wait_ge(s_mc.sem, s_mc.at(turn, G * a + g + 1))
                            sp.dma_start(qs[at:at + 3, J * g:J * g + J, :], mrow[:, :]).then_inc(s_md.sem, 16)
                        if what == "C":
                            sp.wait_ge(s_oc.sem, s_oc.at(turn, G * a + g + 1))
                            sp.dma_start(sums[:, :], sum_rows[:, g, :]).then_inc(s_sum_in.sem, 16)
                        if what == "R":
                            sp.wait_ge(s_rc.sem, s_rc.at(turn, G * a + g + 1))
                            sp.dma_start(recip_rows, sums[:, :]).then_inc(s_rc_in.sem, 16)
                        fill(("attend", a, k))
                    fill(("norm", a))
                    if a == 0:
                        fill("ffn_norm")
                    if a == 2:
                        fill("rms")

            sequence(0, False)
            with sp.Fori(1, NB) as turn:
                sequence(turn, True)
            sp.wait_ge(s_o.sem, s_o.prior(NB, 4 * G))
            first_experts()
            expert_items(NB, 0, ITEMS)
            store(NB, out[NB - 1])
            sp.wait_ge(s_out.sem, s_out.at(NB - 1, 16))

        @block.tensor
        def _(pe):
            def product(dst, lhs_rhs):
                for i, (lhs, rhs) in enumerate(lhs_rhs):
                    ins_ = pe.matmul(dst, lhs, rhs, start=(i == 0), stop=(i == len(lhs_rhs) - 1))
                return ins_

            pe.wait_ge(s_c.sem, 16 * 5)
            pe.wait_ge(s_w.sem, 16)
            a_fc, b_fc = lora[:, 0:D], lora[:, D:D + F]
            a_pr, b_pr = lora[:, D + F:D + 2 * F], lora[:, D + 2 * F:2 * D + 2 * F]
            for c in range(NC):
                for n in range(F // BANK):
                    i = pe.matmul(bank(2 * c + n), a_fc[:, c * P:(c + 1) * P], b_fc[:, n * BANK:(n + 1) * BANK],
                                  start=True, stop=True)
            i.then_inc(s_lora.sem, 1)
            for f in range(NF):
                i = pe.matmul(ps[:, 4 * BANK + f * D:4 * BANK + (f + 1) * D], a_pr[:, f * P:(f + 1) * P], b_pr,
                              start=True, stop=True)
            i.then_inc(s_lora.sem, 1)
            pe.wait_ge(s_prep.sem, 1)

            def expert_items(turn, first, end, ring):
                for k in range(first, end):
                    what, e, m = EXPERT_WORK[k]
                    dst = bank(ring[k % len(ring)])
                    if k >= len(ring):
                        pe.wait_ge(s_done.sem, s_done.prior(turn, k - len(ring) + 1))
                    if what == "up":
                        if m == 0:
                            pe.wait_ge(s_w1[e % 2].sem, s_w1[e % 2].prior(turn, 16 * (e // 2 + 1)))
                        i = product(dst, [(w1[:, e % 2, n, m * P:(m + 1) * P], ht[:, n, :]) for n in range(NC)])
                    else:
                        if m == 0:
                            pe.wait_ge(s_w2[e % 2].sem, s_w2[e % 2].prior(turn, 16 * (e // 2 + 1)))
                            pe.wait_ge(s_done.sem, s_done.prior(turn, ITEM_AT["up", e, NH - 1] + 1))
                        for t in (2 * m, 2 * m + 1):
                            i = product(dst[:, (t % 2) * D:(t % 2 + 1) * D],
                                        [(eh[:, (NH * e + n) % EH_SLOTS, t * P:(t + 1) * P], w2[:, e % 2, n, :])
                                         for n in range(NH)])
                    i.then_inc(s_item.sem, 1)

            def sequence(turn, filled):
                def fill(place):
                    if filled:
                        expert_items(turn, *PLAN[place], EXPERT_BANKS)

                fill("load")
                gates = w("gates").rearrange("p (g c n) -> p g c n", g=2, c=NC)
                pe.wait_ge(s_x.sem, s_x.at(turn, 16 * 2))
                for g in range(2):
                    for c in range(NC):
                        i = pe.matmul(bank(2 * g + c), gates[:, g, c, :], xt[:, c, :], start=True, stop=True)
                i.then_inc(s_gates.sem, 1)
                fill("gates")
                fill("decay")
                pe.wait_ge(s_rg.sem, s_rg.at(turn, 1))
                for t in range(NT):
                    for c in range(NC):
                        i = pe.transpose(ps[:, 4 * BANK + t * D + c * P:4 * BANK + t * D + (c + 1) * P],
                                         xt[:, c, t * P:(t + 1) * P], identf)
                    i.then_inc(s_z.sem, 1)
                fill("rg")

                def to_feature_major(n, norm, src):
                    for t in range(NT):
                        pe.wait_ge(s_norm.sem, s_norm.at(turn, NT * norm + t + 1))
                        for c in range(NC):
                            i = pe.transpose(ps[:, (2 + c) * BANK + t * P:(2 + c) * BANK + (t + 1) * P],
                                             src[:, t, c * P:(c + 1) * P], identf)
                    i.then_inc(s_xtp.sem, 1)
                    pe.wait_ge(s_xt.sem, s_xt.at(turn, n + 1))

                def project(a, q_src, kv_src, nk=NC):
                    q, k, v, _ = attention_weights(a)
                    pe.wait_ge(s_wa[a % 2].sem, s_wa[a % 2].at(turn, 16 * (a // 2 + 1)))
                    for c in range(NC):
                        i = product(bank(c), [(q[:, n, c * P:(c + 1) * P], q_src[:, n, :]) for n in range(NC)])
                    i.then_inc(s_proj.sem, 1)
                    for c in range(NC):
                        i = product(bank(2 + c), [(k[:, n, c * P:(c + 1) * P], kv_src[:, n, :]) for n in range(nk)])
                    i.then_inc(s_proj.sem, 1)
                    for t in range(NT):
                        i = product(ps[:, 4 * BANK + t * D:4 * BANK + (t + 1) * D],
                                    [(kv_src[:, n, t * P:(t + 1) * P], v[:, n, :]) for n in range(nk)])
                    i.then_inc(s_proj.sem, 1)

                def attend(a, kind):
                    rows = ALL_ROWS - 3 if kind == ALIBI else ROWS
                    pe.wait_ge(s_op.sem, s_op.at(turn, 16 * 12 * (a + 1)))
                    pe.wait_ge(s_va.sem, s_va.at(turn, a + 1))
                    if kind == ALIBI:
                        pe.wait_ge(s_alibi.sem, s_alibi.at(turn, 32))
                    score, key = J * QUADS_BEFORE[kind], J * QUADS_BEFORE[kind]
                    for k, (what, g, s, pair) in enumerate(steps_of(kind)):
                        if k:
                            fill(("attend", a, k - 1))
                        if what == "S":
                            for h in range(J * g + 2 * pair, J * g + 2 * pair + 2):
                                if score >= 2:
                                    pe.wait_ge(s_max.sem, s_max.at(turn, score - 1))
                                dst = bank(score % 2)
                                if kind == WINDOW:
                                    for q in range(NT):
                                        t = slice(q * P, (q + 1) * P)
                                        i = pe.matmul(dst[:, t], qs[0:rows, h, t], ks[0:rows, h, t], start=True, stop=True)
                                elif kind == CAUSAL:
                                    t = slice(s * P, (s + 1) * P)
                                    pe.matmul(dst[:, 0:(s + 1) * P], qs[0:rows, h, t], ks[0:rows, h, 0:(s + 1) * P],
                                              start=True, stop=False)
                                    i = pe.matmul(dst[:, t], identb, tri_q, start=False, stop=True)
                                else:
                                    t = slice(s * P, (s + 1) * P)
                                    fix = corrections(h, s) if kind == ALIBI else []
                                    i = pe.matmul(dst, qs[0:rows, h, t], ks[0:rows, h, :], start=True, stop=not fix)
                                    for m, (d, col) in enumerate(fix):
                                        i = pe.matmul(dst[:, (s - d) * P:(s - d + 1) * P], clamp[:, col:col + P], identb,
                                                      start=False, stop=(m == len(fix) - 1))
                                i.then_inc(s_s.sem, 1)
                                score += 1
                        elif what == "M":
                            pe.wait_ge(s_mp.sem, s_mp.at(turn, G * a + g + 1))
                            if g > 0:
                                pe.wait_ge(s_mc.sem, s_mc.at(turn, G * a + g))
                            rows_out = bank(2).bitcast(BF16)
                            for q in range(NT):
                                i = pe.transpose(rows_out[0:3 * J, q * P:(q + 1) * P],
                                                 mp[:, g, q, :, :].rearrange("p i j -> p (i j)"), identb)
                            i.then_inc(s_mt.sem, 1)
                        elif what == "T":
                            pe.wait_ge(s_md.sem, s_md.at(turn, 16 * (G * a + g + 1)))
                            for n in (2 * pair, 2 * pair + 1):
                                h = J * g + n
                                if key >= 2:
                                    pe.wait_ge(s_exp.sem, s_exp.at(turn, key - 1))
                                dst = bank(4 + key % 2)
                                if kind == WINDOW:
                                    for q in range(NT):
                                        t = slice(q * P, (q + 1) * P)
                                        i = pe.matmul(dst[:, t], ks[0:rows + 3, h, t], qs[0:rows + 3, h, t], start=True, stop=True)
                                else:
                                    t = slice(s * P, (s + 1) * P)
                                    lo = s * P if kind == CAUSAL else 0
                                    d, np_ = CLAMPED.get(h, (NT, 0)) if kind == ALIBI else (NT, 0)
                                    fixed = [(d, p) for p in range(np_) if d + s < NT]
                                    if kind == MASKED:
                                        pe.matmul(dst, identb, negt[:, s, :], start=True, stop=False)
                                    i = pe.matmul(dst[:, lo:S], ks[0:rows + 3, h, t], qs[0:rows + 3, h, lo:S],
                                                  start=(kind != MASKED), stop=(kind != CAUSAL and not fixed))
                                    if kind == CAUSAL:
                                        i = pe.matmul(dst[:, t], identb, tri_k, start=False, stop=True)
                                    for m, (d, p) in enumerate(fixed):
                                        width = S - d * P
                                        col = CLAMP_AT[h] + p * width
                                        i = pe.matmul(dst[:, (d + s) * P:S], identb, clamp[:, col:col + S - (d + s) * P],
                                                      start=False, stop=(m == len(fixed) - 1))
                                i.then_inc(s_t.sem, 1)
                                key += 1
                        elif what == "V":
                            q_ = quad(kind, g, s)
                            pe.wait_ge(s_exp.sem, s_exp.at(turn, J * (q_ + 1)))
                            if kind == MASKED:
                                pe.wait_ge(s_pg.sem, s_pg.at(turn, NT * g + s + 1))
                                pe.wait_ge(s_pgp.sem, s_pgp.at(turn, NT * g + s + 1))
                            if s == 0 and (a or g):
                                pe.wait_ge(s_oc.sem, s_oc.at(turn, G * a + g))
                            slot = q_ % 2 if kind == MASKED else q_ % 3
                            first, last = s == 0, s == STEPS[kind] - 1
                            if kind == WINDOW:
                                for q in range(NT):
                                    t = slice(q * P, (q + 1) * P)
                                    for n in range(J):
                                        i = pe.matmul(bank(3)[32 * n:32 * n + 32, t], va[:, q, J * g + n, :],
                                                      prob[:, slot, n, t], start=True, stop=True, tile_position=(0, 32 * n))
                            elif kind == MASKED:
                                for n in range(J):
                                    pe.matmul(bank(3)[32 * n:32 * n + 32, :], ones[:, :], prob[:, slot, n, :],
                                              start=first, stop=False, tile_position=(0, 32 * n), skip_group_check=True)
                                for n in range(J):
                                    i = pe.matmul(bank(3)[32 * n:32 * n + 16, :], va[:, s, J * g + n, 0:HD],
                                                  prob[:, 2 + slot, n, :], start=False, stop=last,
                                                  tile_position=(0, 32 * n), skip_group_check=True)
                            else:
                                lo = s * P if kind == CAUSAL else 0
                                for n in range(J):
                                    i = pe.matmul(bank(3)[32 * n:32 * n + 32, lo:S], va[:, s, J * g + n, :],
                                                  prob[:, slot, n, lo:S], start=first, stop=last, tile_position=(0, 32 * n))
                            i.then_inc(s_pv.sem, 1)
                    fill(("attend", a, k))

                def project_out(a):
                    wo = attention_weights(a)[3]
                    for groups in (range(G - 1), (G - 1,)):
                        pe.wait_ge(s_o.sem, s_o.at(turn, G * a + groups[-1] + 1))
                        for t in range(NT):
                            for g in groups:
                                i = pe.matmul(ps[:, 4 * BANK + t * D:4 * BANK + (t + 1) * D], ot[:, g, t * P:(t + 1) * P],
                                              wo[:, g, :], start=(g == 0 and t % 2 == 0), stop=(g == G - 1), skip_group_check=True)
                            if g == G - 1:
                                i.then_inc(s_z.sem, 1)
                    fill(("norm", a))

                to_feature_major(0, 0, x)
                fill(("xt", 0))
                project(0, xt, ct)
                fill(("project", 0))
                attend(0, WINDOW)
                project_out(0)
                to_feature_major(1, 1, x)
                fc, proj = w3("fc", NC), w3("proj", NF)
                for m in range(NF):
                    if m >= 4:
                        pe.wait_ge(s_hc.sem, s_hc.at(turn, m - 3))
                    i = product(bank(m % 4), [(fc[:, n, m * P:(m + 1) * P], xt[:, n, :]) for n in range(NC)])
                    i.then_inc(s_h.sem, 1)
                pe.wait_ge(s_hc.sem, s_hc.at(turn, NF))
                for t in range(NT):
                    i = product(ps[:, 4 * BANK + t * D:4 * BANK + (t + 1) * D],
                                [(hid[:, m, t * P:(t + 1) * P], proj[:, m, :]) for m in range(NF)])
                    i.then_inc(s_z.sem, 1)
                fill("ffn_norm")
                to_feature_major(2, 2, x)
                fill(("xt", 1))
                project(1, xt, xt)
                fill(("project", 1))
                attend(1, ALIBI)
                project_out(1)
                to_feature_major(3, 3, x)
                fill(("xt", 2))
                project(2, xt, ct)
                fill(("project", 2))
                pe.wait_ge(s_negt.sem, s_negt.at(turn, 1))
                attend(2, MASKED)
                project_out(2)
                fill("rms")
                to_feature_major(4, 5, y)
                product(bank(0), [(w3("m_lat", NC)[:, n, :], xt[:, n, :]) for n in range(NC)]).then_inc(s_lat.sem, 1)
                pe.wait_ge(s_latc.sem, s_latc.at(turn, 1))
                lat = ct[:, 0:1, :]
                fill(("xt", 3))
                project(3, xt, lat, nk=1)
                fill(("project", 3))
                attend(3, CAUSAL)
                project_out(3)
                to_feature_major(5, 6, y)
                router = w3("router", NC)
                for t in range(NT):
                    i = product(bank(4)[:, t * NE:(t + 1) * NE], [(ht[:, n, t * P:(t + 1) * P], router[:, n, :]) for n in range(NC)])
                i.then_inc(s_router.sem, 1)

            sequence(0, False)
            with pe.Fori(1, NB) as turn:
                sequence(turn, True)
            expert_items(NB, 0, ITEMS, TAIL_BANKS)

        @block.scalar
        def _(act):
            step = Steps(s_act)
            act.wait_ge(s_sp.sem, 1)
            act.activation(small[:, 2:4], small[:, 0:2], ACT.Exp, scale=-1.0).then_inc(s_act.sem, step.one())
            act.wait_ge(s_act.sem, step.so_far())
            act.activation(small[:, 4:6], small[:, 2:4], ACT.Copy, bias=1.0).then_inc(s_act.sem, step.one())
            act.wait_ge(s_act.sem, step.so_far())
            act.activation(small[:, 6:8], small[:, 4:6], ACT.Ln).then_inc(s_act.sem, step.one())
            act.wait_ge(s_prep.sem, 1)

            def expert_items(turn, first, end, ring):
                for k in range(first, end):
                    what, e, m = EXPERT_WORK[k]
                    if what == "up":
                        act.wait_ge(s_item.sem, s_item.prior(turn, k + 1))
                        act.activation(eh[:, (NH * e + m) % EH_SLOTS, :], bank(ring[k % len(ring)]), ACT.Tanh, scale=0.5)\
                           .then_inc(s_th.sem, 1)

            def sequence(turn, filled):
                step.begin(turn)

                def fill(place):
                    if filled:
                        expert_items(turn, *PLAN[place], EXPERT_BANKS)

                fill("load")

                act.wait_ge(s_gates.sem, s_gates.at(turn, 1))
                act.activation(tg.rearrange("p g c s -> p (g c s)"), bank(0, 4), ACT.Tanh, scale=0.5).then_inc(s_act.sem, step.one())
                act.wait_ge(s_act.sem, step.so_far())
                for c in range(NC):
                    i = act.activation(dec[:, c, :], tg[:, 1, c, :], ACT.Exp, bias=small[:, 12 + c:13 + c],
                                       scale=small[:, 12 + c:13 + c])
                i.then_inc(s_decay.sem, 1)
                fill("gates")
                act.wait_ge(s_sq.sem, s_sq.at(turn, 1))
                for c in range(NC):
                    i = act.activation(stp[:, c, :], stp[:, c, :], ACT.Sqrt, bias=small[:, 14:15], scale=-0.25)
                i.then_inc(s_mult.sem, 1)
                fill("decay")
                fill("rg")

                def copy_xt(n, dst=xt):
                    act.wait_ge(s_xtp.sem, s_xtp.at(turn, n + 1))
                    act.activation(dst[:, :, :].rearrange("p c s -> p (c s)"), bank(2, 2), ACT.Copy).then_inc(s_xt.sem, 1)

                def squares():
                    for t in range(NT):
                        i = act.activation(big[:, 6144 + t * D:6144 + (t + 1) * D], x[:, t, :], ACT.Square, accum_out=ve[:, t:t + 1])
                    return i

                def split(a, qb, kb):
                    for o, (b, scale) in enumerate(((qb, QSCALE), (kb, 1.0))):
                        act.wait_ge(s_proj.sem, s_proj.at(turn, 3 * a + o + 1))
                        for c in range(NC):
                            bias = b[:, c:c + 1] if b is not None else 0.0
                            i = act.activation(parts[:, o, 0, c, :], bank(2 * o + c), ACT.Identity, bias=bias, scale=scale)
                        i.then_inc(s_p[0].sem, 1)
                        for c in range(NC):
                            bias = b[:, c:c + 1] if b is not None else 0.0
                            i = act.activation(qk[:, o, c, :], bank(2 * o + c), ACT.Identity, bias=bias, scale=scale)
                        i.then_inc(s_f.sem, 1)

                def attend(a, kind):
                    key = J * QUADS_BEFORE[kind]
                    for k, (what, g, s, pair) in enumerate(steps_of(kind)):
                        if k:
                            fill(("attend", a, k - 1))
                        if what == "M":
                            act.wait_ge(s_mt.sem, s_mt.at(turn, G * a + g + 1))
                            if a or g:
                                act.wait_ge(s_md.sem, s_md.at(turn, 16 * (G * a + g)))
                            act.activation(mrow[:, :], bank(2)[0:3 * J, :].bitcast(BF16)[:, 0:S], ACT.Copy)\
                               .then_inc(s_mc.sem, 1)
                        elif what == "C":
                            act.wait_ge(s_pv.sem, s_pv.at(turn, quad(kind, g, STEPS[kind] - 1) + 1))
                            act.activation(ot[:, g, :], bank(3), ACT.Copy).then_inc(s_oc.sem, 1)
                        elif what == "T":
                            q_ = quad(kind, g, s)
                            ring = 2 if kind == MASKED else 3
                            slot = q_ % ring
                            if pair == 0 and q_ - ring >= QUADS_BEFORE[kind]:
                                act.wait_ge(s_pv.sem, s_pv.at(turn, q_ - ring + 1))
                            lo = s * P if kind == CAUSAL else 0
                            for n in (2 * pair, 2 * pair + 1):
                                act.wait_ge(s_t.sem, s_t.at(turn, key + 1))
                                act.activation(prob[:, slot, n, lo:S], bank(4 + key % 2)[:, lo:S], ACT.Exp)\
                                   .then_inc(s_exp.sem, 1)
                                key += 1
                    fill(("attend", a, k))

                copy_xt(0)
                fill(("xt", 0))
                split(0, small[:, 8:10], w("l0_kb"))
                fill(("project", 0))
                attend(0, WINDOW)
                fill(("norm", 0))
                copy_xt(1)
                for m in range(NF):
                    act.wait_ge(s_h.sem, s_h.at(turn, m + 1))
                    act.activation(hid[:, m, :], bank(m % 4), ACT.Gelu, bias=w("fc_b")[:, m:m + 1]).then_inc(s_hc.sem, 1)
                fill("ffn_norm")
                copy_xt(2)
                fill(("xt", 1))
                split(1, small[:, 10:12], w("l1_kb"))
                fill(("project", 1))
                attend(1, ALIBI)
                fill(("norm", 1))
                copy_xt(3)
                fill(("xt", 2))
                split(2, small[:, 16:18], w("x_kb"))
                fill(("project", 2))
                attend(2, MASKED)
                fill(("norm", 2))
                act.wait_ge(s_norm.sem, s_norm.at(turn, 5 * NT))
                squares().then_inc(s_ss.sem, 1)
                fill("rms")
                copy_xt(4)
                act.wait_ge(s_lat.sem, s_lat.at(turn, 1))
                act.activation(ct[:, 0, :], bank(0), ACT.Copy).then_inc(s_latc.sem, 1)
                fill(("xt", 3))
                split(3, None, None)
                fill(("project", 3))
                attend(3, CAUSAL)
                fill(("norm", 3))
                act.wait_ge(s_sum.sem, s_sum.at(turn, 1))
                squares().then_inc(s_ss.sem, 1)
                copy_xt(5, ht)
                act.wait_ge(s_dif.sem, s_dif.at(turn, 1))
                act.activation(logit[:, 2, :], logit[:, 1, :], ACT.Exp).then_inc(s_rexp.sem, 1)
                step.end()

            sequence(0, False)
            with act.Fori(1, NB) as turn:
                sequence(turn, True)
            expert_items(NB, 0, ITEMS, TAIL_BANKS)

        @block.gpsimd
        def _(pool):
            pool.memset(va[:, :, :, :].rearrange("p t h n -> p (t h n)"), 1.0).then_inc(s_set.sem, 1)
            pool.memset(ones[:, 0:HD], 0.0).then_inc(s_set.sem, 1)
            pool.memset(ones[:, HD:32], 1.0).then_inc(s_set.sem, 1)
            pool.memset(small[:, 14:15], 0.25).then_inc(s_set.sem, 1)
            for n in range(2):
                pool.wait_ge(s_amax.sem, n + 1)
                pool.partition_all_reduce(small[:, 20 + n:21 + n], small[:, 18 + n:19 + n], P, RMAX)\
                    .then_inc(s_amaxall.sem, 1)
            pool.wait_ge(s_c.sem, 16 * 5)

            def final_inverse_root(turn):
                pool.wait_ge(s_fvar.sem, s_fvar.prior(turn, 1))
                pool.tensor_tensor(frstd[:, :], fve[:, :], half[:, :], ALU.pow).then_inc(s_frstd.sem, 1)

            def sequence(turn, filled):
                def inverse_root(n):
                    pool.wait_ge(s_var.sem, s_var.at(turn, n + 1))
                    pool.tensor_tensor(rstd[:, :], ve[:, :], half[:, :], ALU.pow).then_inc(s_rstd.sem, 1)

                def add_bias(n, name):
                    pool.wait_ge(s_xtp.sem, s_xtp.at(turn, n + 1))
                    pool.tensor_tensor(x[:, :, :], x[:, :, :], w(name).rearrange("p (a n) -> p a n", a=1)
                                       .to_broadcast([P, NT, D]), ALU.add).then_inc(s_bias.sem, 1)

                for n, name in enumerate(("l0_ob", "proj_b", "l1_ob", "x_ob")):
                    inverse_root(n)
                    add_bias(n, name)
                pool.wait_ge(s_side.sem, s_side.at(turn, 16 * 3))
                for g in range(G):
                    for s in range(NT):
                        q_ = quad(MASKED, g, s)
                        pool.wait_ge(s_exp.sem, s_exp.at(turn, J * (q_ + 1)))
                        if q_ - 2 >= QUADS_BEFORE[MASKED]:
                            pool.wait_ge(s_pv.sem, s_pv.at(turn, q_ - 1))
                        for n in range(2, J):
                            i = pool.tensor_tensor(prob[:, 2 + q_ % 2, n, :], prob[:, q_ % 2, n, :], grp[:, s, :], ALU.mult)
                        i.then_inc(s_pgp.sem, 1)
                inverse_root(4)
                inverse_root(5)
                if filled:
                    final_inverse_root(turn)
                inverse_root(6)

            sequence(0, False)
            with pool.Fori(1, NB) as turn:
                sequence(turn, True)
            final_inverse_root(NB)

        @block.vector
        def _(dve):
            step = Steps(s_vec)
            dve.wait_ge(s_w.sem, 16)
            dve.wait_ge(s_set.sem, 4)
            ap = w("a_param")
            dve.tensor_scalar(small[:, 0:2], ap, -1.0, None, ALU.mult).then_inc(s_vec.sem, step.one())
            dve.wait_ge(s_vec.sem, step.so_far())
            dve.tensor_tensor(small[:, 0:2], small[:, 0:2], ap, ALU.max).then_inc(s_sp.sem, 1)
            for name, at in (("l0_qb", 8), ("l1_qb", 10), ("x_qb", 16)):
                dve.tensor_scalar(small[:, at:at + 2], w(name), QSCALE, None, ALU.mult).then_inc(s_vec.sem, step.one())
            for n, name in enumerate(("fc", "proj")):
                dve.tensor_reduce(small[:, 18 + n:19 + n], w(name), AX.X, ALU.max, apply_absolute_value=True)\
                   .then_inc(s_amax.sem, 1)
            scale, inv = small[:, 20:22], small[:, 22:24]
            dve.wait_ge(s_amaxall.sem, 2)
            dve.tensor_scalar(scale, scale, 1.0 / QMAX, None, ALU.mult).then_inc(s_vec.sem, step.one())
            dve.wait_ge(s_vec.sem, step.so_far())
            dve.reciprocal(inv, scale).then_inc(s_vec.sem, step.one())
            dve.wait_ge(s_vec.sem, step.so_far())
            for n, name in enumerate(("fc", "proj")):
                wt = w(name)
                dve.tensor_scalar(qtmp, wt, inv[:, n:n + 1], ROUND, ALU.mult, ALU.add).then_inc(s_vec.sem, step.one())
                dve.wait_ge(s_vec.sem, step.so_far())
                dve.tensor_scalar(qtmp, qtmp, -ROUND, QMAX, ALU.add, ALU.min).then_inc(s_vec.sem, step.one())
                dve.wait_ge(s_vec.sem, step.so_far())
                dve.tensor_scalar(qtmp, qtmp, -QMAX - 1.0, scale[:, n:n + 1], ALU.max, ALU.mult).then_inc(s_vec.sem, step.one())
                dve.wait_ge(s_vec.sem, step.so_far())
                dve.tensor_tensor(qtmp, qtmp, wt, ALU.subtract).then_inc(s_vec.sem, step.one())
                dve.wait_ge(s_vec.sem, step.so_far())
                dve.tensor_tensor(wt, wt, qtmp, ALU.add).then_inc(s_vec.sem, step.one())
                dve.wait_ge(s_vec.sem, step.so_far())
                dve.wait_ge(s_lora.sem, n + 1)
                dve.scalar_tensor_tensor(wt, bank(4 * n, 4), LORA_SCALING, wt, ALU.mult, ALU.add).then_inc(s_vec.sem, step.one())
            dve.wait_ge(s_act.sem, ACT_ONCE)
            e_, u_, l_ = small[:, 2:4], small[:, 4:6], small[:, 6:8]
            dve.tensor_scalar(u_, u_, -1.0, 1e-30, ALU.add, ALU.add).then_inc(s_vec.sem, step.one())
            dve.tensor_scalar(l_, l_, 1e-30, None, ALU.add).then_inc(s_vec.sem, step.one())
            dve.wait_ge(s_vec.sem, step.so_far())
            dve.reciprocal(u_, u_).then_inc(s_vec.sem, step.one())
            dve.wait_ge(s_vec.sem, step.so_far())
            dve.tensor_tensor(l_, l_, u_, ALU.mult).then_inc(s_vec.sem, step.one())
            dve.wait_ge(s_vec.sem, step.so_far())
            dve.tensor_tensor(l_, l_, e_, ALU.mult).then_inc(s_vec.sem, step.one())
            dve.tensor_scalar(small[:, 12:14], ap, 0.0, None, ALU.max).then_inc(s_vec.sem, step.one())
            dve.wait_ge(s_vec.sem, step.so_far())
            dve.tensor_tensor(l_, l_, small[:, 12:14], ALU.add).then_inc(s_vec.sem, step.one())
            dve.wait_ge(s_vec.sem, step.so_far())
            dve.tensor_scalar(small[:, 12:14], l_, -4.0, None, ALU.mult).then_inc(s_prep.sem, 1)

            carried = []

            def carry():
                dve.memset(spare[:, len(carried):len(carried) + 1], 0.0)
                carried.append(0)

            def expert_item(turn, k, ring):
                what, e, m = EXPERT_WORK[k]
                src = bank(ring[k % len(ring)])
                if what == "up":
                    slot = eh[:, (NH * e + m) % EH_SLOTS, :]
                    dve.wait_ge(s_th.sem, s_th.prior(turn, NH * e + m + 1))
                    dve.scalar_tensor_tensor(slot, slot, 1.0, src, ALU.add, ALU.mult).then_inc(s_done.sem, 1)
                else:
                    dve.wait_ge(s_item.sem, s_item.prior(turn, k + 1))
                    if e:
                        dve.wait_ge(s_done.sem, s_done.prior(turn, ITEM_AT["down", e - 1, m] + 1))
                    for t in (2 * m, 2 * m + 1):
                        i = dve.scalar_tensor_tensor(ys[:, t, :], src[:, (t % 2) * D:(t % 2 + 1) * D], comb[:, t, e:e + 1],
                                                     ys[:, t, :], ALU.mult, ALU.add)
                    i.then_inc(s_done.sem, 1)

            def final_norm(turn):
                dve.wait_ge(s_done.sem, s_done.prior(turn, ITEMS))
                for t in range(NT):
                    dve.bn_stats(fstats[:, t, :], ys[:, t, :]).then_inc(s_fstat.sem, 1)
                dve.wait_ge(s_fstat.sem, s_fstat.prior(turn, NT))
                carry()
                for t in range(NT):
                    dve.bn_aggr(fmv[:, t, :], fstats[:, t, :]).then_inc(s_fmv.sem, 1)
                dve.wait_ge(s_fmv.sem, s_fmv.prior(turn, NT))
                dve.tensor_scalar(fve[:, :], fmv[:, :, 1], LN_EPS, None, ALU.add).then_inc(s_fvar.sem, 1)
                dve.wait_ge(s_frstd.sem, s_frstd.prior(turn, 1))
                for t in range(NT):
                    dve.tensor_scalar(ys[:, t, :], ys[:, t, :], fmv[:, t, 0:1], frstd[:, t:t + 1],
                                      ALU.subtract, ALU.mult).then_inc(s_final.sem, 1)

            def sequence(turn, filled):
                step.begin(turn)
                carried.clear()
                todo = list(range(ITEMS))

                def fill(place):
                    if not filled:
                        return
                    first, end = PLAN[place]
                    while todo and todo[0] < (end if place in CATCH_UP else first):
                        expert_item(turn, todo.pop(0), EXPERT_BANKS)
                    if place == FINAL:
                        final_norm(turn)

                fill("load")

                def z(t):
                    return ps[:, 4 * BANK + t * D:4 * BANK + (t + 1) * D]

                dve.wait_ge(s_decay.sem, s_decay.at(turn, 1))
                dve.tensor_tensor(stp, dec, dec, ALU.mult).then_inc(s_vec.sem, step.one())
                dve.wait_ge(s_vec.sem, step.so_far())
                dve.tensor_scalar(stp, stp, 1.0, None, ALU.min).then_inc(s_sq.sem, 1)
                dve.scalar_tensor_tensor(gx, tg[:, 0, :, :], 1.0, xt[:, :, :], ALU.add, ALU.mult).then_inc(s_vec.sem, step.one())
                dve.wait_ge(s_vec.sem, step.so_far())
                fill("gates")
                dve.wait_ge(s_mult.sem, s_mult.at(turn, 1))
                dve.tensor_tensor(gx, gx, stp, ALU.mult).then_inc(s_vec.sem, step.one())
                dve.wait_ge(s_vec.sem, step.so_far())
                for c in range(NC):
                    dve.tensor_tensor_scan(st[:, c, :], dec[:, c, :], gx[:, c, :], 0.0, ALU.mult, ALU.add).then_inc(s_vec.sem, step.one())
                dve.wait_ge(s_vec.sem, step.so_far())
                dve.tensor_tensor(xt[:, :, :], xt[:, :, :], st, ALU.add).then_inc(s_rg.sem, 1)
                fill("decay")

                def moments(n, src):
                    for t in range(NT):
                        dve.bn_stats(stats[:, t, :], src(t)).then_inc(s_vec.sem, step.one())
                    dve.wait_ge(s_vec.sem, step.so_far())
                    carry()
                    for t in range(NT):
                        dve.bn_aggr(mv[:, t, :], stats[:, t, :]).then_inc(s_vec.sem, step.one())
                    dve.wait_ge(s_vec.sem, step.so_far())
                    dve.tensor_scalar(ve[:, :], mv[:, :, 1], LN_EPS, None, ALU.add).then_inc(s_var.sem, 1)
                    dve.wait_ge(s_rstd.sem, s_rstd.at(turn, n + 1))
                    for t in range(NT):
                        dve.tensor_scalar(x[:, t, :], src(t), mv[:, t, 0:1], rstd[:, t:t + 1],
                                          ALU.subtract, ALU.mult).then_inc(s_norm.sem, 1)

                def layer_norm(n, zi):
                    for t in range(NT):
                        if t % 2 == 0:
                            dve.wait_ge(s_z.sem, s_z.at(turn, NT * zi + t + 2))
                        if zi and t == 0:
                            dve.wait_ge(s_bias.sem, s_bias.at(turn, zi))
                        if zi:
                            dve.tensor_tensor(y[:, t, :], z(t), x[:, t, :], ALU.add).then_inc(s_vec.sem, step.one())
                    if zi:
                        dve.wait_ge(s_vec.sem, step.so_far())
                    moments(n, (lambda t: y[:, t, :]) if zi else z)

                def rms_norm(n, k, gain):
                    dve.wait_ge(s_ss.sem, s_ss.at(turn, k + 1))
                    dve.tensor_scalar(ve[:, :], ve[:, :], 1.0 / D, RMS_EPS, ALU.mult, ALU.add).then_inc(s_var.sem, 1)
                    dve.wait_ge(s_rstd.sem, s_rstd.at(turn, n + 1))
                    for t in range(NT):
                        dve.scalar_tensor_tensor(y[:, t, :], x[:, t, :], rstd[:, t:t + 1], w(gain), ALU.mult, ALU.mult)\
                           .then_inc(s_norm.sem, 1)

                def split(a, vb):
                    for o in range(2):
                        f = qk[:, o, :, :]
                        dve.wait_ge(s_f.sem, s_f.at(turn, 2 * a + o + 1))
                        dve.tensor_tensor(f, f, parts[:, o, 0, :, :], ALU.subtract).then_inc(s_vec.sem, step.one())
                        dve.wait_ge(s_vec.sem, step.so_far())
                        dve.tensor_copy(parts[:, o, 1, :, :], f).then_inc(s_p[1].sem, 1)
                        dve.wait_ge(s_p[1].sem, s_p[1].at(turn, 2 * a + o + 1))
                        dve.tensor_tensor(parts[:, o, 2, :, :], f, parts[:, o, 1, :, :], ALU.subtract)\
                           .then_inc(s_p[2].sem, 1)
                    dve.wait_ge(s_proj.sem, s_proj.at(turn, 3 * a + 3))
                    vout = va[:, :, :, 0:HD]
                    vin = bank(4, 2).rearrange("p (t h d) -> p t h d", t=NT, h=H)
                    if vb is None:
                        i = dve.tensor_copy(vout, vin)
                    else:
                        for t in range(NT):
                            i = dve.tensor_tensor(vout[:, t, :, :], vin[:, t, :, :],
                                                  w(vb).rearrange("p (h d) -> p h d", h=H), ALU.add)
                    i.then_inc(s_va.sem, 1)

                def attend(a, kind):
                    score = J * QUADS_BEFORE[kind]
                    for k, (what, g, s, pair) in enumerate(steps_of(kind)):
                        if k:
                            fill(("attend", a, k - 1))
                        if what == "S":
                            for n in (2 * pair, 2 * pair + 1):
                                dve.wait_ge(s_s.sem, s_s.at(turn, score + 1))
                                if kind == MASKED:
                                    carry()
                                src = bank(score % 2)
                                if kind == WINDOW:
                                    i = dve.tensor_reduce(mx[:, g, :, n], src.rearrange("p (q k) -> p q k", q=NT), AX.X, ALU.max)
                                elif kind == MASKED:
                                    i = dve.tensor_tensor_reduce(out=src, in0=src, in1=neg[:, s, :], scale=1.0, scalar=LOWEST,
                                                                 op0=ALU.add, op1=ALU.max, accum_out=mx[:, g, s, n:n + 1])
                                else:
                                    width = (s + 1) * P if kind == CAUSAL else S
                                    i = dve.tensor_reduce(mx[:, g, s, n:n + 1], src[:, 0:width], AX.X, ALU.max)
                                i.then_inc(s_max.sem, 1)
                                score += 1
                        elif what == "P":
                            m, p3 = mx[:, g, :, :], mp[:, g, :, :, :]
                            dve.wait_ge(s_max.sem, s_max.at(turn, J * (QUADS_BEFORE[kind] + (g + 1) * STEPS[kind])))
                            dve.tensor_scalar(p3[:, :, 0, :], m, -1.0, None, ALU.mult).then_inc(s_vec.sem, step.one())
                            dve.wait_ge(s_vec.sem, step.so_far())
                            dve.scalar_tensor_tensor(mr[:, :, :], m, -1.0, p3[:, :, 0, :], ALU.mult, ALU.subtract).then_inc(s_vec.sem, step.one())
                            dve.wait_ge(s_vec.sem, step.so_far())
                            dve.tensor_copy(p3[:, :, 1, :], mr[:, :, :]).then_inc(s_vec.sem, step.one())
                            dve.wait_ge(s_vec.sem, step.so_far())
                            dve.tensor_tensor(p3[:, :, 2, :], mr[:, :, :], p3[:, :, 1, :], ALU.subtract).then_inc(s_mp.sem, 1)
                        elif what == "E":
                            q_ = quad(kind, g, s)
                            slot = q_ % 2
                            dve.wait_ge(s_exp.sem, s_exp.at(turn, J * q_ + 2))
                            if q_ - 2 >= QUADS_BEFORE[kind]:
                                dve.wait_ge(s_pv.sem, s_pv.at(turn, q_ - 1))
                            if NT * g + s == 0:
                                dve.wait_ge(s_side.sem, s_side.at(turn, 16 * 3))
                            for n in range(2):
                                i = dve.tensor_tensor(prob[:, 2 + slot, n, :], prob[:, slot, n, :], grp[:, s, :], ALU.mult)
                            i.then_inc(s_pg.sem, 1)
                        elif what == "R":
                            dve.wait_ge(s_sum_in.sem, s_sum_in.at(turn, 16 * (G * a + g + 1)))
                            dve.reciprocal(sums[:, :], sums[:, :]).then_inc(s_rc.sem, 1)
                        elif what == "N":
                            dve.wait_ge(s_rc_in.sem, s_rc_in.at(turn, 16 * (G * a + g + 1)))
                            carry()
                            dve.stream_shuffle(rinv, xt[:, 1, :], [HD] * 32).then_inc(s_vec.sem, step.one())
                            dve.wait_ge(s_vec.sem, step.so_far())
                            dve.tensor_tensor(ot[:, g, :], ot[:, g, :], rinv, ALU.mult).then_inc(s_o.sem, 1)
                    fill(("attend", a, k))

                layer_norm(0, 0)
                fill("rg")
                fill(("xt", 0))
                split(0, "l0_vb")
                fill(("project", 0))
                attend(0, WINDOW)
                layer_norm(1, 1)
                fill(("norm", 0))
                layer_norm(2, 2)
                fill("ffn_norm")
                fill(("xt", 1))
                split(1, "l1_vb")
                fill(("project", 1))
                attend(1, ALIBI)
                layer_norm(3, 3)
                fill(("norm", 1))
                dve.wait_ge(s_side.sem, s_side.at(turn, 16 * 2))
                dve.tensor_scalar(neg, neg.bitcast(I32), -NEG, NEG, ALU.mult, ALU.add).then_inc(s_vec.sem, step.one())
                dve.tensor_scalar(negt, grp.bitcast(I32), -NEG, NEG, ALU.mult, ALU.add).then_inc(s_negt.sem, 1)
                dve.wait_ge(s_vec.sem, step.so_far())
                fill(("xt", 2))
                split(2, "x_vb")
                fill(("project", 2))
                attend(2, MASKED)
                layer_norm(4, 4)
                fill(("norm", 2))
                rms_norm(5, 0, "g1")
                fill("rms")
                fill(("xt", 3))
                split(3, None)
                fill(("project", 3))
                attend(3, CAUSAL)
                if filled:
                    dve.wait_ge(s_out.sem, s_out.prior(turn, 16))
                for t in range(NT):
                    if t % 2 == 0:
                        dve.wait_ge(s_z.sem, s_z.at(turn, NT * 5 + t + 2))
                    dve.scalar_tensor_tensor(ys[:, t, :], x[:, t, :], 2.0, z(t), ALU.mult, ALU.add).then_inc(s_vec.sem, step.one())
                dve.wait_ge(s_vec.sem, step.so_far())
                for t in range(NT):
                    i = dve.tensor_tensor(x[:, t, :], z(t), x[:, t, :], ALU.add)
                i.then_inc(s_sum.sem, 1)
                rms_norm(6, 1, "g2")
                fill(("norm", 3))

                lg, ld, le, lr = (logit[:, i, :] for i in range(4))
                te = "p (t e) -> p t e"
                dve.wait_ge(s_router.sem, s_router.at(turn, 1))
                dve.tensor_copy(lg, bank(4)[:, 0:NT * NE]).then_inc(s_vec.sem, step.one())
                dve.wait_ge(s_vec.sem, step.so_far())
                dve.tensor_reduce(gat[:, 0, :], lg.rearrange(te, t=NT), AX.X, ALU.max).then_inc(s_vec.sem, step.one())
                l3 = lg.rearrange(te, t=NT)
                dve.wait_ge(s_vec.sem, step.so_far())
                for t in range(NT):
                    i = dve.tensor_scalar(ld[:, t * NE:(t + 1) * NE], lg[:, t * NE:(t + 1) * NE], gat[:, 0, t:t + 1], None,
                                          ALU.subtract)
                i.then_inc(s_dif.sem, 1)
                for t in range(NT):
                    other = l3[:, t:t + 1, :].to_broadcast([P, NE, NE])
                    own = l3[:, t, :].rearrange("p (e a) -> p e a", a=1).to_broadcast([P, NE, NE])
                    for i, op in enumerate((ALU.is_gt, ALU.is_equal)):
                        dve.tensor_tensor(rank[:, i, t * NE * NE:(t + 1) * NE * NE].rearrange("p (e f) -> p e f", e=NE),
                                                    other, own, op).then_inc(s_vec.sem, step.one())
                dve.wait_ge(s_vec.sem, step.so_far())
                for t in range(NT):
                    r1 = rank[:, 1, t * NE * NE:(t + 1) * NE * NE]
                    dve.tensor_tensor(r1, r1, w("before"), ALU.mult).then_inc(s_vec.sem, step.one())
                dve.wait_ge(s_vec.sem, step.so_far())
                dve.tensor_tensor(rank[:, 0, :], rank[:, 0, :], rank[:, 1, :], ALU.add).then_inc(s_vec.sem, step.one())
                dve.wait_ge(s_vec.sem, step.so_far())
                dve.tensor_reduce(lr, rank[:, 0, :].rearrange("p (a f) -> p a f", f=NE), AX.X, ALU.add).then_inc(s_vec.sem, step.one())
                dve.wait_ge(s_vec.sem, step.so_far())
                dve.wait_ge(s_rexp.sem, s_rexp.at(turn, 1))
                dve.scalar_tensor_tensor(lr, lr, 2.0, le, ALU.is_lt, ALU.mult).then_inc(s_vec.sem, step.one())
                dve.wait_ge(s_vec.sem, step.so_far())
                dve.tensor_reduce(gat[:, 1, :], lr.rearrange(te, t=NT), AX.X, ALU.add).then_inc(s_vec.sem, step.one())
                dve.wait_ge(s_vec.sem, step.so_far())
                dve.reciprocal(gat[:, 2, :], gat[:, 1, :]).then_inc(s_vec.sem, step.one())
                dve.wait_ge(s_vec.sem, step.so_far())
                for t in range(NT):
                    dve.tensor_scalar(comb[:, t, :], lr[:, t * NE:(t + 1) * NE], gat[:, 2, t:t + 1], 0.5, ALU.mult, ALU.mult).then_inc(s_vec.sem, step.one())
                dve.wait_ge(s_vec.sem, step.so_far())
                assert not filled or not todo
                step.end()

            sequence(0, False)
            with dve.Fori(1, NB) as turn:
                sequence(turn, True)
            carried.clear()
            for k in range(ITEMS):
                expert_item(NB, k, TAIL_BANKS)
            final_norm(NB)


def by_heads(np, v):
    a = v.reshape(v.shape[:-1] + (H // NC, NC, HD))
    return np.ascontiguousarray(np.moveaxis(a, (-3, -2, -1), (-1, -3, -2))).reshape(v.shape)


def lay_out(np, i):
    def rows(m):
        return np.ascontiguousarray(m.reshape(m.shape[0] // P, P, -1).transpose(1, 0, 2)).reshape(P, -1)

    def padded(m):
        out = np.zeros((G, J, 32, D), np.float32)
        out[:, :, 0:HD] = m.reshape(G, J, HD, D)
        return np.ascontiguousarray(out.reshape(G, P, D).transpose(1, 0, 2)).reshape(P, G * D)

    def column(v):
        return np.ascontiguousarray(v.reshape(-1, P).T)

    def everywhere(v):
        return np.broadcast_to(v.reshape(1, -1), (P, v.size))

    def diagonal(m):
        out = np.zeros((NC, P, P), np.float32)
        for h in range(8):
            c, at = h // 4, 32 * (h % 4)
            out[c, at:at + 32, at:at + 32] = m[h]
        return np.ascontiguousarray(out.transpose(1, 0, 2)).reshape(P, NC * P)

    w0, b0 = i["L0_xattn_in_proj_w"], i["L0_xattn_in_proj_b"]
    w1, b1 = i["L1_attn_in_proj_weight"], i["L1_attn_in_proj_bias"]
    p = {
        "gates": np.concatenate([diagonal(i["L0_attn_w_in"]), diagonal(i["L0_attn_w_a"])], 1),
        "a_param": column(i["L0_attn_a_param"]),
        "fc": rows(i["L0_ffn_W_fc"].T), "fc_b": column(i["L0_ffn_b_fc"]),
        "proj": rows(i["L0_ffn_W_proj"].T), "proj_b": everywhere(i["L0_ffn_b_proj"]),
        "m_lat": rows(i["L1_ffn_Wdkv"]), "g1": everywhere(i["L1_ffn_g1"]), "g2": everywhere(i["L1_ffn_g2"]),
        "router": rows(i["L1_ffn_gate_w"]), "ident": np.eye(P, dtype=np.float32),
        "before": everywhere(np.tril(np.ones((NE, NE), np.float32), -1)),
    }
    attention = []
    for name, wq, wk, wv, wo, bq, bk, bv, bo in (
        ("l0", w0[:D].T, w0[D:2 * D].T, w0[2 * D:].T, i["L0_xattn_out_w"].T,
         b0[:D], b0[D:2 * D], b0[2 * D:], i["L0_xattn_out_b"]),
        ("l1", w1[:D].T, w1[D:2 * D].T, w1[2 * D:].T, i["L1_attn_out_proj_weight"].T,
         b1[:D], b1[D:2 * D], b1[2 * D:], i["L1_attn_out_proj_bias"]),
        ("x", i["L1_xattn_wq_k"], i["L1_xattn_wk_k"], i["L1_xattn_wv_k"], i["L1_xattn_wo_k"],
         i["L1_xattn_wq_b"], i["L1_xattn_wk_b"], i["L1_xattn_wv_b"], i["L1_xattn_wo_b"]),
    ):
        attention.append([rows(by_heads(np, wq)), rows(by_heads(np, wk)), rows(wv), padded(wo)])
        p |= {name + "_qb": column(by_heads(np, bq)), name + "_kb": column(by_heads(np, bk)),
              name + "_vb": everywhere(bv), name + "_ob": everywhere(bo)}
    half = np.zeros((P, D), np.float32)
    attention.append([rows(by_heads(np, i["L1_ffn_Wq"])),
                      np.concatenate([by_heads(np, i["L1_ffn_Wuk"]), half], 1),
                      np.concatenate([i["L1_ffn_Wuv"], half], 1), padded(i["L1_ffn_Wo"])])
    pack = np.concatenate([p[name].reshape(P, n) for name, n in PACK], 1)

    def tiles(a):
        return np.ascontiguousarray(a.reshape(NB, a.shape[1] // P, P, a.shape[2]).transpose(0, 2, 1, 3))

    return {
        "pack": pack, "attention": np.stack([np.concatenate(m, 1) for m in attention]),
        "lora": np.concatenate([i["L0_ffn_A_fc"], i["L0_ffn_B_fc"].T, i["L0_ffn_A_proj"], i["L0_ffn_B_proj"].T], 1),
        "x": tiles(i["x"].transpose(0, 2, 1)), "c": tiles(i["ctx_1024"].transpose(0, 2, 1)),
        "group": tiles(i["fside_BxSxS2_0"].transpose(0, 2, 1)),
        "mask": tiles(i["mask_BxSxS2_ik1"]), "mask_t": tiles(i["mask_BxSxS2_ik1"].transpose(0, 2, 1)),
        "w1": np.ascontiguousarray(i["L1_ffn_w1"].reshape(NE, NC, P, EH).transpose(0, 2, 1, 3)),
        "w2": np.ascontiguousarray(i["L1_ffn_w2"].reshape(NE, NH, P, D).transpose(0, 2, 1, 3)),
    } | constants(np)


def constants(np):
    bf16 = mybir.dt.np(BF16)

    def in_parts(v):
        out = []
        for _ in range(3):
            out.append(v.astype(bf16))
            v = (v - out[-1].astype(np.float32)).astype(np.float32)
        return out

    slope = np.float32([2.0 ** -0.5 * (2.0 ** -0.5) ** n for n in range(H)])
    pos = np.arange(S, dtype=np.float32)
    line = (slope[:, None] * pos[None, :]).astype(np.float32)
    one = np.ones((3, H, S), bf16)
    k_rows = np.concatenate([one, np.stack(in_parts(-line)), one])
    clamp = np.zeros((P, CLAMP_COLS), bf16)
    for h, (d, n) in CLAMPED.items():
        rel = np.arange(d * P, S, dtype=np.float32)[None, :] - np.arange(P, dtype=np.float32)[:, None]
        fix = np.minimum(8.0 - rel * slope[h], 0.0).astype(np.float32)
        for m, part in enumerate(in_parts(fix)[:n]):
            clamp[:, CLAMP_AT[h] + m * (S - d * P):CLAMP_AT[h] + (m + 1) * (S - d * P)] = part
    q, k = np.arange(P)[:, None], np.arange(P)[None, :]
    const = np.concatenate([np.eye(P), np.where(k > q, NEG, 0.0), np.where(q > k, NEG, 0.0)], 1).astype(bf16)
    return {"k_rows": k_rows, "one_rows": one, "q_rows": np.stack(in_parts(line)), "clamp": clamp, "const": const,
            "half": np.full((P, NT), -0.5, np.float32)}


def kernel(**inputs):
    import numpy as np
    import concourse.bacc as bacc
    from concourse.bass_utils import run_bass_kernel_spmd

    arrays = lay_out(np, {k: np.asarray(v) for k, v in inputs.items()})
    nc = bacc.Bacc("TRN2", target_bir_lowering=False, num_devices=1)
    ins = {name: nc.dram_tensor(f"in_{name}", a.shape, mybir.dt.from_np(a.dtype), kind="ExternalInput").ap()
           for name, a in arrays.items()}
    out = nc.dram_tensor("out", (NB, P, NT, D), F32, kind="ExternalOutput").ap()
    decoder(nc, ins, out)
    result = run_bass_kernel_spmd(nc, [{f"in_{name}": a for name, a in arrays.items()}], core_ids=[0])
    tokens = result.results[0]["out"]
    return np.ascontiguousarray(tokens.transpose(0, 2, 1, 3)).reshape(NB, S, D)
```

```python
import concourse.bass as bass
from concourse import mybir
from contextlib import ExitStack

F32 = mybir.dt.float32
BF16 = mybir.dt.bfloat16
F16 = mybir.dt.float16
I32 = mybir.dt.int32
ALU = mybir.AluOpType
ACT = mybir.ActivationFunctionType
AX = mybir.AxisListType

P = 128
NB, S, D = 4, 512, 256
H, HD = 16, 16
NT = S // P
NC = D // P
G, J = 4, 4
F = 1024
NF = F // P
R = 16
LAT = 128
NE, EH = 8, 512
NH = EH // P
BANK = 512
QSCALE = 0.25
LN_EPS, RMS_EPS = 1e-5, 1e-6
LORA_SCALING = 2.0
QMAX = 127.0
ROUND = 1.5 * 2.0 ** 23
NEG = -998244352.0
LOWEST = -3.0e38
RMAX = bass.bass_isa.ReduceOp.max

Q_PARTS = (0, 0, 1, 1, 0, 2)
K_PARTS = (0, 1, 0, 1, 2, 0)
ROWS = len(Q_PARTS) * HD
Q_SLOPE = ROWS
K_SLOPE = ROWS + 3
ALL_ROWS = ROWS + 9

CLAMPED = {h: (0 if h < 7 else 1 if h < 9 else 2, 2 if h % 2 == 0 else 1) for h in range(11)}
CLAMP_SCALE = 128.0
CLAMP_AT = {}
_at = 0
for _h, (_d, _n) in CLAMPED.items():
    CLAMP_AT[_h] = _at
    _at += _n * (S - _d * P)
CLAMP_COLS = _at

PACK = [
    ("gates", 2 * NC * P), ("a_param", NC), ("l0_qb", NC), ("l0_kb", NC), ("l0_vb", D), ("l0_ob", D),
    ("fc_b", NF), ("proj_b", D),
    ("l1_qb", NC), ("l1_kb", NC), ("l1_vb", D), ("l1_ob", D),
    ("x_qb", NC), ("x_kb", NC), ("x_vb", D), ("x_ob", D), ("m_lat", NC * LAT),
    ("g1", D), ("g2", D), ("router", NC * NE), ("ident", P), ("before", NE * NE),
    ("fc", NC * F), ("proj", NF * D),
]
PACK_AT, _at = {}, 0
for _name, _n in PACK:
    PACK_AT[_name] = (_at, _n)
    _at += _n
PACK_COLS = _at
FFN_AT = PACK_AT["fc"][0]
QKVO = 3 * NC * D + G * D
CONST = {"ident": 0, "tri_q": P, "tri_k": 2 * P}
CONST["clamp_ident"] = 3 * P
CONST_COLS = 4 * P

WINDOW, ALIBI, MASKED, CAUSAL = range(4)
STEPS = {WINDOW: 1, ALIBI: NT, MASKED: NT, CAUSAL: NT}
KINDS = (WINDOW, ALIBI, MASKED, CAUSAL)
QUADS_BEFORE = {WINDOW: 0, ALIBI: G, MASKED: G * 5, CAUSAL: G * 9}
QUADS = G * 13


def corrections(h, q):
    first, n = CLAMPED.get(h, (NT, 0))
    return [(d, CLAMP_AT[h] + m * (S - first * P) + (d - first) * P) for d in range(first, q + 1) for m in range(n)]


def steps_of(kind):
    n, out = STEPS[kind], []
    ahead = [("S", g, s, head) for g in range(G) for s in range(n) for head in range(J)]
    waiting = []

    def scores(count):
        for _ in range(min(count, len(ahead))):
            out.append(ahead.pop(0))
            _, g, s, head = out[-1]
            tick()
            if (s, head) == (n - 1, J - 1):
                out.append(("P", g, 0, 0))
                waiting.append([M_AFTER[kind], ("M", g, 0, 0)])

    def tick():
        for entry in waiting:
            entry[0] -= 1
        take(lambda count, entry: count <= 0)

    def take(due):
        for late in [w for w in waiting if due(*w)]:
            waiting.remove(late)
            out.append(late[1])

    def way_out(g):
        out.append(("C", g, 0, 0))
        waiting.append([R_AFTER[kind], ("R", g, 0, 0)])
        waiting.append([N_AFTER[kind], ("N", g, 0, 0)])

    scores(J * n + LEAD[kind])
    for g in range(G):
        for s in range(n):
            for head in range(J):
                take(lambda count, entry: entry[:2] == ("M", g))
                out.append(("T", g, s, head))
                tick()
                scores(1)
            if s > 0:
                out.append(("V", g, s - 1, 0))
            elif g > 0:
                take(lambda count, entry: entry[1] < g - 1)
                out.append(("V", g - 1, n - 1, 0))
                way_out(g - 1)
            if kind == MASKED:
                out.append(("E", g, s, 0))
    take(lambda count, entry: True)
    out.append(("V", G - 1, n - 1, 0))
    way_out(G - 1)
    take(lambda count, entry: True)
    return out


LEAD = {WINDOW: 4, ALIBI: 9, MASKED: 8, CAUSAL: 8}
R_AFTER = {WINDOW: 4, ALIBI: 8, MASKED: 6, CAUSAL: 8}
N_AFTER = {WINDOW: 8, ALIBI: 16, MASKED: 12, CAUSAL: 16}
M_AFTER = {WINDOW: 2, ALIBI: 4, MASKED: 4, CAUSAL: 4}


def score_bank(kind, i):
    return (0, 1, 4, 5)[i % 4] if i < J * STEPS[kind] + LEAD[kind] else i % 2


def score_bank_free(kind, i):
    return i - 3 if i < J * STEPS[kind] + LEAD[kind] else i - 1


def key_bank(kind, i):
    return (4, 5, 0, 1)[i % 4] if i >= J * STEPS[kind] * (G - 1) else 4 + i % 2


def key_bank_free(kind, i):
    alone = i - J * STEPS[kind] * (G - 1)
    return i - 1 if alone < 2 else i - 3 if alone >= 4 else 0


def scores_before_keys(kind):
    return 1 + max(i for i in range(J * STEPS[kind] + LEAD[kind]) if i % 4 >= 2)


EXPERT_WORK = [("up", 0, 0)]
for _e in range(NE):
    EXPERT_WORK += [("up", _e, m) for m in range(1, NH)]
    EXPERT_WORK += [("up", _e + 1, 0)] if _e + 1 < NE else []
    EXPERT_WORK += [("down", _e, m) for m in range(NT // 2)]
ITEMS = len(EXPERT_WORK)
ITEM_AT = {w: k for k, w in enumerate(EXPERT_WORK)}
EH_SLOTS = NH + 1
EXPERT_BANKS = (6, 7)
TAIL_BANKS = (6, 7, 1, 2)


def fill_plan():
    plan, at = {}, 0

    def put(place, n):
        nonlocal at
        n = min(n, ITEMS - at)
        plan[place] = (at, at + n)
        at += n

    put("gates", FILL["gates"])
    put("decay", FILL["decay"])
    put("rg", FILL["norm"])
    for a, kind in enumerate(KINDS):
        put(("xt", a), FILL["xt"])
        put(("project", a), FILL["project"])
        steps = steps_of(kind)
        for k, (what, g, s, head) in enumerate(steps):
            put(("attend", a, k), 1 if (what, g, s, head) in FILL["after"][kind] or (what, g) == ("N", G - 1) else 0)
        put(("norm", a), FILL["norm"])
        if a == 0:
            put("ffn", 0)
            put("ffn_norm", FILL["norm"])
        if a == 2:
            put("squares", 0)
            put("rms", FILL["norm"])
    assert at == ITEMS, at
    steps = steps_of(CAUSAL)
    final = ("attend", 3, steps.index(("T", G - 1, 0, 1)))
    assert plan[final][1] == ITEMS, final
    return plan, final


_FIRST = (("S", 0, 1, J - 1), ("S", 0, 3, J - 1), ("S", 1, 1, J - 1))
_LAST = tuple(("T", G - 1, s, 0) for s in range(1, NT))
FILL = {"gates": 1, "decay": 1, "norm": 2, "xt": 0, "project": 3,
        "after": {WINDOW: (("S", 0, 0, J - 1), ("S", 1, 0, J - 1), ("V", 1, 0, 0), ("V", 2, 0, 0)),
                  ALIBI: _FIRST + _LAST, MASKED: _FIRST + _LAST, CAUSAL: _FIRST + _LAST}}
PLAN, FINAL = fill_plan()
CATCH_UP = {FINAL, "ffn", "squares"} | {("attend", a, len(steps_of(kind)) - 1) for a, kind in enumerate(KINDS)} | {(what, a) for what in ("xt", "project") for a in range(len(KINDS))}


class Events:

    def __init__(self, ctx, nc, name, per_turn, once=0):
        self.sem = ctx.enter_context(nc.semaphore(name))
        self.per_turn, self.once, self.name = per_turn, once, name

    def at(self, turn, count):
        return turn * self.per_turn + (self.once + count)

    def prior(self, turn, count):
        return turn * self.per_turn + (self.once + count - self.per_turn)


class Steps:

    def __init__(self, counted, late=False):
        self.counted, self.late, self.count, self.turn = counted, late, 0, None

    def one(self):
        self.count += 1
        return 1

    def so_far(self):
        if self.turn is None:
            return self.count
        return (self.counted.prior if self.late else self.counted.at)(self.turn, self.count)

    def begin(self, turn):
        if self.turn is None:
            assert self.count == self.counted.once, (self.counted.name, "once", self.count)
        self.count, self.turn = 0, turn

    def end(self):
        assert self.count == self.counted.per_turn, (self.counted.name, "per turn", self.count)


VECTOR_ONCE, VECTOR_TURN = 11, 134
ACT_ONCE, ACT_TURN = 3, 1
TAIL_TURN = 27


def decoder(nc, ins, out):
    ctx = ExitStack()
    with ctx:
        def sb(name, shape, dt=F32):
            return ctx.enter_context(nc.sbuf_tensor(name, shape, dt))

        def events(name, per_turn, once=0):
            return Events(ctx, nc, name, per_turn, once)

        pack = sb("pack", [P, PACK_COLS])
        const = sb("const", [P, CONST_COLS], BF16)
        x = sb("x", [P, NT, D])
        y = sb("y", [P, NT, D])
        xt = sb("xt", [P, NC, S])
        ct = sb("ct", [P, NC, S])
        qs = sb("qs", [P, H, S], BF16)
        ks = sb("ks", [P, H, S], BF16)
        va = sb("va", [P, NT, H, 32])
        sums = sb("sums", [P, J * S // P])
        ones = sb("ones", [P, 32])
        ot = sb("ot", [P, G, S])
        big = sb("big", [P, 4 * J * S])
        side = sb("side", [P, max(CLAMP_COLS // 2, 2 * NT * S + NT * S // 2)])
        wa = sb("wa", [P, 2, QKVO])
        w1 = sb("w1", [P, 2, NC, EH])
        w2 = sb("w2", [P, 2, NH, D])
        ht = sb("ht", [P, NC, S])
        eh = sb("eh", [P, EH_SLOTS, S])
        ys = sb("ys", [P, NT, D])
        mx = sb("mx", [P, G, NT, J])
        mr = sb("mr", [P, NT, J])
        mp = sb("mp", [P, G, NT, 3, J], BF16)
        mrow = sb("mrow", [3 * J, S], BF16)
        stats = sb("stats", [P, NT, 6])
        mv = sb("mv", [P, NT, 2])
        ve = sb("ve", [P, NT])
        rstd = sb("rstd", [P, NT])
        fstats = sb("fstats", [P, NT, 6])
        fmv = sb("fmv", [P, NT, 2])
        fve = sb("fve", [P, NT])
        frstd = sb("frstd", [P, NT])
        half = sb("half", [P, NT])
        small = sb("small", [P, 24])
        logit = sb("logit", [P, 4, NT * NE])
        spare = sb("spare", [P, 88])
        comb = sb("comb", [P, NT, NE])
        gat = sb("gat", [P, 3, NT])
        ps = ctx.enter_context(nc.psum_tensor("ps", [P, 8 * BANK], F32))

        def bank(b, n=1):
            return ps[:, b * BANK:(b + n) * BANK]

        def attention_weights(a):
            at, out = wa[:, a % 2, :], []
            for n, c in enumerate((NC, NC, NC, G)):
                out.append(at[:, n * NC * D:(n * NC + c) * D].rearrange("p (c n) -> p c n", c=c))
            return out

        def w(name):
            at, n = PACK_AT[name]
            return pack[:, at:at + n]

        def w3(name, a):
            return w(name).rearrange("p (a n) -> p a n", a=a)

        def part(at, *dims):
            n = 1
            for d in dims:
                n *= d
            v = big[:, at:at + n]
            if len(dims) == 2:
                return v.rearrange("p (a b) -> p a b", a=dims[0])
            return v.rearrange("p (a b c) -> p a b c", a=dims[0], b=dims[1])

        tg = part(0, 2, NC, S)
        dec = part(2048, NC, S)
        stp = part(3072, NC, S)
        gx = part(4096, NC, S)
        st = part(5120, NC, S)
        qk = part(0, 2, NC, S)
        parts = big[:, 2048:2048 + 3072].bitcast(BF16).rearrange(
            "p (o i c s) -> p o i c s", o=2, i=3, c=NC)
        hid = part(0, NF, S)
        prob = part(0, 4, J, S)
        rank = big[:, 7168:7168 + 2 * NT * NE * NE].rearrange("p (a n) -> p a n", a=2)
        qtmp = eh[:, :, :].rearrange("p m s -> p (m s)")[:, 0:NC * F]
        lora = qs[0:R, :, :].rearrange("p h s -> p (h s)").bitcast(F32)[:, 0:2 * (D + F)]
        lora_product = (w1[:, :, :, :].rearrange("p a b c -> p (a b c)"), w2[:, :, :, :].rearrange("p a b c -> p (a b c)"))
        clamp = side[:, 0:CLAMP_COLS // 2].bitcast(F16)
        grp = side[:, 0:NT * S].rearrange("p (a s) -> p a s", a=NT)
        neg = side[:, NT * S:2 * NT * S].rearrange("p (a s) -> p a s", a=NT)
        negt = side[:, 2 * NT * S:2 * NT * S + NT * S // 2].bitcast(BF16).rearrange(
            "p (a s) -> p a s", a=NT)
        rinv = xt[:, 0, :]
        sum_rows = ot[HD:P:32, :, :]
        recip_rows = xt[HD:P:32, 1, :]
        identf = w("ident")
        identb = const[:, CONST["ident"]:CONST["ident"] + P]
        clamp_ident = const[:, CONST["clamp_ident"]:CONST["clamp_ident"] + P].bitcast(F16)
        tri_q = const[:, CONST["tri_q"]:CONST["tri_q"] + P]
        tri_k = const[:, CONST["tri_k"]:CONST["tri_k"] + P]

        s_w = events("weights_loaded", 0, 16)
        s_wf = events("ffn_weights_loaded", 0, 16)
        s_l = events("lora_loaded", 0, 16)
        s_c = events("constants_loaded", 0, 16 * 4)
        s_set = events("buffers_set", 0, 4)
        s_amax = events("weight_max", 0, 2)
        s_amaxall = events("weight_max_everywhere", 0, 2)
        s_lora = events("lora_product", 0, 2)
        s_loraout = events("lora_copied", 0, 2)
        s_quant = events("quantisation_steps", 0, 12)
        s_ffn = events("ffn_weights_ready", 0, 2)
        s_sp = events("softplus_exp", 0, 1)
        s_prep = events("softplus_ready", 0, 1)
        s_x = events("inputs_loaded", 16 * 2)
        s_alibi = events("alibi_loaded", 16 * 2)
        s_side = events("group_and_mask_loaded", 16 * 3)
        s_vec = events("vector_steps", VECTOR_TURN, VECTOR_ONCE)
        s_tail = events("vector_steps_of_tail", TAIL_TURN)
        s_act = events("scalar_steps", ACT_TURN, ACT_ONCE)
        s_gates = events("gates_ready", 1)
        s_decay = events("decay_ready", 1)
        s_sq = events("decay_squared", 1)
        s_mult = events("step_ready", 1)
        s_rg = events("recurrence_done", 1)
        s_z = events("output_tile_ready", 6 * NT)
        s_var = events("variance_ready", 7)
        s_rstd = events("rstd_ready", 7)
        s_norm = events("normalised_tile", 7 * NT)
        s_final = events("result_normalised", NT)
        s_fstat = events("result_statistics", NT)
        s_fmv = events("result_moments", NT)
        s_fvar = events("result_variance_ready", 1)
        s_frstd = events("result_rstd_ready", 1)
        s_xtp = events("transposed", 6)
        s_xt = events("feature_major_ready", 6)
        s_bias = events("residual_plus_bias", 4)
        s_proj = events("projection_ready", 12)
        s_lat = events("latent_ready", 1)
        s_latc = events("latent_copied", 1)
        s_f = events("q_or_k_float", 2 * 4)
        s_p = [events(f"part_{i}_ready", 2 * 4) for i in range(3)]
        s_negt = events("mask_turned", 1)
        s_sum = events("latent_attention_added", 1)
        s_op = events("operands_loaded", 16 * 12 * 4)
        s_va = events("values_ready", 4)
        s_s = events("scores_ready", J * QUADS)
        s_max = events("maximum_taken", J * QUADS)
        s_mp = events("maximum_split", 4 * G)
        s_mt = events("maximum_transposed", 4 * G)
        s_mc = events("maximum_copied", 4 * G)
        s_md = events("maximum_in_operand", 16 * 4 * G)
        s_t = events("key_major_ready", J * QUADS)
        s_exp = events("exp_done", J * QUADS)
        s_pg = events("grouped_by_vector", G * NT)
        s_pgp = events("grouped_by_gpsimd", G * NT)
        s_pv = events("values_summed", QUADS)
        s_oc = events("heads_copied", 4 * G)
        s_sum_in = events("sums_spread", 16 * 4 * G)
        s_rc = events("reciprocals_ready", 4 * G)
        s_rc_in = events("reciprocals_in_rows", 16 * 4 * G)
        s_o = events("heads_normalised", 4 * G)
        s_h = events("hidden_ready", NF)
        s_hc = events("hidden_done", NF)
        s_item = events("expert_product", ITEMS)
        s_th = events("expert_tanh", NE * NH)
        s_done = events("expert_item_done", ITEMS)
        s_router = events("router_ready", 1)
        s_dif = events("router_shifted", 1)
        s_rexp = events("router_exp", 1)
        s_w1 = [events(f"expert_up_{i}_loaded", 16 * NE // 2) for i in range(2)]
        s_w2 = [events(f"expert_down_{i}_loaded", 16 * NE // 2) for i in range(2)]
        s_wa = [events(f"attention_weights_{i}_loaded", 16 * 2) for i in range(2)]
        s_ss = events("squares_summed", 2)
        s_out = events("stored", 16)

        def quad(kind, g, s):
            return QUADS_BEFORE[kind] + g * STEPS[kind] + s

        block = ctx.enter_context(nc.Block())

        @block.sync
        def _(sp):
            sp.dma_start(lora, ins["lora"]).then_inc(s_l.sem, 16)
            sp.dma_start(pack[:, 0:FFN_AT], ins["pack"][:, 0:FFN_AT]).then_inc(s_w.sem, 16)
            sp.dma_start(const[:, :], ins["const"]).then_inc(s_c.sem, 16)
            sp.dma_start(ks[ROWS:ALL_ROWS, :, :], ins["k_rows"]).then_inc(s_c.sem, 16)
            sp.dma_start(qs[K_SLOPE:K_SLOPE + 3, :, :], ins["one_rows"]).then_inc(s_c.sem, 16)
            sp.dma_start(half[:, :], ins["half"]).then_inc(s_c.sem, 16)

            def weights_up(e):
                sp.dma_start(w1[:, e % 2, :, :], ins["w1"][e]).then_inc(s_w1[e % 2].sem, 16)

            def weights_down(e):
                sp.dma_start(w2[:, e % 2, :, :], ins["w2"][e]).then_inc(s_w2[e % 2].sem, 16)

            def first_experts():
                for e in range(2):
                    weights_up(e)
                    weights_down(e)

            def expert_items(turn, first, end):
                for k in range(first, end):
                    what, e, m = EXPERT_WORK[k]
                    if what == "up" and m == NH - 1 and e + 2 < NE:
                        sp.wait_ge(s_item.sem, s_item.prior(turn, k + 1))
                        weights_up(e + 2)
                    if what == "down" and m == NT // 2 - 1 and e + 2 < NE:
                        sp.wait_ge(s_item.sem, s_item.prior(turn, k + 1))
                        weights_down(e + 2)

            def store(turn, place):
                sp.wait_ge(s_final.sem, s_final.prior(turn, NT))
                sp.dma_start(place, ys[:, :, :]).then_inc(s_out.sem, 16)

            def sequence(turn, filled):
                def one(name):
                    return ins[name][bass.ds(turn, 1)].rearrange("a p n m -> (a p) n m")

                def fill(place):
                    if filled:
                        expert_items(turn, *PLAN[place])
                        if place == FINAL[:2] + (FINAL[2] + 8,):
                            store(turn, o_out)

                def weights(a):
                    sp.dma_start(wa[:, a % 2, :], ins["attention"][a]).then_inc(s_wa[a % 2].sem, 16)

                x_in, c_in = one("x"), one("c")
                if filled:
                    o_out = out[bass.ds(turn - 1, 1)].rearrange("a p n m -> (a p) n m")
                g_in, m_in, mt_in = one("group"), one("mask"), one("mask_t")
                if filled:
                    sp.wait_ge(s_o.sem, s_o.prior(turn, 4 * G))
                sp.dma_start(xt[:, :, :], x_in).then_inc(s_x.sem, 16)
                sp.dma_start(ct[:, :, :], c_in).then_inc(s_x.sem, 16)
                if filled:
                    first_experts()
                weights(0)
                if not filled:
                    sp.dma_start(pack[:, FFN_AT:], ins["pack"][:, FFN_AT:]).then_inc(s_wf.sem, 16)
                sp.dma_start(clamp, ins["clamp"]).then_inc(s_alibi.sem, 16)
                if filled:
                    sp.wait_ge(s_z.sem, s_z.prior(turn, 6 * NT))
                weights(1)
                fill("gates")
                fill("decay")
                fill("rg")
                for a, kind in enumerate(KINDS):
                    if kind == ALIBI:
                        sp.wait_ge(s_pv.sem, s_pv.at(turn, QUADS_BEFORE[ALIBI]))
                        sp.dma_start(qs[Q_SLOPE:Q_SLOPE + 3, :, :], ins["q_rows"]).then_inc(s_alibi.sem, 16)
                    if kind == MASKED:
                        sp.wait_ge(s_pv.sem, s_pv.at(turn, QUADS_BEFORE[MASKED]))
                        sp.dma_start(neg.bitcast(I32), m_in).then_inc(s_side.sem, 16)
                        sp.dma_start(grp.bitcast(I32), mt_in).then_inc(s_side.sem, 16)
                    for o, dst, slots in ((0, qs, Q_PARTS), (1, ks, K_PARTS)):
                        for i in range(3):
                            sp.wait_ge(s_p[i].sem, s_p[i].at(turn, 2 * a + o + 1))
                            for slot in range(6):
                                if slots[slot] == i:
                                    sp.dma_start(dst[slot * HD:(slot + 1) * HD, :, :], parts[:, o, i, :, :])\
                                      .then_inc(s_op.sem, 16)
                    if kind == MASKED:
                        sp.wait_ge(s_negt.sem, s_negt.at(turn, 1))
                        sp.dma_start(grp, g_in).then_inc(s_side.sem, 16)
                    at = Q_SLOPE + 6 if kind == ALIBI else ROWS
                    fill(("xt", a))
                    fill(("project", a))
                    for k, (what, g, s, half_) in enumerate(steps_of(kind)):
                        if what == "M":
                            sp.wait_ge(s_mc.sem, s_mc.at(turn, G * a + g + 1))
                            sp.dma_start(qs[at:at + 3, J * g:J * g + J, :], mrow[:, :]).then_inc(s_md.sem, 16)
                        if what == "C":
                            sp.wait_ge(s_oc.sem, s_oc.at(turn, G * a + g + 1))
                            sp.dma_start(sums[:, :], sum_rows[:, g, :]).then_inc(s_sum_in.sem, 16)
                        if (what, g) == ("R", 0) and kind in (ALIBI, MASKED):
                            sp.wait_ge(s_z.sem, s_z.at(turn, NT * 2 * a))
                            weights(a + 1)
                        if what == "R":
                            sp.wait_ge(s_rc.sem, s_rc.at(turn, G * a + g + 1))
                            sp.dma_start(recip_rows, sums[:, :]).then_inc(s_rc_in.sem, 16)
                        fill(("attend", a, k))
                    fill(("norm", a))
                    if a == 0:
                        fill("ffn_norm")
                    if a == 2:
                        fill("rms")

            sequence(0, False)
            with sp.Fori(1, NB) as turn:
                sequence(turn, True)
            sp.wait_ge(s_o.sem, s_o.prior(NB, 4 * G))
            first_experts()
            expert_items(NB, 0, ITEMS)
            store(NB, out[NB - 1])
            sp.wait_ge(s_out.sem, s_out.at(NB - 1, 16))

        @block.tensor
        def _(pe):
            def product(dst, lhs_rhs):
                for i, (lhs, rhs) in enumerate(lhs_rhs):
                    ins_ = pe.matmul(dst, lhs, rhs, start=(i == 0), stop=(i == len(lhs_rhs) - 1))
                return ins_

            pe.wait_ge(s_l.sem, 16)
            a_fc, b_fc = lora[:, 0:D], lora[:, D:D + F]
            a_pr, b_pr = lora[:, D + F:D + 2 * F], lora[:, D + 2 * F:2 * D + 2 * F]
            for c in range(NC):
                for n in range(F // BANK):
                    i = pe.matmul(bank(2 * c + n), a_fc[:, c * P:(c + 1) * P], b_fc[:, n * BANK:(n + 1) * BANK],
                                  start=True, stop=True)
            i.then_inc(s_lora.sem, 1)
            for f in range(NF):
                i = pe.matmul(ps[:, 4 * BANK + f * D:4 * BANK + (f + 1) * D], a_pr[:, f * P:(f + 1) * P], b_pr,
                              start=True, stop=True)
            i.then_inc(s_lora.sem, 1)
            pe.wait_ge(s_w.sem, 16)
            pe.wait_ge(s_c.sem, 16 * 4)
            pe.wait_ge(s_loraout.sem, 2)

            def expert_items(turn, first, end, ring):
                for k in range(first, end):
                    what, e, m = EXPERT_WORK[k]
                    dst = bank(ring[k % len(ring)])
                    if k >= len(ring):
                        pe.wait_ge(s_done.sem, s_done.prior(turn, k - len(ring) + 1))
                    if what == "up":
                        if m == 0:
                            pe.wait_ge(s_w1[e % 2].sem, s_w1[e % 2].prior(turn, 16 * (e // 2 + 1)))
                        i = product(dst, [(w1[:, e % 2, n, m * P:(m + 1) * P], ht[:, n, :]) for n in range(NC)])
                    else:
                        if m == 0:
                            pe.wait_ge(s_w2[e % 2].sem, s_w2[e % 2].prior(turn, 16 * (e // 2 + 1)))
                            pe.wait_ge(s_done.sem, s_done.prior(turn, ITEM_AT["up", e, NH - 1] + 1))
                        for t in (2 * m, 2 * m + 1):
                            i = product(dst[:, (t % 2) * D:(t % 2 + 1) * D],
                                        [(eh[:, (NH * e + n) % EH_SLOTS, t * P:(t + 1) * P], w2[:, e % 2, n, :])
                                         for n in range(NH)])
                    i.then_inc(s_item.sem, 1)

            def tail(turn):
                for t in range(NT):
                    pe.wait_ge(s_norm.sem, s_norm.prior(turn, NT * 6 + t + 1))
                    for c in range(NC):
                        i = pe.transpose(ps[:, (6 + c) * BANK + t * P:(6 + c) * BANK + (t + 1) * P],
                                         y[:, t, c * P:(c + 1) * P], identf)
                i.then_inc(s_xtp.sem, 1)
                router = w3("router", NC)
                pe.wait_ge(s_xt.sem, s_xt.prior(turn, 6))
                for t in range(NT):
                    i = product(bank(0)[:, t * NE:(t + 1) * NE], [(ht[:, n, t * P:(t + 1) * P], router[:, n, :]) for n in range(NC)])
                i.then_inc(s_router.sem, 1)

            def sequence(turn, filled):
                def fill(place):
                    if filled:
                        expert_items(turn, *PLAN[place], EXPERT_BANKS)

                gates = w("gates").rearrange("p (g c n) -> p g c n", g=2, c=NC)
                pe.wait_ge(s_x.sem, s_x.at(turn, 16 * 2))
                for g in range(2):
                    for c in range(NC):
                        i = pe.matmul(bank(2 * g + c), gates[:, g, c, :], xt[:, c, :], start=True, stop=True)
                i.then_inc(s_gates.sem, 1)
                if filled:
                    tail(turn)
                fill("gates")
                fill("decay")
                pe.wait_ge(s_rg.sem, s_rg.at(turn, 1))
                for t in range(NT):
                    for c in range(NC):
                        i = pe.transpose(ps[:, 4 * BANK + t * D + c * P:4 * BANK + t * D + (c + 1) * P],
                                         xt[:, c, t * P:(t + 1) * P], identf)
                    i.then_inc(s_z.sem, 1)
                fill("rg")

                def to_feature_major(n, norm, src):
                    for t in range(NT):
                        pe.wait_ge(s_norm.sem, s_norm.at(turn, NT * norm + t + 1))
                        for c in range(NC):
                            i = pe.transpose(ps[:, (2 + c) * BANK + t * P:(2 + c) * BANK + (t + 1) * P],
                                             src[:, t, c * P:(c + 1) * P], identf)
                    i.then_inc(s_xtp.sem, 1)
                    pe.wait_ge(s_xt.sem, s_xt.at(turn, n + 1))

                def project(a, q_src, kv_src, nk=NC):
                    q, k, v, _ = attention_weights(a)
                    pe.wait_ge(s_wa[a % 2].sem, s_wa[a % 2].at(turn, 16 * (a // 2 + 1)))
                    for c in range(NC):
                        i = product(bank(c), [(q[:, n, c * P:(c + 1) * P], q_src[:, n, :]) for n in range(NC)])
                    i.then_inc(s_proj.sem, 1)
                    for c in range(NC):
                        i = product(bank(2 + c), [(k[:, n, c * P:(c + 1) * P], kv_src[:, n, :]) for n in range(nk)])
                    i.then_inc(s_proj.sem, 1)
                    for t in range(NT):
                        i = product(ps[:, 4 * BANK + t * D:4 * BANK + (t + 1) * D],
                                    [(kv_src[:, n, t * P:(t + 1) * P], v[:, n, :]) for n in range(nk)])
                    i.then_inc(s_proj.sem, 1)

                def attend(a, kind):
                    rows = ALL_ROWS - 3 if kind == ALIBI else ROWS
                    pe.wait_ge(s_op.sem, s_op.at(turn, 16 * 12 * (a + 1)))
                    pe.wait_ge(s_va.sem, s_va.at(turn, a + 1))
                    if kind == ALIBI:
                        pe.wait_ge(s_alibi.sem, s_alibi.at(turn, 32))
                    first, score, key = J * QUADS_BEFORE[kind], 0, 0
                    for k, (what, g, s, n) in enumerate(steps_of(kind)):
                        if k:
                            fill(("attend", a, k - 1))
                        if what == "S":
                            h = J * g + n
                            if score_bank_free(kind, score) > 0:
                                pe.wait_ge(s_max.sem, s_max.at(turn, first + score_bank_free(kind, score)))
                            dst = bank(score_bank(kind, score))
                            if kind == WINDOW:
                                for q in range(NT):
                                    t = slice(q * P, (q + 1) * P)
                                    i = pe.matmul(dst[:, t], qs[0:rows, h, t], ks[0:rows, h, t], start=True, stop=True)
                            elif kind == CAUSAL:
                                t = slice(s * P, (s + 1) * P)
                                pe.matmul(dst[:, 0:(s + 1) * P], qs[0:rows, h, t], ks[0:rows, h, 0:(s + 1) * P],
                                          start=True, stop=False)
                                i = pe.matmul(dst[:, t], identb, tri_q, start=False, stop=True)
                            else:
                                t = slice(s * P, (s + 1) * P)
                                fix = corrections(h, s) if kind == ALIBI else []
                                i = pe.matmul(dst, qs[0:rows, h, t], ks[0:rows, h, :], start=True, stop=not fix)
                                for m, (d, col) in enumerate(fix):
                                    i = pe.matmul(dst[:, (s - d) * P:(s - d + 1) * P], clamp[:, col:col + P], clamp_ident,
                                                  start=False, stop=(m == len(fix) - 1))
                            i.then_inc(s_s.sem, 1)
                            score += 1
                        elif what == "M":
                            pe.wait_ge(s_mp.sem, s_mp.at(turn, G * a + g + 1))
                            if g > 0:
                                pe.wait_ge(s_mc.sem, s_mc.at(turn, G * a + g))
                            rows_out = bank(2).bitcast(BF16)
                            for q in range(NT):
                                i = pe.transpose(rows_out[0:3 * J, q * P:(q + 1) * P],
                                                 mp[:, g, q, :, :].rearrange("p i j -> p (i j)"), identb)
                            i.then_inc(s_mt.sem, 1)
                        elif what == "T":
                            pe.wait_ge(s_md.sem, s_md.at(turn, 16 * (G * a + g + 1)))
                            h = J * g + n
                            if key == 0:
                                pe.wait_ge(s_max.sem, s_max.at(turn, first + scores_before_keys(kind)))
                            if key_bank_free(kind, key) > 0:
                                pe.wait_ge(s_exp.sem, s_exp.at(turn, first + key_bank_free(kind, key)))
                            dst = bank(key_bank(kind, key))
                            if kind == WINDOW:
                                for q in range(NT):
                                    t = slice(q * P, (q + 1) * P)
                                    i = pe.matmul(dst[:, t], ks[0:rows + 3, h, t], qs[0:rows + 3, h, t], start=True, stop=True)
                            else:
                                t = slice(s * P, (s + 1) * P)
                                lo = s * P if kind == CAUSAL else 0
                                d, np_ = CLAMPED.get(h, (NT, 0)) if kind == ALIBI else (NT, 0)
                                fixed = [(d, p) for p in range(np_) if d + s < NT]
                                if kind == MASKED:
                                    pe.matmul(dst, identb, negt[:, s, :], start=True, stop=False)
                                i = pe.matmul(dst[:, lo:S], ks[0:rows + 3, h, t], qs[0:rows + 3, h, lo:S],
                                              start=(kind != MASKED), stop=(kind != CAUSAL and not fixed))
                                if kind == CAUSAL:
                                    i = pe.matmul(dst[:, t], identb, tri_k, start=False, stop=True)
                                for m, (d, p) in enumerate(fixed):
                                    width = S - d * P
                                    col = CLAMP_AT[h] + p * width
                                    i = pe.matmul(dst[:, (d + s) * P:S], clamp_ident, clamp[:, col:col + S - (d + s) * P],
                                                  start=False, stop=(m == len(fixed) - 1))
                            i.then_inc(s_t.sem, 1)
                            key += 1
                        elif what == "V":
                            q_ = quad(kind, g, s)
                            pe.wait_ge(s_exp.sem, s_exp.at(turn, J * (q_ + 1)))
                            if kind == MASKED:
                                pe.wait_ge(s_pg.sem, s_pg.at(turn, NT * g + s + 1))
                                pe.wait_ge(s_pgp.sem, s_pgp.at(turn, NT * g + s + 1))
                            if s == 0 and (a or g):
                                pe.wait_ge(s_oc.sem, s_oc.at(turn, G * a + g))
                            slot = q_ % 2 if kind == MASKED else q_ % 3
                            begins, last = s == 0, s == STEPS[kind] - 1
                            if kind == WINDOW:
                                for q in range(NT):
                                    t = slice(q * P, (q + 1) * P)
                                    for n in range(J):
                                        i = pe.matmul(bank(3)[32 * n:32 * n + 32, t], va[:, q, J * g + n, :],
                                                      prob[:, slot, n, t], start=True, stop=True, tile_position=(0, 32 * n))
                            elif kind == MASKED:
                                for n in range(J):
                                    pe.matmul(bank(3)[32 * n:32 * n + 32, :], ones[:, :], prob[:, slot, n, :],
                                              start=begins, stop=False, tile_position=(0, 32 * n), skip_group_check=True)
                                for n in range(J):
                                    i = pe.matmul(bank(3)[32 * n:32 * n + 16, :], va[:, s, J * g + n, 0:HD],
                                                  prob[:, 2 + slot, n, :], start=False, stop=last,
                                                  tile_position=(0, 32 * n), skip_group_check=True)
                            else:
                                lo = s * P if kind == CAUSAL else 0
                                for n in range(J):
                                    i = pe.matmul(bank(3)[32 * n:32 * n + 32, lo:S], va[:, s, J * g + n, :],
                                                  prob[:, slot, n, lo:S], start=begins, stop=last, tile_position=(0, 32 * n))
                            i.then_inc(s_pv.sem, 1)
                    fill(("attend", a, k))

                def project_out(a):
                    wo = attention_weights(a)[3]
                    for groups in (range(G - 1), (G - 1,)):
                        pe.wait_ge(s_o.sem, s_o.at(turn, G * a + groups[-1] + 1))
                        for t in range(NT):
                            for g in groups:
                                i = pe.matmul(ps[:, 4 * BANK + t * D:4 * BANK + (t + 1) * D], ot[:, g, t * P:(t + 1) * P],
                                              wo[:, g, :], start=(g == 0 and t % 2 == 0), stop=(g == G - 1), skip_group_check=True)
                            if g == G - 1:
                                i.then_inc(s_z.sem, 1)
                    fill(("norm", a))

                to_feature_major(0, 0, x)
                fill(("xt", 0))
                project(0, xt, ct)
                fill(("project", 0))
                attend(0, WINDOW)
                project_out(0)
                to_feature_major(1, 1, x)
                fc, proj = w3("fc", NC), w3("proj", NF)
                if not filled:
                    pe.wait_ge(s_ffn.sem, 1)
                for m in range(NF):
                    if m >= 4:
                        pe.wait_ge(s_hc.sem, s_hc.at(turn, m - 3))
                    i = product(bank(m % 4), [(fc[:, n, m * P:(m + 1) * P], xt[:, n, :]) for n in range(NC)])
                    i.then_inc(s_h.sem, 1)
                pe.wait_ge(s_hc.sem, s_hc.at(turn, NF))
                if not filled:
                    pe.wait_ge(s_ffn.sem, 2)
                for t in range(NT):
                    i = product(ps[:, 4 * BANK + t * D:4 * BANK + (t + 1) * D],
                                [(hid[:, m, t * P:(t + 1) * P], proj[:, m, :]) for m in range(NF)])
                    i.then_inc(s_z.sem, 1)
                fill("ffn_norm")
                to_feature_major(2, 2, x)
                fill(("xt", 1))
                project(1, xt, xt)
                fill(("project", 1))
                attend(1, ALIBI)
                project_out(1)
                to_feature_major(3, 3, x)
                fill(("xt", 2))
                project(2, xt, ct)
                fill(("project", 2))
                pe.wait_ge(s_negt.sem, s_negt.at(turn, 1))
                attend(2, MASKED)
                project_out(2)
                fill("rms")
                to_feature_major(4, 5, y)
                product(bank(0), [(w3("m_lat", NC)[:, n, :], xt[:, n, :]) for n in range(NC)]).then_inc(s_lat.sem, 1)
                pe.wait_ge(s_latc.sem, s_latc.at(turn, 1))
                lat = ct[:, 0:1, :]
                fill(("xt", 3))
                project(3, xt, lat, nk=1)
                fill(("project", 3))
                attend(3, CAUSAL)
                project_out(3)
            sequence(0, False)
            with pe.Fori(1, NB) as turn:
                sequence(turn, True)
            tail(NB)
            expert_items(NB, 0, ITEMS, TAIL_BANKS)

        @block.scalar
        def _(act):
            step = Steps(s_act)
            act.wait_ge(s_sp.sem, 1)
            act.activation(small[:, 2:4], small[:, 0:2], ACT.Exp, scale=-1.0).then_inc(s_act.sem, step.one())
            act.wait_ge(s_act.sem, step.so_far())
            act.activation(small[:, 4:6], small[:, 2:4], ACT.Copy, bias=1.0).then_inc(s_act.sem, step.one())
            act.wait_ge(s_act.sem, step.so_far())
            act.activation(small[:, 6:8], small[:, 4:6], ACT.Ln).then_inc(s_act.sem, step.one())
            for n in range(2):
                act.wait_ge(s_lora.sem, n + 1)
                act.activation(lora_product[n], bank(4 * n, 4), ACT.Copy, scale=LORA_SCALING).then_inc(s_loraout.sem, 1)
            act.wait_ge(s_prep.sem, 1)

            def expert_items(turn, first, end, ring):
                for k in range(first, end):
                    what, e, m = EXPERT_WORK[k]
                    if what == "up":
                        act.wait_ge(s_item.sem, s_item.prior(turn, k + 1))
                        act.activation(eh[:, (NH * e + m) % EH_SLOTS, :], bank(ring[k % len(ring)]), ACT.Tanh, scale=0.5)\
                           .then_inc(s_th.sem, 1)

            def squares():
                for t in range(NT):
                    i = act.activation(big[:, 6144 + t * D:6144 + (t + 1) * D], x[:, t, :], ACT.Square, accum_out=ve[:, t:t + 1])
                return i

            def tail_squares(turn):
                act.wait_ge(s_sum.sem, s_sum.prior(turn, 1))
                squares().then_inc(s_ss.sem, 1)

            def tail_copy(turn):
                act.wait_ge(s_xtp.sem, s_xtp.prior(turn, 6))
                act.activation(ht[:, :, :].rearrange("p c s -> p (c s)"), bank(6, 2), ACT.Copy).then_inc(s_xt.sem, 1)

            def tail_exp(turn):
                act.wait_ge(s_dif.sem, s_dif.prior(turn, 1))
                act.activation(logit[:, 2, :], logit[:, 1, :], ACT.Exp).then_inc(s_rexp.sem, 1)

            def sequence(turn, filled):
                step.begin(turn)

                def fill(place):
                    if filled:
                        expert_items(turn, *PLAN[place], EXPERT_BANKS)

                if filled:
                    tail_squares(turn)

                act.wait_ge(s_gates.sem, s_gates.at(turn, 1))
                act.activation(tg.rearrange("p g c s -> p (g c s)"), bank(0, 4), ACT.Tanh, scale=0.5).then_inc(s_act.sem, step.one())
                act.wait_ge(s_act.sem, step.so_far())
                for c in range(NC):
                    i = act.activation(dec[:, c, :], tg[:, 1, c, :], ACT.Exp, bias=small[:, 12 + c:13 + c],
                                       scale=small[:, 12 + c:13 + c])
                i.then_inc(s_decay.sem, 1)
                if filled:
                    tail_copy(turn)
                act.wait_ge(s_sq.sem, s_sq.at(turn, 1))
                for c in range(NC):
                    i = act.activation(stp[:, c, :], stp[:, c, :], ACT.Sqrt, bias=small[:, 14:15], scale=-0.25)
                i.then_inc(s_mult.sem, 1)
                fill("gates")
                fill("decay")
                fill("rg")

                def copy_xt(n):
                    act.wait_ge(s_xtp.sem, s_xtp.at(turn, n + 1))
                    act.activation(xt[:, :, :].rearrange("p c s -> p (c s)"), bank(2, 2), ACT.Copy).then_inc(s_xt.sem, 1)

                def split(a, qb, kb):
                    for o, (b, scale) in enumerate(((qb, QSCALE), (kb, 1.0))):
                        act.wait_ge(s_proj.sem, s_proj.at(turn, 3 * a + o + 1))
                        for c in range(NC):
                            bias = b[:, c:c + 1] if b is not None else 0.0
                            i = act.activation(parts[:, o, 0, c, :], bank(2 * o + c), ACT.Identity, bias=bias, scale=scale)
                        i.then_inc(s_p[0].sem, 1)
                        for c in range(NC):
                            bias = b[:, c:c + 1] if b is not None else 0.0
                            i = act.activation(qk[:, o, c, :], bank(2 * o + c), ACT.Identity, bias=bias, scale=scale)
                        i.then_inc(s_f.sem, 1)

                def attend(a, kind):
                    first, key = J * QUADS_BEFORE[kind], 0
                    for k, (what, g, s, n) in enumerate(steps_of(kind)):
                        if k:
                            fill(("attend", a, k - 1))
                        if what == "M":
                            act.wait_ge(s_mt.sem, s_mt.at(turn, G * a + g + 1))
                            if a or g:
                                act.wait_ge(s_md.sem, s_md.at(turn, 16 * (G * a + g)))
                            act.activation(mrow[:, :], bank(2)[0:3 * J, :].bitcast(BF16)[:, 0:S], ACT.Copy)\
                               .then_inc(s_mc.sem, 1)
                        elif what == "C":
                            act.wait_ge(s_pv.sem, s_pv.at(turn, quad(kind, g, STEPS[kind] - 1) + 1))
                            act.activation(ot[:, g, :], bank(3), ACT.Copy).then_inc(s_oc.sem, 1)
                        elif what == "T":
                            q_ = quad(kind, g, s)
                            ring = 2 if kind == MASKED else 3
                            slot = q_ % ring
                            if n == 0 and q_ - ring >= QUADS_BEFORE[kind]:
                                act.wait_ge(s_pv.sem, s_pv.at(turn, q_ - ring + 1))
                            lo = s * P if kind == CAUSAL else 0
                            act.wait_ge(s_t.sem, s_t.at(turn, first + key + 1))
                            act.activation(prob[:, slot, n, lo:S], bank(key_bank(kind, key))[:, lo:S], ACT.Exp)\
                               .then_inc(s_exp.sem, 1)
                            key += 1
                    fill(("attend", a, k))

                copy_xt(0)
                if filled:
                    tail_exp(turn)
                fill(("xt", 0))
                split(0, small[:, 8:10], w("l0_kb"))
                fill(("project", 0))
                attend(0, WINDOW)
                fill(("norm", 0))
                copy_xt(1)
                for m in range(NF):
                    act.wait_ge(s_h.sem, s_h.at(turn, m + 1))
                    act.activation(hid[:, m, :], bank(m % 4), ACT.Gelu, bias=w("fc_b")[:, m:m + 1]).then_inc(s_hc.sem, 1)
                fill("ffn_norm")
                copy_xt(2)
                fill(("xt", 1))
                split(1, small[:, 10:12], w("l1_kb"))
                fill(("project", 1))
                attend(1, ALIBI)
                fill(("norm", 1))
                copy_xt(3)
                fill(("xt", 2))
                split(2, small[:, 16:18], w("x_kb"))
                fill(("project", 2))
                attend(2, MASKED)
                fill(("norm", 2))
                act.wait_ge(s_norm.sem, s_norm.at(turn, 5 * NT))
                squares().then_inc(s_ss.sem, 1)
                fill("rms")
                copy_xt(4)
                act.wait_ge(s_lat.sem, s_lat.at(turn, 1))
                act.activation(ct[:, 0, :], bank(0), ACT.Copy).then_inc(s_latc.sem, 1)
                fill(("xt", 3))
                split(3, None, None)
                fill(("project", 3))
                attend(3, CAUSAL)
                fill(("norm", 3))
                step.end()

            sequence(0, False)
            with act.Fori(1, NB) as turn:
                sequence(turn, True)
            tail_squares(NB)
            tail_copy(NB)
            tail_exp(NB)
            expert_items(NB, 0, ITEMS, TAIL_BANKS)

        @block.gpsimd
        def _(pool):
            pool.memset(va[:, :, :, :].rearrange("p t h n -> p (t h n)"), 1.0).then_inc(s_set.sem, 1)
            pool.memset(ones[:, 0:HD], 0.0).then_inc(s_set.sem, 1)
            pool.memset(ones[:, HD:32], 1.0).then_inc(s_set.sem, 1)
            pool.memset(small[:, 14:15], 0.25).then_inc(s_set.sem, 1)
            pool.wait_ge(s_c.sem, 16 * 4)

            def weights_maximum():
                for n in range(2):
                    pool.wait_ge(s_amax.sem, n + 1)
                    pool.partition_all_reduce(small[:, 20 + n:21 + n], small[:, 18 + n:19 + n], P, RMAX)\
                        .then_inc(s_amaxall.sem, 1)

            def final_inverse_root(turn):
                pool.wait_ge(s_fvar.sem, s_fvar.prior(turn, 1))
                pool.tensor_tensor(frstd[:, :], fve[:, :], half[:, :], ALU.pow).then_inc(s_frstd.sem, 1)

            def tail(turn):
                pool.wait_ge(s_var.sem, s_var.prior(turn, 7))
                pool.tensor_tensor(rstd[:, :], ve[:, :], half[:, :], ALU.pow).then_inc(s_rstd.sem, 1)

            def sequence(turn, filled):
                if filled:
                    tail(turn)

                def inverse_root(n):
                    pool.wait_ge(s_var.sem, s_var.at(turn, n + 1))
                    pool.tensor_tensor(rstd[:, :], ve[:, :], half[:, :], ALU.pow).then_inc(s_rstd.sem, 1)

                def add_bias(n, name):
                    pool.wait_ge(s_xtp.sem, s_xtp.at(turn, n + 1))
                    pool.tensor_tensor(x[:, :, :], x[:, :, :], w(name).rearrange("p (a n) -> p a n", a=1)
                                       .to_broadcast([P, NT, D]), ALU.add).then_inc(s_bias.sem, 1)

                for n, name in enumerate(("l0_ob", "proj_b", "l1_ob", "x_ob")):
                    inverse_root(n)
                    add_bias(n, name)
                    if n == 0 and not filled:
                        weights_maximum()
                pool.wait_ge(s_side.sem, s_side.at(turn, 16 * 3))
                for g in range(G):
                    for s in range(NT):
                        q_ = quad(MASKED, g, s)
                        pool.wait_ge(s_exp.sem, s_exp.at(turn, J * (q_ + 1)))
                        if q_ - 2 >= QUADS_BEFORE[MASKED]:
                            pool.wait_ge(s_pv.sem, s_pv.at(turn, q_ - 1))
                        for n in range(2, J):
                            i = pool.tensor_tensor(prob[:, 2 + q_ % 2, n, :], prob[:, q_ % 2, n, :], grp[:, s, :], ALU.mult)
                        i.then_inc(s_pgp.sem, 1)
                inverse_root(4)
                inverse_root(5)
                if filled:
                    final_inverse_root(turn)

            sequence(0, False)
            with pool.Fori(1, NB) as turn:
                sequence(turn, True)
            tail(NB)
            final_inverse_root(NB)

        @block.vector
        def _(dve):
            step = Steps(s_vec)
            dve.wait_ge(s_w.sem, 16)
            dve.wait_ge(s_set.sem, 4)
            ap = w("a_param")
            dve.tensor_scalar(small[:, 0:2], ap, -1.0, None, ALU.mult).then_inc(s_vec.sem, step.one())
            dve.wait_ge(s_vec.sem, step.so_far())
            dve.tensor_tensor(small[:, 0:2], small[:, 0:2], ap, ALU.max).then_inc(s_sp.sem, 1)
            for name, at in (("l0_qb", 8), ("l1_qb", 10), ("x_qb", 16)):
                dve.tensor_scalar(small[:, at:at + 2], w(name), QSCALE, None, ALU.mult).then_inc(s_vec.sem, step.one())
            dve.wait_ge(s_act.sem, ACT_ONCE)
            e_, u_, l_ = small[:, 2:4], small[:, 4:6], small[:, 6:8]
            dve.tensor_scalar(u_, u_, -1.0, 1e-30, ALU.add, ALU.add).then_inc(s_vec.sem, step.one())
            dve.tensor_scalar(l_, l_, 1e-30, None, ALU.add).then_inc(s_vec.sem, step.one())
            dve.wait_ge(s_vec.sem, step.so_far())
            dve.reciprocal(u_, u_).then_inc(s_vec.sem, step.one())
            dve.wait_ge(s_vec.sem, step.so_far())
            dve.tensor_tensor(l_, l_, u_, ALU.mult).then_inc(s_vec.sem, step.one())
            dve.wait_ge(s_vec.sem, step.so_far())
            dve.tensor_tensor(l_, l_, e_, ALU.mult).then_inc(s_vec.sem, step.one())
            dve.tensor_scalar(small[:, 12:14], ap, 0.0, None, ALU.max).then_inc(s_vec.sem, step.one())
            dve.wait_ge(s_vec.sem, step.so_far())
            dve.tensor_tensor(l_, l_, small[:, 12:14], ALU.add).then_inc(s_vec.sem, step.one())
            dve.wait_ge(s_vec.sem, step.so_far())
            dve.tensor_scalar(small[:, 12:14], l_, -4.0, None, ALU.mult).then_inc(s_prep.sem, 1)

            quant = Steps(s_quant)
            scale, inv = small[:, 20:22], small[:, 22:24]

            def weights_maximum():
                dve.wait_ge(s_wf.sem, 16)
                for n, name in enumerate(("fc", "proj")):
                    dve.tensor_reduce(small[:, 18 + n:19 + n], w(name), AX.X, ALU.max, apply_absolute_value=True)\
                       .then_inc(s_amax.sem, 1)

            def weights_scales():
                dve.wait_ge(s_amaxall.sem, 2)
                dve.tensor_scalar(scale, scale, 1.0 / QMAX, None, ALU.mult).then_inc(s_quant.sem, quant.one())
                dve.wait_ge(s_quant.sem, quant.so_far())
                dve.reciprocal(inv, scale).then_inc(s_quant.sem, quant.one())
                dve.wait_ge(s_quant.sem, quant.so_far())

            def quantise(n, name):
                wt = w(name)
                dve.tensor_scalar(qtmp, wt, inv[:, n:n + 1], ROUND, ALU.mult, ALU.add).then_inc(s_quant.sem, quant.one())
                dve.wait_ge(s_quant.sem, quant.so_far())
                dve.tensor_scalar(qtmp, qtmp, -ROUND, QMAX, ALU.add, ALU.min).then_inc(s_quant.sem, quant.one())
                dve.wait_ge(s_quant.sem, quant.so_far())
                dve.tensor_scalar(qtmp, qtmp, -QMAX - 1.0, scale[:, n:n + 1], ALU.max, ALU.mult).then_inc(s_quant.sem, quant.one())
                dve.wait_ge(s_quant.sem, quant.so_far())
                dve.tensor_tensor(qtmp, qtmp, wt, ALU.subtract).then_inc(s_quant.sem, quant.one())
                dve.wait_ge(s_quant.sem, quant.so_far())
                dve.tensor_tensor(wt, wt, qtmp, ALU.add).then_inc(s_quant.sem, quant.one())
                dve.wait_ge(s_quant.sem, quant.so_far())
                dve.wait_ge(s_loraout.sem, n + 1)
                dve.tensor_tensor(wt, wt, lora_product[n], ALU.add).then_inc(s_ffn.sem, 1)

            carried = []

            def carry():
                dve.memset(spare[:, len(carried):len(carried) + 1], 0.0)
                carried.append(0)

            def expert_item(turn, k, ring):
                what, e, m = EXPERT_WORK[k]
                src = bank(ring[k % len(ring)])
                if what == "up":
                    slot = eh[:, (NH * e + m) % EH_SLOTS, :]
                    dve.wait_ge(s_th.sem, s_th.prior(turn, NH * e + m + 1))
                    dve.scalar_tensor_tensor(slot, slot, 1.0, src, ALU.add, ALU.mult).then_inc(s_done.sem, 1)
                else:
                    dve.wait_ge(s_item.sem, s_item.prior(turn, k + 1))
                    if e:
                        dve.wait_ge(s_done.sem, s_done.prior(turn, ITEM_AT["down", e - 1, m] + 1))
                    for t in (2 * m, 2 * m + 1):
                        i = dve.scalar_tensor_tensor(ys[:, t, :], src[:, (t % 2) * D:(t % 2 + 1) * D], comb[:, t, e:e + 1],
                                                     ys[:, t, :], ALU.mult, ALU.add)
                    i.then_inc(s_done.sem, 1)

            def final_norm(turn):
                dve.wait_ge(s_done.sem, s_done.prior(turn, ITEMS))
                for t in range(NT):
                    dve.bn_stats(fstats[:, t, :], ys[:, t, :]).then_inc(s_fstat.sem, 1)
                dve.wait_ge(s_fstat.sem, s_fstat.prior(turn, NT))
                carry()
                for t in range(NT):
                    dve.bn_aggr(fmv[:, t, :], fstats[:, t, :]).then_inc(s_fmv.sem, 1)
                dve.wait_ge(s_fmv.sem, s_fmv.prior(turn, NT))
                dve.tensor_scalar(fve[:, :], fmv[:, :, 1], LN_EPS, None, ALU.add).then_inc(s_fvar.sem, 1)

            def final_scale(turn):
                dve.wait_ge(s_frstd.sem, s_frstd.prior(turn, 1))
                for t in range(NT):
                    dve.tensor_scalar(ys[:, t, :], ys[:, t, :], fmv[:, t, 0:1], frstd[:, t:t + 1],
                                      ALU.subtract, ALU.mult).then_inc(s_final.sem, 1)

            def z(t):
                return ps[:, 4 * BANK + t * D:4 * BANK + (t + 1) * D]

            tail = Steps(s_tail, late=True)

            def tail_norm(turn):
                tail.begin(turn)
                for t in range(NT):
                    if t % 2 == 0:
                        dve.wait_ge(s_z.sem, s_z.prior(turn, NT * 5 + t + 2))
                    dve.scalar_tensor_tensor(ys[:, t, :], x[:, t, :], 2.0, z(t), ALU.mult, ALU.add).then_inc(s_tail.sem, tail.one())
                dve.wait_ge(s_tail.sem, tail.so_far())
                for t in range(NT):
                    i = dve.tensor_tensor(x[:, t, :], z(t), x[:, t, :], ALU.add)
                i.then_inc(s_sum.sem, 1)
                dve.wait_ge(s_ss.sem, s_ss.prior(turn, 2))
                dve.tensor_scalar(ve[:, :], ve[:, :], 1.0 / D, RMS_EPS, ALU.mult, ALU.add).then_inc(s_var.sem, 1)
                dve.wait_ge(s_rstd.sem, s_rstd.prior(turn, 7))
                for t in range(NT):
                    dve.scalar_tensor_tensor(y[:, t, :], x[:, t, :], rstd[:, t:t + 1], w("g2"), ALU.mult, ALU.mult)\
                       .then_inc(s_norm.sem, 1)

            def tail_logits(turn):
                dve.wait_ge(s_router.sem, s_router.prior(turn, 1))
                dve.tensor_copy(logit[:, 0, :], bank(0)[:, 0:NT * NE]).then_inc(s_tail.sem, tail.one())

            def tail_router(turn):
                lg, ld, le, lr = (logit[:, i, :] for i in range(4))
                te = "p (t e) -> p t e"
                dve.wait_ge(s_tail.sem, tail.so_far())
                dve.tensor_reduce(gat[:, 0, :], lg.rearrange(te, t=NT), AX.X, ALU.max).then_inc(s_tail.sem, tail.one())
                l3 = lg.rearrange(te, t=NT)
                dve.wait_ge(s_tail.sem, tail.so_far())
                for t in range(NT):
                    i = dve.tensor_scalar(ld[:, t * NE:(t + 1) * NE], lg[:, t * NE:(t + 1) * NE], gat[:, 0, t:t + 1], None,
                                          ALU.subtract)
                i.then_inc(s_dif.sem, 1)
                for t in range(NT):
                    other = l3[:, t:t + 1, :].to_broadcast([P, NE, NE])
                    own = l3[:, t, :].rearrange("p (e a) -> p e a", a=1).to_broadcast([P, NE, NE])
                    for i, op in enumerate((ALU.is_gt, ALU.is_equal)):
                        dve.tensor_tensor(rank[:, i, t * NE * NE:(t + 1) * NE * NE].rearrange("p (e f) -> p e f", e=NE),
                                                    other, own, op).then_inc(s_tail.sem, tail.one())
                dve.wait_ge(s_tail.sem, tail.so_far())
                for t in range(NT):
                    r1 = rank[:, 1, t * NE * NE:(t + 1) * NE * NE]
                    dve.tensor_tensor(r1, r1, w("before"), ALU.mult).then_inc(s_tail.sem, tail.one())
                dve.wait_ge(s_tail.sem, tail.so_far())
                dve.tensor_tensor(rank[:, 0, :], rank[:, 0, :], rank[:, 1, :], ALU.add).then_inc(s_tail.sem, tail.one())
                dve.wait_ge(s_tail.sem, tail.so_far())
                dve.tensor_reduce(lr, rank[:, 0, :].rearrange("p (a f) -> p a f", f=NE), AX.X, ALU.add).then_inc(s_tail.sem, tail.one())
                dve.wait_ge(s_tail.sem, tail.so_far())
                dve.wait_ge(s_rexp.sem, s_rexp.prior(turn, 1))
                dve.scalar_tensor_tensor(lr, lr, 2.0, le, ALU.is_lt, ALU.mult).then_inc(s_tail.sem, tail.one())
                dve.wait_ge(s_tail.sem, tail.so_far())
                dve.tensor_reduce(gat[:, 1, :], lr.rearrange(te, t=NT), AX.X, ALU.add).then_inc(s_tail.sem, tail.one())
                dve.wait_ge(s_tail.sem, tail.so_far())
                dve.reciprocal(gat[:, 2, :], gat[:, 1, :]).then_inc(s_tail.sem, tail.one())
                dve.wait_ge(s_tail.sem, tail.so_far())
                for t in range(NT):
                    dve.tensor_scalar(comb[:, t, :], lr[:, t * NE:(t + 1) * NE], gat[:, 2, t:t + 1], 0.5, ALU.mult, ALU.mult).then_inc(s_tail.sem, tail.one())
                dve.wait_ge(s_tail.sem, tail.so_far())
                tail.end()

            def sequence(turn, filled):
                step.begin(turn)
                carried.clear()
                todo = list(range(ITEMS))

                def fill(place):
                    if not filled:
                        return
                    first, end = PLAN[place]
                    while todo and todo[0] < (end if place in CATCH_UP else first):
                        expert_item(turn, todo.pop(0), EXPERT_BANKS)
                    if place == FINAL:
                        final_norm(turn)
                    if place == FINAL[:2] + (FINAL[2] + 8,):
                        final_scale(turn)
                    if place == ("attend", 3, len(steps_of(CAUSAL)) - 1):
                        dve.wait_ge(s_out.sem, s_out.prior(turn, 16))
                        carry()

                if filled:
                    tail_norm(turn)

                dve.wait_ge(s_decay.sem, s_decay.at(turn, 1))
                dve.tensor_tensor(stp, dec, dec, ALU.mult).then_inc(s_vec.sem, step.one())
                dve.wait_ge(s_vec.sem, step.so_far())
                dve.tensor_scalar(stp, stp, 1.0, None, ALU.min).then_inc(s_sq.sem, 1)
                dve.scalar_tensor_tensor(gx, tg[:, 0, :, :], 1.0, xt[:, :, :], ALU.add, ALU.mult).then_inc(s_vec.sem, step.one())
                dve.wait_ge(s_vec.sem, step.so_far())
                dve.wait_ge(s_mult.sem, s_mult.at(turn, 1))
                dve.tensor_tensor(gx, gx, stp, ALU.mult).then_inc(s_vec.sem, step.one())
                dve.wait_ge(s_vec.sem, step.so_far())
                for c in range(NC):
                    dve.tensor_tensor_scan(st[:, c, :], dec[:, c, :], gx[:, c, :], 0.0, ALU.mult, ALU.add).then_inc(s_vec.sem, step.one())
                dve.wait_ge(s_vec.sem, step.so_far())
                dve.tensor_tensor(xt[:, :, :], xt[:, :, :], st, ALU.add).then_inc(s_rg.sem, 1)

                def moments(n, src, place):
                    for t in range(NT):
                        dve.bn_stats(stats[:, t, :], src(t)).then_inc(s_vec.sem, step.one())
                    dve.wait_ge(s_vec.sem, step.so_far())
                    carry()
                    for t in range(NT):
                        dve.bn_aggr(mv[:, t, :], stats[:, t, :]).then_inc(s_vec.sem, step.one())
                    dve.wait_ge(s_vec.sem, step.so_far())
                    dve.tensor_scalar(ve[:, :], mv[:, :, 1], LN_EPS, None, ALU.add).then_inc(s_var.sem, 1)
                    fill(place)
                    dve.wait_ge(s_rstd.sem, s_rstd.at(turn, n + 1))
                    for t in range(NT):
                        dve.tensor_scalar(x[:, t, :], src(t), mv[:, t, 0:1], rstd[:, t:t + 1],
                                          ALU.subtract, ALU.mult).then_inc(s_norm.sem, 1)

                def layer_norm(n, zi, place):
                    for t in range(NT):
                        if t % 2 == 0:
                            dve.wait_ge(s_z.sem, s_z.at(turn, NT * zi + t + 2))
                        if zi and t == 0:
                            dve.wait_ge(s_bias.sem, s_bias.at(turn, zi))
                        if zi:
                            dve.tensor_tensor(y[:, t, :], z(t), x[:, t, :], ALU.add).then_inc(s_vec.sem, step.one())
                    if zi:
                        dve.wait_ge(s_vec.sem, step.so_far())
                    moments(n, (lambda t: y[:, t, :]) if zi else z, place)

                def rms_norm(n, k, gain, place):
                    dve.wait_ge(s_ss.sem, s_ss.at(turn, k + 1))
                    dve.tensor_scalar(ve[:, :], ve[:, :], 1.0 / D, RMS_EPS, ALU.mult, ALU.add).then_inc(s_var.sem, 1)
                    fill(place)
                    dve.wait_ge(s_rstd.sem, s_rstd.at(turn, n + 1))
                    for t in range(NT):
                        dve.scalar_tensor_tensor(y[:, t, :], x[:, t, :], rstd[:, t:t + 1], w(gain), ALU.mult, ALU.mult)\
                           .then_inc(s_norm.sem, 1)

                def split(a, vb):
                    for o in range(2):
                        f = qk[:, o, :, :]
                        dve.wait_ge(s_f.sem, s_f.at(turn, 2 * a + o + 1))
                        dve.tensor_tensor(f, f, parts[:, o, 0, :, :], ALU.subtract).then_inc(s_vec.sem, step.one())
                        dve.wait_ge(s_vec.sem, step.so_far())
                        dve.tensor_copy(parts[:, o, 1, :, :], f).then_inc(s_p[1].sem, 1)
                        dve.wait_ge(s_p[1].sem, s_p[1].at(turn, 2 * a + o + 1))
                        dve.tensor_tensor(parts[:, o, 2, :, :], f, parts[:, o, 1, :, :], ALU.subtract)\
                           .then_inc(s_p[2].sem, 1)
                    dve.wait_ge(s_proj.sem, s_proj.at(turn, 3 * a + 3))
                    vout = va[:, :, :, 0:HD]
                    vin = bank(4, 2).rearrange("p (t h d) -> p t h d", t=NT, h=H)
                    if vb is None:
                        i = dve.tensor_copy(vout, vin)
                    else:
                        for t in range(NT):
                            i = dve.tensor_tensor(vout[:, t, :, :], vin[:, t, :, :],
                                                  w(vb).rearrange("p (h d) -> p h d", h=H), ALU.add)
                    i.then_inc(s_va.sem, 1)

                def attend(a, kind):
                    first, score = J * QUADS_BEFORE[kind], 0
                    for k, (what, g, s, n) in enumerate(steps_of(kind)):
                        if k:
                            fill(("attend", a, k - 1))
                        if what == "S":
                            dve.wait_ge(s_s.sem, s_s.at(turn, first + score + 1))
                            if kind == MASKED:
                                carry()
                            src = bank(score_bank(kind, score))
                            if kind == WINDOW:
                                i = dve.tensor_reduce(mx[:, g, :, n], src.rearrange("p (q k) -> p q k", q=NT), AX.X, ALU.max)
                            elif kind == MASKED:
                                i = dve.tensor_tensor_reduce(out=src, in0=src, in1=neg[:, s, :], scale=1.0, scalar=LOWEST,
                                                             op0=ALU.add, op1=ALU.max, accum_out=mx[:, g, s, n:n + 1])
                            else:
                                width = (s + 1) * P if kind == CAUSAL else S
                                i = dve.tensor_reduce(mx[:, g, s, n:n + 1], src[:, 0:width], AX.X, ALU.max)
                            i.then_inc(s_max.sem, 1)
                            score += 1
                        elif what == "P":
                            m, p3 = mx[:, g, :, :], mp[:, g, :, :, :]
                            dve.wait_ge(s_max.sem, s_max.at(turn, J * (QUADS_BEFORE[kind] + (g + 1) * STEPS[kind])))
                            dve.tensor_scalar(p3[:, :, 0, :], m, -1.0, None, ALU.mult).then_inc(s_vec.sem, step.one())
                            dve.wait_ge(s_vec.sem, step.so_far())
                            dve.scalar_tensor_tensor(mr[:, :, :], m, -1.0, p3[:, :, 0, :], ALU.mult, ALU.subtract).then_inc(s_vec.sem, step.one())
                            dve.wait_ge(s_vec.sem, step.so_far())
                            dve.tensor_copy(p3[:, :, 1, :], mr[:, :, :]).then_inc(s_vec.sem, step.one())
                            dve.wait_ge(s_vec.sem, step.so_far())
                            dve.tensor_tensor(p3[:, :, 2, :], mr[:, :, :], p3[:, :, 1, :], ALU.subtract).then_inc(s_mp.sem, 1)
                        elif what == "E":
                            q_ = quad(kind, g, s)
                            slot = q_ % 2
                            dve.wait_ge(s_exp.sem, s_exp.at(turn, J * q_ + 2))
                            if q_ - 2 >= QUADS_BEFORE[kind]:
                                dve.wait_ge(s_pv.sem, s_pv.at(turn, q_ - 1))
                            if NT * g + s == 0:
                                dve.wait_ge(s_side.sem, s_side.at(turn, 16 * 3))
                            for n in range(2):
                                i = dve.tensor_tensor(prob[:, 2 + slot, n, :], prob[:, slot, n, :], grp[:, s, :], ALU.mult)
                            i.then_inc(s_pg.sem, 1)
                        elif what == "R":
                            dve.wait_ge(s_sum_in.sem, s_sum_in.at(turn, 16 * (G * a + g + 1)))
                            dve.reciprocal(sums[:, :], sums[:, :]).then_inc(s_rc.sem, 1)
                        elif what == "N":
                            dve.wait_ge(s_rc_in.sem, s_rc_in.at(turn, 16 * (G * a + g + 1)))
                            carry()
                            dve.stream_shuffle(rinv, xt[:, 1, :], [HD] * 32).then_inc(s_vec.sem, step.one())
                            dve.wait_ge(s_vec.sem, step.so_far())
                            dve.tensor_tensor(ot[:, g, :], ot[:, g, :], rinv, ALU.mult).then_inc(s_o.sem, 1)
                    fill(("attend", a, k))

                fill("decay")
                if filled:
                    tail_logits(turn)
                layer_norm(0, 0, "rg")
                if filled:
                    tail_router(turn)
                else:
                    weights_maximum()
                fill(("xt", 0))
                split(0, "l0_vb")
                if not filled:
                    weights_scales()
                    quantise(0, "fc")
                fill(("project", 0))
                attend(0, WINDOW)
                layer_norm(1, 1, ("norm", 0))
                fill("ffn")
                if not filled:
                    quantise(1, "proj")
                layer_norm(2, 2, "ffn_norm")
                fill(("xt", 1))
                split(1, "l1_vb")
                fill(("project", 1))
                attend(1, ALIBI)
                layer_norm(3, 3, ("norm", 1))
                fill(("xt", 2))
                split(2, "x_vb")
                dve.wait_ge(s_side.sem, s_side.at(turn, 16 * 2))
                dve.tensor_scalar(neg, neg.bitcast(I32), -NEG, NEG, ALU.mult, ALU.add).then_inc(s_vec.sem, step.one())
                dve.tensor_scalar(negt, grp.bitcast(I32), -NEG, NEG, ALU.mult, ALU.add).then_inc(s_negt.sem, 1)
                dve.wait_ge(s_vec.sem, step.so_far())
                fill(("project", 2))
                attend(2, MASKED)
                layer_norm(4, 4, ("norm", 2))
                fill("squares")
                rms_norm(5, 0, "g1", "rms")
                fill(("xt", 3))
                split(3, None)
                fill(("project", 3))
                attend(3, CAUSAL)
                assert not filled or not todo
                step.end()

            sequence(0, False)
            with dve.Fori(1, NB) as turn:
                sequence(turn, True)
            carried.clear()
            tail_norm(NB)
            tail_logits(NB)
            tail_router(NB)
            for k in range(ITEMS):
                expert_item(NB, k, TAIL_BANKS)
            final_norm(NB)
            final_scale(NB)


def by_heads(np, v):
    a = v.reshape(v.shape[:-1] + (H // NC, NC, HD))
    return np.ascontiguousarray(np.moveaxis(a, (-3, -2, -1), (-1, -3, -2))).reshape(v.shape)


def lay_out(np, i):
    def rows(m):
        return np.ascontiguousarray(m.reshape(m.shape[0] // P, P, -1).transpose(1, 0, 2)).reshape(P, -1)

    def padded(m):
        out = np.zeros((G, J, 32, D), np.float32)
        out[:, :, 0:HD] = m.reshape(G, J, HD, D)
        return np.ascontiguousarray(out.reshape(G, P, D).transpose(1, 0, 2)).reshape(P, G * D)

    def column(v):
        return np.ascontiguousarray(v.reshape(-1, P).T)

    def everywhere(v):
        return np.broadcast_to(v.reshape(1, -1), (P, v.size))

    def diagonal(m):
        out = np.zeros((NC, P, P), np.float32)
        for h in range(8):
            c, at = h // 4, 32 * (h % 4)
            out[c, at:at + 32, at:at + 32] = m[h]
        return np.ascontiguousarray(out.transpose(1, 0, 2)).reshape(P, NC * P)

    w0, b0 = i["L0_xattn_in_proj_w"], i["L0_xattn_in_proj_b"]
    w1, b1 = i["L1_attn_in_proj_weight"], i["L1_attn_in_proj_bias"]
    p = {
        "gates": np.concatenate([diagonal(i["L0_attn_w_in"]), diagonal(i["L0_attn_w_a"])], 1),
        "a_param": column(i["L0_attn_a_param"]),
        "fc": rows(i["L0_ffn_W_fc"].T), "fc_b": column(i["L0_ffn_b_fc"]),
        "proj": rows(i["L0_ffn_W_proj"].T), "proj_b": everywhere(i["L0_ffn_b_proj"]),
        "m_lat": rows(i["L1_ffn_Wdkv"]), "g1": everywhere(i["L1_ffn_g1"]), "g2": everywhere(i["L1_ffn_g2"]),
        "router": rows(i["L1_ffn_gate_w"]), "ident": np.eye(P, dtype=np.float32),
        "before": everywhere(np.tril(np.ones((NE, NE), np.float32), -1)),
    }
    attention = []
    for name, wq, wk, wv, wo, bq, bk, bv, bo in (
        ("l0", w0[:D].T, w0[D:2 * D].T, w0[2 * D:].T, i["L0_xattn_out_w"].T,
         b0[:D], b0[D:2 * D], b0[2 * D:], i["L0_xattn_out_b"]),
        ("l1", w1[:D].T, w1[D:2 * D].T, w1[2 * D:].T, i["L1_attn_out_proj_weight"].T,
         b1[:D], b1[D:2 * D], b1[2 * D:], i["L1_attn_out_proj_bias"]),
        ("x", i["L1_xattn_wq_k"], i["L1_xattn_wk_k"], i["L1_xattn_wv_k"], i["L1_xattn_wo_k"],
         i["L1_xattn_wq_b"], i["L1_xattn_wk_b"], i["L1_xattn_wv_b"], i["L1_xattn_wo_b"]),
    ):
        attention.append([rows(by_heads(np, wq)), rows(by_heads(np, wk)), rows(wv), padded(wo)])
        p |= {name + "_qb": column(by_heads(np, bq)), name + "_kb": column(by_heads(np, bk)),
              name + "_vb": everywhere(bv), name + "_ob": everywhere(bo)}
    half = np.zeros((P, D), np.float32)
    attention.append([rows(by_heads(np, i["L1_ffn_Wq"])),
                      np.concatenate([by_heads(np, i["L1_ffn_Wuk"]), half], 1),
                      np.concatenate([i["L1_ffn_Wuv"], half], 1), padded(i["L1_ffn_Wo"])])
    pack = np.concatenate([p[name].reshape(P, n) for name, n in PACK], 1)

    def tiles(a):
        return np.ascontiguousarray(a.reshape(NB, a.shape[1] // P, P, a.shape[2]).transpose(0, 2, 1, 3))

    return {
        "pack": pack, "attention": np.stack([np.concatenate(m, 1) for m in attention]),
        "lora": np.concatenate([i["L0_ffn_A_fc"], i["L0_ffn_B_fc"].T, i["L0_ffn_A_proj"], i["L0_ffn_B_proj"].T], 1),
        "x": tiles(i["x"].transpose(0, 2, 1)), "c": tiles(i["ctx_1024"].transpose(0, 2, 1)),
        "group": tiles(i["fside_BxSxS2_0"].transpose(0, 2, 1)),
        "mask": tiles(i["mask_BxSxS2_ik1"]), "mask_t": tiles(i["mask_BxSxS2_ik1"].transpose(0, 2, 1)),
        "w1": np.ascontiguousarray(i["L1_ffn_w1"].reshape(NE, NC, P, EH).transpose(0, 2, 1, 3)),
        "w2": np.ascontiguousarray(i["L1_ffn_w2"].reshape(NE, NH, P, D).transpose(0, 2, 1, 3)),
    } | constants(np)


def constants(np):
    bf16 = mybir.dt.np(BF16)

    def in_parts(v, count=3, dtype=bf16):
        out = []
        for _ in range(count):
            out.append(v.astype(dtype))
            v = (v - out[-1].astype(np.float32)).astype(np.float32)
        return out

    slope = np.float32([2.0 ** -0.5 * (2.0 ** -0.5) ** n for n in range(H)])
    pos = np.arange(S, dtype=np.float32)
    line = (slope[:, None] * pos[None, :]).astype(np.float32)
    one = np.ones((3, H, S), bf16)
    k_rows = np.concatenate([one, np.stack(in_parts(-line)), one])
    clamp = np.zeros((P, CLAMP_COLS), np.float16)
    for h, (d, n) in CLAMPED.items():
        rel = np.arange(d * P, S, dtype=np.float32)[None, :] - np.arange(P, dtype=np.float32)[:, None]
        fix = np.minimum(8.0 - rel * slope[h], 0.0).astype(np.float32)
        for m, part in enumerate(in_parts(fix * np.float32(CLAMP_SCALE), n, np.float16)):
            clamp[:, CLAMP_AT[h] + m * (S - d * P):CLAMP_AT[h] + (m + 1) * (S - d * P)] = part
    q, k = np.arange(P)[:, None], np.arange(P)[None, :]
    const = np.concatenate([np.eye(P), np.where(k > q, NEG, 0.0), np.where(q > k, NEG, 0.0)], 1).astype(bf16)
    clamp_ident = (np.eye(P) / CLAMP_SCALE).astype(np.float16)
    const = np.concatenate([const, clamp_ident.view(bf16)], 1)
    return {"k_rows": k_rows, "one_rows": one, "q_rows": np.stack(in_parts(line)), "clamp": clamp, "const": const,
            "half": np.full((P, NT), -0.5, np.float32)}


def kernel(**inputs):
    import numpy as np
    import concourse.bacc as bacc
    from concourse.bass_utils import run_bass_kernel_spmd

    arrays = lay_out(np, {k: np.asarray(v) for k, v in inputs.items()})
    nc = bacc.Bacc("TRN2", target_bir_lowering=False, num_devices=1)
    ins = {name: nc.dram_tensor(f"in_{name}", a.shape, mybir.dt.from_np(a.dtype), kind="ExternalInput").ap()
           for name, a in arrays.items()}
    out = nc.dram_tensor("out", (NB, P, NT, D), F32, kind="ExternalOutput").ap()
    decoder(nc, ins, out)
    result = run_bass_kernel_spmd(nc, [{f"in_{name}": a for name, a in arrays.items()}], core_ids=[0])
    tokens = result.results[0]["out"]
    return np.ascontiguousarray(tokens.transpose(0, 2, 1, 3)).reshape(NB, S, D)
```
